# Optimizing a Trainium2 kernel written in Bass

```python
import numpy as np
import jax
import jax.numpy as jnp

def _softmax(x, axis=-1):
    return jax.nn.softmax(x, axis=axis)

def _gelu(x):
    return jax.nn.gelu(x, approximate=True)

def _silu(x):
    return jax.nn.silu(x)

def _sigmoid(x):
    return jax.nn.sigmoid(x)

def _layernorm(x, axis=-1, eps=1e-05):
    m = jnp.mean(x, axis=axis, keepdims=True)
    v = jnp.var(x, axis=axis, keepdims=True)
    return (x - m) / jnp.sqrt(v + eps)

def _scatter_add(tgt, idx, src, axis=0):
    return tgt.at[idx].add(src)

def _segment_sum(src, seg, n):
    return jax.ops.segment_sum(src, seg, n)
kernel_name = 'mk_gnn_preln_d4_gnn_r64_5e6bd3'

def setup_inputs(seed: int=0):
    np.random.seed(seed)
    _w = jnp.asarray

    def _rec_inputs():
        import jax
        import jax.numpy as jnp
        _gk = jax.random.key(seed)
        x = -0.0003713 + 1 * jax.random.normal(jax.random.fold_in(_gk, 1), (100000, 128), jnp.float32)
        src = jax.random.randint(jax.random.fold_in(_gk, 2), (25000,), 0, 100000, jnp.int32)
        dst = jax.random.randint(jax.random.fold_in(_gk, 3), (25000,), 0, 100000, jnp.int32)
        _o = jnp.argsort(dst, stable=True)
        src = src[_o]
        dst = dst[_o]
        edge_type_4 = jax.random.randint(jax.random.fold_in(_gk, 13), (25000,), 0, 4, jnp.int32)
        edge_type_8 = jax.random.randint(jax.random.fold_in(_gk, 14), (25000,), 0, 8, jnp.int32)
        return (x, src, dst, edge_type_4, edge_type_8)
    x, src, dst, edge_type_4, edge_type_8 = _rec_inputs()

    def _L0_gnn_setup():
        import jax, jax.numpy as jnp
        import numpy as np
        N_NODES = 100000
        N_EDGES = 25000
        D_IN = 128
        D_HID = 128

        def _degree_norms(src, dst, n, dtype):
            ones = jnp.ones(src.shape[0], dtype=dtype)
            deg_out = jax.ops.segment_sum(ones, src, num_segments=n)
            deg_in = jax.ops.segment_sum(ones, dst, num_segments=n)
            norm_out = jax.lax.rsqrt(jnp.clip(deg_out, 1.0))
            norm_in = jax.lax.rsqrt(jnp.clip(deg_in, 1.0))
            return (norm_out, norm_in)

        def _graph_conv(x, W, b, src, dst, norm_out, norm_in, n):
            h = x * norm_out[:, None] @ W
            agg = jax.ops.segment_sum(h[src], dst, num_segments=n)
            return agg * norm_in[:, None] + b
        key = jax.random.key(seed)
        k1, k2, k3, k4, k5 = jax.random.split(key, 5)
        x = jax.random.normal(k1, (N_NODES, D_IN), dtype=jnp.float32)
        W1 = jax.random.normal(k2, (D_IN, D_HID), dtype=jnp.float32) * np.float32(1.0 / np.sqrt(D_IN))
        b1 = jnp.zeros((D_HID,), dtype=jnp.float32)
        W2 = jax.random.normal(k3, (D_HID, D_HID), dtype=jnp.float32) * np.float32(1.0 / np.sqrt(D_HID))
        b2 = jnp.zeros((D_HID,), dtype=jnp.float32)
        src = jax.random.randint(k4, (N_EDGES,), 0, N_NODES, dtype=jnp.int64)
        dst = jax.random.randint(k5, (N_EDGES,), 0, N_NODES, dtype=jnp.int64)
        return {'x': x, 'W1': W1, 'b1': b1, 'W2': W2, 'b2': b2, 'src': src, 'dst': dst}
    _L0_gnn_all = _L0_gnn_setup()
    _L0_gnn_in = {k: v for k, v in _L0_gnn_all.items() if k in ('W1', 'b1', 'W2', 'b2')}
    del _L0_gnn_all

    def _L1_gnn_setup():
        import jax, jax.numpy as jnp
        import numpy as np
        N_NODES = 100000
        N_EDGES = 25000
        IN_FEAT = 128
        OUT_FEAT = 128
        NUM_RELS = 8
        NUM_BASES = 4
        NUM_HEADS = 8
        HEAD_DIM = OUT_FEAT // NUM_HEADS
        NEG_SLOPE = 0.2
        BN_EPS = 1e-05
        key = jax.random.key(seed)
        ks = jax.random.split(key, 8)
        h = jax.random.normal(ks[0], (N_NODES, IN_FEAT), dtype=jnp.float32)
        weight = jax.random.normal(ks[1], (NUM_BASES, IN_FEAT, OUT_FEAT), dtype=jnp.float32) * 0.05
        w_comp = jax.random.normal(ks[2], (NUM_RELS, NUM_BASES), dtype=jnp.float32)
        attn_l = jax.random.normal(ks[3], (NUM_HEADS, HEAD_DIM), dtype=jnp.float32) * 0.1
        attn_r = jax.random.normal(ks[4], (NUM_HEADS, HEAD_DIM), dtype=jnp.float32) * 0.1
        gamma = jnp.ones((OUT_FEAT,), dtype=jnp.float32)
        beta = jnp.zeros((OUT_FEAT,), dtype=jnp.float32)
        src = jax.random.randint(ks[5], (N_EDGES,), 0, N_NODES, dtype=jnp.int32)
        dst = jax.random.randint(ks[6], (N_EDGES,), 0, N_NODES, dtype=jnp.int32)
        rel = jax.random.randint(ks[7], (N_EDGES,), 0, NUM_RELS, dtype=jnp.int32)
        return {'h': h, 'weight': weight, 'w_comp': w_comp, 'attn_l': attn_l, 'attn_r': attn_r, 'gamma': gamma, 'beta': beta, 'src': src, 'dst': dst, 'rel': rel}
    _L1_gnn_all = _L1_gnn_setup()
    _L1_gnn_in = {k: v for k, v in _L1_gnn_all.items() if k in ('weight', 'w_comp', 'attn_l', 'attn_r', 'gamma', 'beta')}
    del _L1_gnn_all

    def _L2_gnn_setup():
        import jax, jax.numpy as jnp
        import numpy as np
        N_NODES = 50000
        N_EDGES = 12500
        IN_DIM = 128
        OUT_DIM = 32
        N_HEADS = 4
        N_REL = 4
        NEG_SLOPE = 0.2
        LN_EPS = 1e-05
        key = jax.random.key(seed)
        ks = jax.random.split(key, 8)
        x = jax.random.normal(ks[0], (N_NODES, IN_DIM), dtype=jnp.float32)
        edge_index = jax.random.randint(ks[1], (2, N_EDGES), 0, N_NODES)
        edge_type = jax.random.randint(ks[2], (N_EDGES,), 0, N_REL)
        W = jax.random.normal(ks[3], (N_REL, IN_DIM, N_HEADS * OUT_DIM), dtype=jnp.float32) * 0.1
        attn_src = jax.random.normal(ks[4], (N_REL, N_HEADS, OUT_DIM), dtype=jnp.float32) * 0.1
        attn_dst = jax.random.normal(ks[5], (N_REL, N_HEADS, OUT_DIM), dtype=jnp.float32) * 0.1
        bias = jnp.zeros((N_HEADS * OUT_DIM,), dtype=jnp.float32)
        ln_gamma = jnp.ones((N_HEADS * OUT_DIM,), dtype=jnp.float32)
        ln_beta = jnp.zeros((N_HEADS * OUT_DIM,), dtype=jnp.float32)
        return {'x': x, 'edge_index': edge_index, 'edge_type': edge_type, 'W': W, 'attn_src': attn_src, 'attn_dst': attn_dst, 'bias': bias, 'ln_gamma': ln_gamma, 'ln_beta': ln_beta}
    _L2_gnn_all = _L2_gnn_setup()
    _L2_gnn_in = {k: v for k, v in _L2_gnn_all.items() if k in ('W', 'attn_src', 'attn_dst', 'bias', 'ln_gamma', 'ln_beta')}
    del _L2_gnn_all

    def _L3_gnn_setup():
        import jax, jax.numpy as jnp
        import numpy as np
        N_NODES = 50000
        N_EDGES = 12500
        IN_FEATS = 128
        H_FEATS = 128

        def _gin_conv(h, src, dst, Wa, ba, Wb, bb):
            agg = jax.ops.segment_sum(h[src], dst, num_segments=h.shape[0])
            z = h + agg
            z = jax.nn.relu(z @ Wa + ba)
            return jax.nn.relu(z @ Wb + bb)
        key = jax.random.key(seed)
        ks = jax.random.split(key, 10)
        x = jax.random.normal(ks[0], (N_NODES, IN_FEATS), dtype=jnp.float32)
        edge_index = jax.random.randint(ks[1], (2, N_EDGES), 0, N_NODES, dtype=jnp.int64)
        s1 = 1.0 / np.sqrt(IN_FEATS)
        s2 = 1.0 / np.sqrt(H_FEATS)
        return {'x': x, 'edge_index': edge_index, 'W1a': jax.random.normal(ks[2], (IN_FEATS, H_FEATS), dtype=jnp.float32) * s1, 'b1a': jnp.zeros((H_FEATS,), dtype=jnp.float32), 'W1b': jax.random.normal(ks[3], (H_FEATS, H_FEATS), dtype=jnp.float32) * s2, 'b1b': jnp.zeros((H_FEATS,), dtype=jnp.float32), 'W2a': jax.random.normal(ks[4], (H_FEATS, H_FEATS), dtype=jnp.float32) * s2, 'b2a': jnp.zeros((H_FEATS,), dtype=jnp.float32), 'W2b': jax.random.normal(ks[5], (H_FEATS, H_FEATS), dtype=jnp.float32) * s2, 'b2b': jnp.zeros((H_FEATS,), dtype=jnp.float32)}
    _L3_gnn_all = _L3_gnn_setup()
    _L3_gnn_in = {k: v for k, v in _L3_gnn_all.items() if k in ('W1a', 'b1a', 'W1b', 'b1b', 'W2a', 'b2a', 'W2b', 'b2b')}
    del _L3_gnn_all
    return {'x': x, 'src': src, 'dst': dst, 'edge_type_4': edge_type_4, 'edge_type_8': edge_type_8, 'L0_gnn_W1': _L0_gnn_in['W1'], 'L0_gnn_b1': _L0_gnn_in['b1'], 'L0_gnn_W2': _L0_gnn_in['W2'], 'L0_gnn_b2': _L0_gnn_in['b2'], 'L1_gnn_weight': _L1_gnn_in['weight'], 'L1_gnn_w_comp': _L1_gnn_in['w_comp'], 'L1_gnn_attn_l': _L1_gnn_in['attn_l'], 'L1_gnn_attn_r': _L1_gnn_in['attn_r'], 'L1_gnn_gamma': _L1_gnn_in['gamma'], 'L1_gnn_beta': _L1_gnn_in['beta'], 'L2_gnn_W': _L2_gnn_in['W'], 'L2_gnn_attn_src': _L2_gnn_in['attn_src'], 'L2_gnn_attn_dst': _L2_gnn_in['attn_dst'], 'L2_gnn_bias': _L2_gnn_in['bias'], 'L2_gnn_ln_gamma': _L2_gnn_in['ln_gamma'], 'L2_gnn_ln_beta': _L2_gnn_in['ln_beta'], 'L3_gnn_W1a': _L3_gnn_in['W1a'], 'L3_gnn_b1a': _L3_gnn_in['b1a'], 'L3_gnn_W1b': _L3_gnn_in['W1b'], 'L3_gnn_b1b': _L3_gnn_in['b1b'], 'L3_gnn_W2a': _L3_gnn_in['W2a'], 'L3_gnn_b2a': _L3_gnn_in['b2a'], 'L3_gnn_W2b': _L3_gnn_in['W2b'], 'L3_gnn_b2b': _L3_gnn_in['b2b']}

def reference(x, src, dst, edge_type_4, edge_type_8, L0_gnn_W1, L0_gnn_b1, L0_gnn_W2, L0_gnn_b2, L1_gnn_weight, L1_gnn_w_comp, L1_gnn_attn_l, L1_gnn_attn_r, L1_gnn_gamma, L1_gnn_beta, L2_gnn_W, L2_gnn_attn_src, L2_gnn_attn_dst, L2_gnn_bias, L2_gnn_ln_gamma, L2_gnn_ln_beta, L3_gnn_W1a, L3_gnn_b1a, L3_gnn_W1b, L3_gnn_b1b, L3_gnn_W2a, L3_gnn_b2a, L3_gnn_W2b, L3_gnn_b2b):
    import jax
    import jax.numpy as jnp

    def _L0_gnn_ref(x, W1, b1, W2, b2, src, dst):
        import jax, jax.numpy as jnp
        import numpy as np
        N_NODES = 100000
        N_EDGES = 25000
        D_IN = 128
        D_HID = 128

        def _degree_norms(src, dst, n, dtype):
            ones = jnp.ones(src.shape[0], dtype=dtype)
            deg_out = jax.ops.segment_sum(ones, src, num_segments=n)
            deg_in = jax.ops.segment_sum(ones, dst, num_segments=n)
            norm_out = jax.lax.rsqrt(jnp.clip(deg_out, 1.0))
            norm_in = jax.lax.rsqrt(jnp.clip(deg_in, 1.0))
            return (norm_out, norm_in)

        def _graph_conv(x, W, b, src, dst, norm_out, norm_in, n):
            h = x * norm_out[:, None] @ W
            agg = jax.ops.segment_sum(h[src], dst, num_segments=n)
            return agg * norm_in[:, None] + b
        n = x.shape[0]
        norm_out, norm_in = _degree_norms(src, dst, n, x.dtype)
        h = jax.nn.relu(_graph_conv(x, W1, b1, src, dst, norm_out, norm_in, n))
        return _graph_conv(h, W2, b2, src, dst, norm_out, norm_in, n)

    def _L1_gnn_ref(h, weight, w_comp, attn_l, attn_r, gamma, beta, src, dst, rel):
        import jax, jax.numpy as jnp
        import numpy as np
        N_NODES = 100000
        N_EDGES = 25000
        IN_FEAT = 128
        OUT_FEAT = 128
        NUM_RELS = 8
        NUM_BASES = 4
        NUM_HEADS = 8
        HEAD_DIM = OUT_FEAT // NUM_HEADS
        NEG_SLOPE = 0.2
        BN_EPS = 1e-05
        n_nodes, in_feat = h.shape
        num_bases, _, out_feat = weight.shape
        num_rels = w_comp.shape[0]
        num_heads, head_dim = attn_l.shape
        w = weight.reshape(in_feat, num_bases, out_feat)
        w_rel = jnp.einsum('rb,ibo->iro', w_comp, w).reshape(num_rels, in_feat, out_feat)
        xh = jnp.einsum('nd,rdo->nro', h, w_rel)
        msg = xh[src, rel]
        msg_h = msg.reshape(-1, num_heads, head_dim)
        dst_h = h[dst].reshape(-1, num_heads, head_dim)
        score_l = jnp.sum(msg_h * attn_l, axis=-1)
        score_r = jnp.sum(dst_h * attn_r, axis=-1)
        score = jax.nn.leaky_relu(score_l + score_r, negative_slope=NEG_SLOPE)
        score = jax.nn.softmax(score, axis=1)
        msg = (msg_h * score[..., None]).reshape(-1, out_feat)
        agg = jax.ops.segment_sum(msg, dst, num_segments=n_nodes)
        mean = jnp.mean(agg, axis=0)
        var = jnp.mean((agg - mean) ** 2, axis=0)
        out = (agg - mean) / jnp.sqrt(var + BN_EPS) * gamma + beta
        return out

    def _L2_gnn_ref(x, edge_index, edge_type, W, attn_src, attn_dst, bias, ln_gamma, ln_beta):
        import jax, jax.numpy as jnp
        import numpy as np
        N_NODES = 50000
        N_EDGES = 12500
        IN_DIM = 128
        OUT_DIM = 32
        N_HEADS = 4
        N_REL = 4
        NEG_SLOPE = 0.2
        LN_EPS = 1e-05
        N = x.shape[0]
        R, H, D = attn_src.shape
        src = edge_index[0]
        dst = edge_index[1]
        out = jnp.zeros((N, H * D), dtype=x.dtype)
        for r in range(R):
            mask = (edge_type == r)[:, None]
            h = (x @ W[r]).reshape(N, H, D)
            e_src = jnp.einsum('ehd,hd->eh', h[src], attn_src[r])
            e_dst = jnp.einsum('ehd,hd->eh', h[dst], attn_dst[r])
            e = jax.nn.leaky_relu(e_src + e_dst, negative_slope=NEG_SLOPE)
            e_for_max = jnp.where(mask, e, -1e+30)
            e_max = jnp.maximum(jax.ops.segment_max(e_for_max, dst, num_segments=N), 0.0)
            e_exp = jnp.where(mask, jnp.exp(e - e_max[dst]), 0.0)
            e_sum = jax.ops.segment_sum(e_exp, dst, num_segments=N)
            alpha = e_exp / (e_sum[dst] + 1e-08)
            msg = alpha[:, :, None] * h[src]
            out_rel = jax.ops.segment_sum(msg, dst, num_segments=N)
            out = out + out_rel.reshape(N, H * D)
        out = out + bias
        out = out + x
        mu = jnp.mean(out, axis=-1, keepdims=True)
        var = jnp.mean(jnp.square(out - mu), axis=-1, keepdims=True)
        out = (out - mu) * jax.lax.rsqrt(var + LN_EPS) * ln_gamma + ln_beta
        return out

    def _L3_gnn_ref(x, edge_index, W1a, b1a, W1b, b1b, W2a, b2a, W2b, b2b):
        import jax, jax.numpy as jnp
        import numpy as np
        N_NODES = 50000
        N_EDGES = 12500
        IN_FEATS = 128
        H_FEATS = 128

        def _gin_conv(h, src, dst, Wa, ba, Wb, bb):
            agg = jax.ops.segment_sum(h[src], dst, num_segments=h.shape[0])
            z = h + agg
            z = jax.nn.relu(z @ Wa + ba)
            return jax.nn.relu(z @ Wb + bb)
        src, dst = (edge_index[0], edge_index[1])
        h = _gin_conv(x, src, dst, W1a, b1a, W1b, b1b)
        h = jax.nn.relu(h)
        return _gin_conv(h, src, dst, W2a, b2a, W2b, b2b)
    edge_index = jnp.stack([src, dst])
    h = jnp.maximum(_layernorm(x, axis=-1), 0.0)
    x = x + _L0_gnn_ref(h, L0_gnn_W1, L0_gnn_b1, L0_gnn_W2, L0_gnn_b2, src, dst)
    h = jnp.maximum(_layernorm(x, axis=-1), 0.0)
    x = x + _L1_gnn_ref(h, L1_gnn_weight, L1_gnn_w_comp, L1_gnn_attn_l, L1_gnn_attn_r, L1_gnn_gamma, L1_gnn_beta, src, dst, edge_type_8)
    h = jnp.maximum(_layernorm(x, axis=-1), 0.0)
    x = x + _L2_gnn_ref(h, edge_index, edge_type_4, L2_gnn_W, L2_gnn_attn_src, L2_gnn_attn_dst, L2_gnn_bias, L2_gnn_ln_gamma, L2_gnn_ln_beta)
    h = jnp.maximum(_layernorm(x, axis=-1), 0.0)
    x = x + _L3_gnn_ref(h, edge_index, L3_gnn_W1a, L3_gnn_b1a, L3_gnn_W1b, L3_gnn_b1b, L3_gnn_W2a, L3_gnn_b2a, L3_gnn_W2b, L3_gnn_b2b)
    return x

_drawn_inputs = setup_inputs


def setup_inputs(seed=0):
    import zlib

    import numpy as np

    out = dict(_drawn_inputs(seed))
    spreads = {'L0_gnn_b1': (0.0, 0.286),
     'L0_gnn_b2': (0.0, 0.1),
     'L1_gnn_gamma': (1.0, 0.2),
     'L1_gnn_beta': (0.0, 0.1),
     'L2_gnn_bias': (0.0, 0.1),
     'L2_gnn_ln_gamma': (1.0, 0.2),
     'L2_gnn_ln_beta': (0.0, 0.1),
     'L3_gnn_b1a': (0.0, 0.589),
     'L3_gnn_b1b': (0.0, 0.472),
     'L3_gnn_b2a': (0.0, 0.366),
     'L3_gnn_b2b': (0.0, 0.288)}
    factors = {'L2_gnn_attn_src': 108.527, 'L2_gnn_attn_dst': 200.0}
    for name, (base, spread) in spreads.items():
        noise = np.random.default_rng([zlib.crc32(name.encode()), seed]).standard_normal(out[name].shape)
        drawn = base * np.exp(spread * noise) if base else spread * noise
        out[name] = jnp.asarray(drawn.astype(out[name].dtype))
    for name, factor in factors.items():
        out[name] = (out[name] * factor).astype(out[name].dtype)
    return out
```

```python
import concourse.bass as bass
from concourse import mybir
from contextlib import ExitStack

F32 = mybir.dt.float32
BF16 = mybir.dt.bfloat16
FP16 = mybir.dt.float16
I32 = mybir.dt.int32
ALU = mybir.AluOpType
ACT = mybir.ActivationFunctionType
AX = mybir.AxisListType

P = 128
D = 128
NODES = 100000
EDGES = 25000
T = 196
EPAD = P * T
REAL_LAST = EDGES - (P - 1) * T
G = 7
W = G * D
NI = T // (2 * G)
HI = 784
PAD_NODE = 2**24 - 1
SKIP = 1 << 20
NONE = EPAD
EPS = 1e-5
R8, H8 = 8, 8
R4, H4 = 4, 4
SLOPE = 0.2


class Shared:
    pass


class Steps:

    def __init__(self, *names):
        self.order = []
        for n in names:
            self.order += [n] if isinstance(n, tuple) else [(n, 0), (n, 1)]
        self.per = len(self.order)

    def at(self, i, name, s=0):
        return (i + 1) * self.per + self.order.index((name, s)) + 1

    def last(self, n=NI):
        return (n + 1) * self.per


def slotwise(*names):
    return [(n, s) for s in range(2) for n in names]


SUMS = tuple(f"sum{c}" for c in range(G))


def place(s, k=0):
    return s * W + k * D


def slot(buf, s):
    return buf[:, s * W:(s + 1) * W]


def tile(buf, s, k):
    return buf[:, s * W + k * D:s * W + (k + 1) * D]


def by_tile(ap):
    return ap.rearrange("p (k f) -> p k f", f=D)


def every(row, count=G):
    return row.unsqueeze(1).to_broadcast([P, count, D])


def cols(arr, i, s, k=0, n=1):
    return arr[:, bass.ds(i * (2 * G) + (s * G + k), n)]


def part(table, i, s):
    return table[0:EPAD, :].rearrange("(p t) f -> p (t f)", p=P)[:, bass.ds(i * (2 * W) + s * W, W)]



def stats(nc, x, s, st):
    for k in range(G):
        last = nc.vector.bn_stats(st[:, s, k, :], tile(x, s, k))
    return last


def aggregate(nc, s, st, mv):
    for c in range(G):
        last = nc.vector.bn_aggr(mv[:, s, c, :], st[:, s, c, :])
    return last


def deviation(nc, k, s, mv, sd):
    return nc.scalar.activation(sd[:, s, :], mv[:, s, :, 1], ACT.Sqrt, bias=k.eps[:, 0:1])


def normalise(nc, x, s, mv, rs, out):
    for k in range(G):
        last = nc.vector.tensor_scalar(tile(out, s, k), tile(x, s, k), mv[:, s, k, 0:1], rs[:, s, k:k + 1],
                                       ALU.subtract, ALU.mult)
    return last


def transposed(nc, k, x, s, psum):
    for c in range(G):
        last = nc.tensor.transpose(psum[:, c * D:(c + 1) * D], tile(x, s, c), k.ident[:, :])
    return last


def times_rows(nc, xT, s, w, psum):
    for c in range(G):
        last = nc.tensor.matmul(psum[:, c * D:(c + 1) * D], tile(xT, s, c), w, start=True, stop=True)
    return last


def times_cols(nc, xT, s, w, psum):
    v = slot(xT, s)
    nc.tensor.matmul(psum[:, 0:512], w, v[:, 0:512], start=True, stop=True)
    return nc.tensor.matmul(psum[:, 512:W], w, v[:, 512:W], start=True, stop=True)


class Phase:

    def __init__(self, nc, k, name):
        self.nc, self.k, self.name = nc, k, name

    def __enter__(self):
        self.ctx = ExitStack()
        self.ctx.__enter__()
        self.sems = []
        return self

    def sb(self, name, shape, dt=F32):
        return self.ctx.enter_context(self.nc.sbuf_tensor(f"{self.name}_{name}", shape, dt))

    def ring(self, name):
        return self.sb(name, [P, 2 * W])

    def sem(self, name):
        s = self.ctx.enter_context(self.nc.semaphore(f"{self.name}_{name}"))
        self.sems.append(s)
        return s

    def sem2(self, name):
        return [self.sem(f"{name}{s}") for s in range(2)]

    def moves(self, name, raised):
        base = self.k.raised[name]
        self.k.raised[name] += raised
        return self.k.gpsimd_sems[name], base

    def block(self):
        self.open = self.nc.Block()
        return self.open.__enter__()

    def __exit__(self, *a):
        if a[0] is None:
            self.open.__exit__(None, None, None)
            for s in self.sems:
                self.nc.gpsimd.sem_clear(s)
            self.nc.all_engine_barrier()
        return self.ctx.__exit__(*a)


def setup(nc, k):
    with Phase(nc, k, "setup") as ph:
        loaded, consts, v, edge_cols, weights = (ph.sem(n) for n in ("loaded", "consts", "vector_done", "edge_cols", "weights_loaded"))
        pe_done, act_done, stored = ph.sem("tensor_done"), ph.sem("scalar_done"), ph.sem("stored")
        dst_i = ph.sb("dst_i", [P, T + 2], I32)
        src_t = ph.sb("src_t", [P, T], I32)
        rel_i = ph.sb("rel_i", [P, 2, T], I32)
        tmp_i = ph.sb("tmp_i", [P, T], I32)
        tmp = ph.sb("tmp", [P, T])
        tmp2 = ph.sb("tmp2", [P, T])
        pos = ph.sb("pos", [P, T])
        sq = ph.sb("sq", [P, 4, P])
        hasfix = ph.sb("hasfix", [P, 2])
        upper = ph.sb("upper", [P, P])
        lower = ph.sb("lower", [P, P])
        relT = ph.sb("relT", [98, 4, P])
        row = ph.sb("row", [P, 8, D])
        none_rows = ph.sb("none_rows", [P, D])
        wv = ph.sb("wv", [P, 2, R4, D])
        wT = ph.sb("wT", [P, R4, D])
        att = ph.sb("att", [P, 2, R4, H4])
        wfT = ph.sb("wfT", [P, 4, D])
        attl = ph.sb("attl", [P, H8])
        compb = ph.sb("compb", [P, 32])
        jdx = ph.sb("jdx", [P, 2, 128])
        qm = ph.sb("qm", [P, 3, 64])
        big_none = ph.sb("big_none", [P, HI], I32)
        block = ph.block()
        PS = k.psum

        @block.sync
        def _(sp):
            sp.wait_ge(consts, 4)
            head = (P - 1) * T
            sp.dma_start(dst_i[0:P - 1, 1:T + 1], k.dst[0:head].rearrange("(p t) -> p t", t=T)).then_inc(loaded, 16)
            sp.dma_start(dst_i[P - 1:P, 1:1 + REAL_LAST], k.dst[head:EDGES].rearrange("(a t) -> a t", a=1)).then_inc(loaded, 16)
            sp.dma_start(src_t[0:P - 1, :], k.src[0:head].rearrange("(p t) -> p t", t=T)).then_inc(loaded, 16)
            sp.dma_start(src_t[P - 1:P, 0:REAL_LAST], k.src[head:EDGES].rearrange("(a t) -> a t", a=1)).then_inc(loaded, 16)
            for n, et in enumerate((k.et4, k.et8)):
                sp.dma_start(rel_i[0:P - 1, n, :], et[0:head].rearrange("(p t) -> p t", t=T)).then_inc(loaded, 16)
                sp.dma_start(rel_i[P - 1:P, n, 0:REAL_LAST], et[head:EDGES].rearrange("(a t) -> a t", a=1)).then_inc(loaded, 16)
            with nc.allow_non_contiguous_dma(reason="two columns of the edge list"):
                sp.dma_start(dst_i[1:P, 0:1], k.dst[0:head].rearrange("(p t) -> p t", t=T)[:, T - 1:T]).then_inc(edge_cols, 16)
                sp.dma_start(dst_i[0:P - 2, T + 1:T + 2], k.dst[T:head].rearrange("(p t) -> p t", t=T)[:, 0:1]).then_inc(edge_cols, 16)
                sp.dma_start(dst_i[P - 2:P - 1, T + 1:T + 2], k.dst[head:head + 1].rearrange("(a t) -> a t", a=1)).then_inc(edge_cols, 16)
            sp.wait_ge(v, 5)
            sp.dma_start(k.slot_table.rearrange("(p j) a -> p (j a)", p=P), big_none[:, :]).then_inc(stored, 16)
            sp.wait_ge(act_done, 1)
            for h in range(2):
                sp.dma_start(k.relT8[98 * h:98 * h + 98, :], relT[:, h, :]).then_inc(stored, 16)
                sp.dma_start(k.relT4[98 * h:98 * h + 98, :], relT[:, 2 + h, :]).then_inc(stored, 16)
            sp.wait_ge(v, k.setup_rows)
            sp.dma_start(k.T1[EPAD:EPAD + P, :], none_rows[:, :]).then_inc(stored, 16)
            sp.dma_start(k.T2[EPAD:EPAD + P, :], k.b2_0[:, :]).then_inc(stored, 16)
            for t in (k.V2, k.V3, k.V4):
                sp.dma_start(t[EPAD:EPAD + P, :], k.zeros[:, 0:D]).then_inc(stored, 16)
            sp.wait_ge(stored, 16 * 10)

        @block.gpsimd
        def _(g):
            g.memset(dst_i[:, 0:1], -1)
            g.memset(dst_i[:, 1:T + 1], PAD_NODE)
            g.memset(dst_i[:, T + 1:T + 2], -1)
            g.memset(src_t[:, :], 0)
            g.memset(rel_i[:, :, :], 0)
            g.memset(k.ident[:, :], 0.0)
            g.memset(upper[:, :], 1.0)
            g.memset(lower[:, :], 1.0)
            g.memset(k.zeros[:, :], 0.0)
            g.memset(k.ones[:, :], 1.0)
            g.memset(k.eps[:, :], EPS)
            g.memset(qm[:, 0, :], 0.0)
            g.iota(tmp_i[:, :], pattern=[[1, T]], base=0, channel_multiplier=T)
            g.iota(k.hi_row[:, :], pattern=[[1, HI]], base=0, channel_multiplier=0, allow_small_or_imprecise_dtypes=True)
            g.iota(k.p_col[:, :], pattern=[[0, 1]], base=0, channel_multiplier=1, allow_small_or_imprecise_dtypes=True)\
                .then_inc(consts, 4)
            g.wait_ge(consts, 4)
            g.affine_select(out=k.ident[:, :], in_=k.ident[:, :], compare_op=ALU.not_equal, fill=1.0,
                            base=0, pattern=[[-1, P]], channel_multiplier=1)
            g.affine_select(out=upper[:, :], in_=upper[:, :], compare_op=ALU.is_gt, fill=0.0,
                            base=0, pattern=[[1, P]], channel_multiplier=-1)
            g.affine_select(out=lower[:, :], in_=lower[:, :], compare_op=ALU.is_gt, fill=0.0,
                            base=0, pattern=[[-1, P]], channel_multiplier=1)
            g.memset(qm[:, 1, :], 1.0).then_inc(consts, 1)
            g.wait_ge(consts, 5)
            q3 = qm[:, 1, :].rearrange("p (j b) -> p j b", b=4)
            g.affine_select(out=q3, in_=q3, compare_op=ALU.is_ge, fill=0.0,
                            base=0, pattern=[[-8, 16], [0, 4]], channel_multiplier=1).then_inc(consts, 1)
            g.wait_ge(consts, 6)
            g.affine_select(out=q3, in_=q3, compare_op=ALU.is_ge, fill=0.0,
                            base=7, pattern=[[8, 16], [0, 4]], channel_multiplier=-1).then_inc(consts, 1)

        @block.scalar
        def _(a):
            def rows(dst, src):
                a.dma_start(dst, src).then_inc(weights, 16)
            bc = lambda ap: ap.rearrange("(a n) -> a n", a=1).to_broadcast([P, D])
            rows(k.w0[:, 0, :], k.w['L0_gnn_W1'])
            rows(k.w0[:, 1, :], k.w['L0_gnn_W2'])
            rows(k.wf[:, :, 0:D], k.w['L1_gnn_weight'].rearrange("b i o -> (b i) o").rearrange("(c k) o -> k c o", k=P))
            rows(k.w2[:, :, 0:D], k.w['L2_gnn_W'].rearrange("r i o -> i r o"))
            for n, name in enumerate(('L3_gnn_W1a', 'L3_gnn_W1b', 'L3_gnn_W2a', 'L3_gnn_W2b')):
                rows(k.w3[:, n, :], k.w[name])
            with nc.allow_non_contiguous_dma(reason="bias columns and attention vectors"):
                for n, name in enumerate(('L3_gnn_b1a', 'L3_gnn_b1b', 'L3_gnn_b2a')):
                    rows(k.b3[:, n:n + 1], k.w[name].rearrange("(n a) -> n a", a=1))
                rows(k.gb[:, 0:1], k.w['L1_gnn_gamma'].rearrange("(n a) -> n a", a=1))
                rows(k.gb[:, 1:2], k.w['L1_gnn_beta'].rearrange("(n a) -> n a", a=1))
                rows(attl[:, 0:1], k.w['L1_gnn_attn_l'].rearrange("h (d a) -> (h d) a", a=1))
                for m, name in enumerate(('L2_gnn_attn_src', 'L2_gnn_attn_dst')):
                    rows(att[:, m, :, 0:1], k.w[name].rearrange("r h (d a) -> (h d) r a", a=1))
                for n in range(16):
                    rows(compb[8 * n:8 * n + 8, 0:4], k.w['L1_gnn_w_comp'])
            rows(k.b1_0[:, :], bc(k.w['L0_gnn_b1']))
            rows(k.b2_0[:, :], bc(k.w['L0_gnn_b2']))
            rows(k.attn_r[:, :], k.w['L1_gnn_attn_r'].rearrange("h d -> (h d)").rearrange("(a n) -> a n", a=1).to_broadcast([P, D]))
            rows(k.bias2[:, :], bc(k.w['L2_gnn_bias']))
            rows(k.ln_g[:, :], bc(k.w['L2_gnn_ln_gamma']))
            rows(k.ln_b[:, :], bc(k.w['L2_gnn_ln_beta']))
            rows(k.b3_row[:, 0, :], bc(k.w['L3_gnn_b1b']))
            rows(k.b3_row[:, 1, :], bc(k.w['L3_gnn_b2b']))
            a.wait_ge(pe_done, 2)
            a.activation(relT[:, :, :], PS[0:98, 0:4 * P], ACT.Copy).then_inc(act_done, 1)
            a.wait_ge(pe_done, 4)
            a.activation(wfT[:, :, :], PS[:, 2048:2560], ACT.Copy).then_inc(act_done, 1)
            a.activation(wT[:, :, :], PS[:, 2560:3072], ACT.Copy).then_inc(act_done, 1)
            a.wait_ge(pe_done, 6)
            a.activation(k.wf[:, :, D:D + H8], PS[:, 3072:3072 + 32].rearrange("p (c h) -> p c h", h=H8), ACT.Copy).then_inc(act_done, 1)
            pv = PS[:, 3584:3584 + 32].rearrange("p (m r h) -> p m r h", m=2, h=H4)
            a.activation(k.intoT[:, :], PS[:, 768:896], ACT.Copy)
            a.activation(k.w2[:, :, D:D + H4], pv[:, 0, :, :], ACT.Copy)
            a.activation(k.vdst[:, :].rearrange("p (r h) -> p r h", h=H4), pv[:, 1, :, :], ACT.Copy).then_inc(act_done, 1)

        @block.vector
        def _(d):
            n = [0]

            def chain(ins):
                n[0] += 1
                ins.then_inc(v, 1)
                d.wait_ge(v, n[0])

            d.wait_ge(loaded, 16 * 8)
            d.wait_ge(edge_cols, 48)
            chain(d.tensor_copy(k.dstf[:, :], dst_i[:, :]))
            chain(d.tensor_copy(k.src_i[:, :], src_t[:, :]))
            d.wait_ge(consts, 7)
            chain(d.tensor_copy(pos[:, :], tmp_i[:, :]))
            chain(d.memset(tmp[:, :], float(NONE)))
            chain(d.tensor_copy(big_none[:, :], tmp[:, 0:1].to_broadcast([P, HI])))
            chain(d.tensor_copy(k.rel4[:, :], rel_i[:, 0, :]))
            chain(d.tensor_copy(k.rel8[:, :], rel_i[:, 1, :]))
            chain(d.tensor_scalar(tmp_i[:, :], src_t[:, :], 127, None, ALU.bitwise_and))
            chain(d.tensor_copy(k.lo[:, :], tmp_i[:, :]))
            chain(d.tensor_scalar(tmp_i[:, :], src_t[:, :], 7, None, ALU.arith_shift_right))
            chain(d.tensor_copy(k.hi[:, :], tmp_i[:, :]))
            chain(d.scalar_tensor_tensor(tmp[:, :], k.lo[:, :], float(HI), k.hi[:, :], ALU.mult, ALU.add))
            chain(d.tensor_copy(k.src_tab[:, :], tmp[:, :]))
            chain(d.tensor_scalar(tmp2[:, :], pos[:, :], float(EDGES), 1.0, ALU.is_lt, ALU.mult))
            chain(d.scalar_tensor_tensor(k.lo[:, :], k.lo[:, :], 1.0, tmp2[:, :], ALU.add, ALU.mult))
            chain(d.tensor_scalar(k.lo[:, :], k.lo[:, :], 1.0, None, ALU.subtract))
            chain(d.tensor_tensor(k.cont[:, :], k.dstf[:, 1:T + 1], k.dstf[:, 0:T], ALU.is_equal))
            chain(d.memset(k.cont[:, 0:1], 0.0))
            chain(d.tensor_tensor(k.end[:, :], k.dstf[:, 1:T + 1], k.dstf[:, 2:T + 2], ALU.not_equal))
            chain(d.tensor_tensor(k.real_end[:, :], k.end[:, :], tmp2[:, :], ALU.mult))
            chain(d.tensor_scalar(k.more[:, :], k.end[:, :], -1.0, 1.0, ALU.mult, ALU.add))
            chain(d.tensor_scalar(k.fix[:, :], k.dstf[:, 1:T + 1], k.dstf[:, 1:2], None, ALU.is_equal))
            chain(d.tensor_tensor(k.fix[:, :], k.fix[:, :], k.end[:, :], ALU.mult))
            chain(d.tensor_reduce(hasfix[:, 0:1], k.fix[:, :], AX.X, ALU.add))
            chain(d.tensor_tensor(tmp[:, :], k.fix[:, :], pos[:, :], ALU.mult))
            chain(d.tensor_reduce(hasfix[:, 1:2], tmp[:, :], AX.X, ALU.add))
            chain(d.scalar_tensor_tensor(hasfix[:, 1:2], hasfix[:, 0:1], -float(SKIP), hasfix[:, 1:2], ALU.mult, ALU.add))
            chain(d.tensor_scalar(hasfix[:, 1:2], hasfix[:, 1:2], float(SKIP), None, ALU.add))
            chain(d.tensor_copy(k.fix_i[:, :], hasfix[:, 1:2]))
            chain(d.tensor_copy(tmp_i[:, :], k.dstf[:, 1:T + 1]))
            chain(d.tensor_scalar(tmp[:, :], k.dstf[:, 1:T + 1], -float(SKIP), None, ALU.add))
            chain(d.tensor_tensor(tmp[:, :], tmp[:, :], k.end[:, :], ALU.mult))
            chain(d.tensor_scalar(tmp[:, :], tmp[:, :], float(SKIP), None, ALU.add))
            chain(d.tensor_copy(k.out_i[:, :], tmp[:, :]))
            chain(d.tensor_scalar(rel_i[:, 0, :], tmp_i[:, :], 127, None, ALU.bitwise_and))
            chain(d.tensor_scalar(rel_i[:, 1, :], tmp_i[:, :], 7, None, ALU.arith_shift_right))
            chain(d.tensor_copy(tmp[:, :], rel_i[:, 0, :]))
            chain(d.tensor_copy(tmp2[:, :], rel_i[:, 1, :]))
            chain(d.scalar_tensor_tensor(tmp[:, :], tmp[:, :], float(HI), tmp2[:, :], ALU.mult, ALU.add))
            chain(d.tensor_scalar(tmp[:, :], tmp[:, :], -float(SKIP), None, ALU.add))
            chain(d.tensor_tensor(tmp[:, :], tmp[:, :], k.end[:, :], ALU.mult))
            chain(d.tensor_scalar(tmp[:, :], tmp[:, :], float(SKIP), None, ALU.add))
            chain(d.tensor_copy(k.slot_at[:, :], tmp[:, :]))
            chain(d.tensor_copy(k.pos_i[:, :], pos[:, :]))
            chain(d.tensor_scalar(tmp[:, :], k.dstf[:, 1:T + 1], float(NODES), None, ALU.is_lt))
            chain(d.tensor_tensor(tmp[:, :], tmp[:, :], k.dstf[:, 1:T + 1], ALU.mult))
            chain(d.tensor_copy(k.dst_i[:, :], tmp[:, :]))
            chain(d.tensor_copy(sq[:, 0, :], k.dstf[:, 1:2].to_broadcast([P, P])))
            chain(d.tensor_copy(sq[:, 1, :], k.dstf[:, T:T + 1].to_broadcast([P, P])))
            assert n[0] == SQUARES
            d.wait_ge(pe_done, 1)
            chain(d.tensor_scalar(sq[:, 2, :], PS[:, 512:640], k.dstf[:, T:T + 1], None, ALU.is_equal))
            chain(d.tensor_tensor(k.into[:, :], sq[:, 2, :], upper[:, :], ALU.mult))
            chain(d.tensor_scalar(sq[:, 3, :], PS[:, 640:768], k.dstf[:, 1:2], hasfix[:, 0:1], ALU.is_equal, ALU.mult))
            chain(d.tensor_tensor(k.back[:, :], sq[:, 3, :], lower[:, :], ALU.mult))
            d.wait_ge(weights, 16 * NWEIGHTS)
            chain(d.tensor_scalar(none_rows[:, :], k.b1_0[:, :], 0.0, None, ALU.max))
            assert n[0] == k.setup_rows
            q4 = k.q2[:, :].rearrange("p (c j b) -> p c j b", c=2, b=4)
            m3 = qm[:, 1, :].rearrange("p (j b) -> p j b", b=4)
            cb = compb[:, 0:4].unsqueeze(1).to_broadcast([P, 16, 4])
            chain(d.tensor_tensor(q4[:, 0, :, :], m3, cb, ALU.mult))
            chain(d.tensor_tensor(q4[:, 1, :, :], m3, cb, ALU.mult))
            for c in range(4):
                chain(d.memset(k.rel_of[0:64, c:c + 1], float(2 * c)))
                chain(d.memset(k.rel_of[64:P, c:c + 1], float(2 * c + 1)))
            hm8 = k.hm8[:, :]
            hm4 = k.hm4[:, :]
            chain(d.tensor_reduce(hm8, k.ident[:, :].rearrange("p (h e) -> p h e", h=H8), AX.X, ALU.add))
            chain(d.tensor_reduce(hm4, k.ident[:, :].rearrange("p (h e) -> p h e", h=H4), AX.X, ALU.add))
            chain(d.tensor_scalar(k.al[:, :], hm8, attl[:, 0:1], None, ALU.mult))
            for m in range(2):
                for r in range(R4):
                    chain(d.tensor_scalar(k.a4[:, m, r, :], hm4, att[:, m, r, 0:1], None, ALU.mult))
            assert n[0] == ATTENTION

        @block.tensor
        def _(t):
            t.wait_ge(v, SQUARES)
            nc.tensor.transpose(PS[:, 512:640], sq[:, 0, :], k.ident[:, :])
            nc.tensor.transpose(PS[:, 640:768], sq[:, 1, :], k.ident[:, :]).then_inc(pe_done, 1)
            for h in range(2):
                nc.tensor.transpose(PS[0:98, h * P:(h + 1) * P], k.rel8[:, 98 * h:98 * h + 98], k.ident[:, :])
                last = nc.tensor.transpose(PS[0:98, (h + 2) * P:(h + 3) * P], k.rel4[:, 98 * h:98 * h + 98], k.ident[:, :])
            last.then_inc(pe_done, 1)
            t.wait_ge(weights, 16 * NWEIGHTS)
            for c in range(4):
                last = nc.tensor.transpose(PS[:, 2048 + c * D:2048 + (c + 1) * D], k.wf[:, c, 0:D], k.ident[:, :])
            last.then_inc(pe_done, 1)
            for r in range(R4):
                last = nc.tensor.transpose(PS[:, 2560 + r * D:2560 + (r + 1) * D], k.w2[:, r, 0:D], k.ident[:, :])
            last.then_inc(pe_done, 1)
            t.wait_ge(act_done, 3)
            t.wait_ge(v, ATTENTION)
            for c in range(4):
                last = nc.tensor.matmul(PS[:, 3072 + c * H8:3072 + (c + 1) * H8], wfT[:, c, :], k.al[:, :], start=True, stop=True)
            last.then_inc(pe_done, 1)
            nc.tensor.transpose(PS[:, 768:896], k.into[:, :], k.ident[:, :])
            for m in range(2):
                for r in range(R4):
                    o = 3584 + (m * R4 + r) * H4
                    last = nc.tensor.matmul(PS[:, o:o + H4], wT[:, r, :], k.a4[:, m, r, :], start=True, stop=True)
            last.then_inc(pe_done, 1)


SQUARES = 49
ATTENTION = SQUARES + 5 + 2 + 8 + 3 + 8
NWEIGHTS = 4 + 4 + 3 + 2 + 1 + 2 + 16 + 8


def out_degrees(nc, k):
    S = Steps("hot")
    M = Steps("counted")
    with Phase(nc, k, "deg") as ph:
        vec, pe, staged, done, tab, act = (ph.sem(n) for n in ("vector_steps", "tensor_steps", "staged", "vector_done", "table_moved", "scalar_done"))
        scattered, sbase = ph.moves("scattered", NI * 16 * G)
        lo_hot = ph.sb("lo_hot", [P, 2, G, P], BF16)
        hi_hot = ph.sb("hi_hot", [P, 2, G, HI], BF16)
        at = ph.sb("at", [P, 2 * G], I32)
        what = ph.sb("what", [P, 2 * G], I32)
        deg = ph.sb("deg", [P, HI])
        slots = ph.sb("slots", [P, HI], I32)
        pair = ph.sb("pair", [P, HI, 2])
        zero = ph.sb("zero", [P, 512], BF16)
        block = ph.block()
        PS = k.psum

        @block.gpsimd
        def _(g):
            g.sem_inc(staged, 2)
            with g.Fori(0, NI) as i:
                for s in range(2):
                    wait_apart(g, k, scattered[s], i * (16 * G) + sbase)
                    g.tensor_copy(at[:, s * G:(s + 1) * G], cols(k.slot_at, i, s, 0, G)).then_inc(staged, 1)
                    g.tensor_copy(what[:, s * G:(s + 1) * G], cols(k.pos_i, i, s, 0, G)).then_inc(staged, 1)
                    wait_apart(g, k, staged, i * 4 + (2 * s + 4))
                    for c in range(s * G, (s + 1) * G):
                        g.indirect_dma_start(k.slot_table, bass.IndirectOffsetOnAxis(ap=at[:, c:c + 1], axis=0),
                                             what[:, c:c + 1], None, bounds_check=P * HI - 1,
                                             oob_is_err=False).then_inc(scattered[s], 16)

        @block.vector
        def _(d):
            d.memset(zero[:, :], 0.0).then_inc(done, 1)
            d.sem_inc(vec, S.per)
            with d.Fori(0, NI) as i:
                for s in range(2):
                    d.wait_ge(pe, M.at(i - 1, "counted", s))
                    for c in range(G):
                        nc.vector.tensor_scalar(lo_hot[:, s, c, :], k.hi_row[:, 0:P], cols(k.lo, i, s, c), None, ALU.is_equal)
                        last = nc.vector.tensor_scalar(hi_hot[:, s, c, :], k.hi_row[:, :], cols(k.hi, i, s, c), None, ALU.is_equal)
                    last.then_inc(vec, 1)
            d.wait_ge(pe, M.last())
            d.tensor_scalar(deg[:, 0:HI // 2], PS[:, 0:HI // 2], 1.0, None, ALU.max)
            d.tensor_scalar(deg[:, HI // 2:HI], PS[:, 512:512 + HI // 2], 1.0, None, ALU.max).then_inc(done, 1)
            d.wait_ge(act, 1)
            d.reciprocal(pair[:, :, 1], deg[:, :]).then_inc(done, 1)
            d.wait_ge(tab, 16)
            d.tensor_copy(pair[:, :, 0], slots[:, :]).then_inc(done, 1)

        @block.scalar
        def _(a):
            a.wait_ge(done, 2)
            a.activation(deg[:, :], deg[:, :], ACT.Sqrt).then_inc(act, 1)

        @block.tensor
        def _(t):
            t.wait_ge(done, 1)
            nc.tensor.matmul(PS[:, 0:HI // 2], zero[:, 0:P], zero[:, 0:HI // 2], start=True, stop=False, skip_group_check=True)
            nc.tensor.matmul(PS[:, 512:512 + HI // 2], zero[:, 0:P], zero[:, 0:HI // 2], start=True, stop=False, skip_group_check=True)
            t.sem_inc(pe, M.per)
            with t.Fori(0, NI) as i:
                for s in range(2):
                    t.wait_ge(vec, S.at(i, "hot", s))
                    for c in range(G):
                        nc.tensor.matmul(PS[:, 0:HI // 2], lo_hot[:, s, c, :], hi_hot[:, s, c, 0:HI // 2],
                                         start=False, stop=False, skip_group_check=True)
                        last = nc.tensor.matmul(PS[:, 512:512 + HI // 2], lo_hot[:, s, c, :], hi_hot[:, s, c, HI // 2:HI],
                                                start=False, stop=False, skip_group_check=True)
                    last.then_inc(pe, 1)

        @block.sync
        def _(sp):
            for s in range(2):
                sp.wait_ge(scattered[s], NI * 16 * G + sbase)
            sp.dma_start(slots[:, :], k.slot_table.rearrange("(p j) a -> p (j a)", p=P)).then_inc(tab, 16)
            sp.wait_ge(done, 4)
            sp.dma_start(k.pair_table.rearrange("(p j) a -> p (j a)", p=P), pair[:, :, :].rearrange("p j a -> p (j a)")).then_inc(tab, 16)
            sp.wait_ge(tab, 32)


def wait_apart(eng, k, sem, value):
    eng.wait_ge(sem, value)
    eng.sem_inc(k.passed, 1)


def gather_columns(nc, k, g, i, s, index, ring, staged, table, out, width, gathered):
    g.tensor_copy(ring[:, s * G:(s + 1) * G], cols(index, i, s, 0, G)).then_inc(staged, 1)
    wait_apart(g, k, staged, i * 2 + (s + 3))
    for c in range(G):
        o = (s * G + c) * width
        g.indirect_dma_start(out[:, o:o + width], None, table,
                             bass.IndirectOffsetOnAxis(ap=ring[:, s * G + c:s * G + c + 1], axis=0)).then_inc(gathered[s], 16)


def lookups(nc, k):
    S = Steps("kept")
    with Phase(nc, k, "look") as ph:
        vec, staged, v, pe, act = (ph.sem(n) for n in ("vector_steps", "staged", "vector_done", "tensor_done", "scalar_done"))
        gathered, gbase = ph.moves("gathered", NI * 16 * G)
        ring = ph.sb("ring", [P, 2 * G], I32)
        pairs = ph.sb("pairs", [P, 2 * G * 2])
        slotf = ph.sb("slotf", [P, T])
        none = ph.sb("none", [P, T])
        count = ph.sb("count", [P, T])
        carry = ph.sb("carry", [P, 1])
        block = ph.block()

        @block.gpsimd
        def _(g):
            g.sem_inc(staged, 2)
            with g.Fori(0, NI) as i:
                for s in range(2):
                    wait_apart(g, k, vec, S.at(i - 1, "kept", s))
                    gather_columns(nc, k, g, i, s, k.src_tab, ring, staged, k.pair_table, pairs, 2, gathered)

        @block.vector
        def _(d):
            d.sem_inc(vec, S.per)
            with d.Fori(0, NI) as i:
                for s in range(2):
                    d.wait_ge(gathered[s], i * (16 * G) + (16 * G + gbase))
                    got = pairs[:, s * 2 * G:(s + 1) * 2 * G].rearrange("p (c a) -> p c a", a=2)
                    nc.vector.tensor_copy(cols(slotf, i, s, 0, G), got[:, :, 0])
                    nc.vector.tensor_copy(cols(k.norm_out, i, s, 0, G), got[:, :, 1]).then_inc(vec, 1)
            n = [0]

            def chain(ins):
                n[0] += 1
                ins.then_inc(v, 1)
                d.wait_ge(v, n[0])
            d.wait_ge(vec, S.last())
            chain(d.tensor_scalar(none[:, :], slotf[:, :], float(NONE), k.p_col[:, 0:1], ALU.is_equal, ALU.mult))
            chain(d.tensor_tensor(slotf[:, :], slotf[:, :], none[:, :], ALU.add))
            chain(d.tensor_copy(k.slot_i[:, :], slotf[:, :]))
            chain(d.tensor_tensor_scan(count[:, :], k.cont[:, :], k.ones[:, 0:1].to_broadcast([P, T]), 0.0, ALU.mult, ALU.add))
            d.wait_ge(pe, 1)
            chain(d.tensor_copy(carry[:, :], k.psum[:, 0:1]))
            chain(d.scalar_tensor_tensor(count[:, :], k.fix[:, :], carry[:, 0:1], count[:, :], ALU.mult, ALU.add))
            d.wait_ge(act, 1)
            chain(d.reciprocal(k.norm_in[:, :], count[:, :]))

        @block.tensor
        def _(t):
            t.wait_ge(v, 4)
            nc.tensor.matmul(k.psum[:, 0:1], k.into[:, :], count[:, T - 1:T], start=True, stop=True).then_inc(pe, 1)

        @block.scalar
        def _(a):
            a.wait_ge(v, 6)
            a.activation(count[:, :], count[:, :], ACT.Sqrt).then_inc(act, 1)


def pair(k, j):
    return k.psum[:, j * 1024:j * 1024 + W]


def wide(k, j, c, n):
    o = j * 1024 + (c // 3) * 512 + (c % 3) * n
    return k.psum[:, o:o + n]


def running_sum(nc, k, d, vec, S, i, s, message, sums):
    for c in range(G):
        before = (tile(sums, s, c - 1), i, f"sum{c - 1}", s) if c else \
                 (tile(sums, 1 - s, G - 1), i if s else i - 1, SUMS[-1], 1 - s)
        d.wait_ge(vec, S.at(*before[1:]))
        nc.vector.scalar_tensor_tensor(tile(sums, s, c), before[0], cols(k.cont, i, s, c), tile(message, s, c),
                                       ALU.mult, ALU.add).then_inc(vec, 1)


def join_partitions(nc, k, V, name):
    with Phase(nc, k, name) as ph:
        pe, v, zeroed = (ph.sem(n) for n in ("tensor_done", "vector_done", "zeroed"))
        (fetched, _), fbase = ph.moves("fetched", 32)
        rows = ph.sb("rows", [P, D])
        block = ph.block()

        @block.tensor
        def _(t):
            nc.tensor.matmul(k.psum[:, 0:D], k.into[:, :], k.tail[:, :], start=True, stop=True).then_inc(pe, 1)

        @block.gpsimd
        def _(g):
            g.memset(rows[:, :], 0.0).then_inc(zeroed, 1)
            g.wait_ge(zeroed, 1)
            at = bass.IndirectOffsetOnAxis(ap=k.fix_i[:, 0:1], axis=0)
            g.indirect_dma_start(rows[:, :], None, V, at, bounds_check=EPAD - 1, oob_is_err=False).then_inc(fetched, 16)
            g.wait_ge(v, 1)
            g.indirect_dma_start(V, at, rows[:, :], None, bounds_check=EPAD - 1, oob_is_err=False).then_inc(fetched, 16)
            g.wait_ge(fetched, fbase + 32)

        @block.vector
        def _(d):
            d.wait_ge(fetched, fbase + 16)
            d.wait_ge(pe, 1)
            nc.vector.tensor_tensor(rows[:, :], rows[:, :], k.psum[:, 0:D], ALU.add).then_inc(v, 1)


def conv1_edges(nc, k):
    V = Steps("stats", "aggr", "rs", "rsn", "norm", *slotwise(*SUMS))
    A = Steps("sd", "relu")
    with Phase(nc, k, "c1e") as ph:
        vec, act, staged, cleared = (ph.sem(n) for n in ("vector_steps", "scalar_steps", "staged", "cleared"))
        gathered, gbase = ph.moves("gathered", NI * 16 * G)
        kept, stored = ph.sem2("kept"), ph.sem2("stored")
        ring = ph.sb("ring", [P, 2 * G], I32)
        x, h, sums = ph.ring("x"), ph.ring("h"), ph.ring("sums")
        st, mv = ph.sb("st", [P, 2, G, 6]), ph.sb("mv", [P, 2, G, 2])
        sd, rs = ph.sb("sd", [P, 2, G]), ph.sb("rs", [P, 2, G])
        block = ph.block()

        @block.gpsimd
        def _(g):
            g.sem_inc(staged, 2)
            with g.Fori(0, NI) as i:
                for s in range(2):
                    wait_apart(g, k, vec, V.at(i - 1, "norm", s))
                    wait_apart(g, k, kept[s], i * 16)
                    gather_columns(nc, k, g, i, s, k.src_i, ring, staged, k.x, x, D, gathered)

        @block.sync
        def _(sp):
            with sp.Fori(0, NI) as i:
                for s in range(2):
                    sp.wait_ge(gathered[s], i * (16 * G) + (16 * G + gbase))
                    sp.dma_start(part(k.XS, i, s), slot(x, s)).then_inc(kept[s], 16)
                for s in range(2):
                    sp.wait_ge(vec, V.at(i, SUMS[-1], s))
                    sp.dma_start(part(k.V0, i, s), slot(sums, s)).then_inc(stored[s], 16)
            for s in range(2):
                sp.wait_ge(kept[s], NI * 16)
                sp.wait_ge(stored[s], NI * 16)

        @block.vector
        def _(d):
            d.memset(tile(sums, 1, G - 1), 0.0).then_inc(cleared, 1)
            d.wait_ge(cleared, 1)
            d.sem_inc(vec, V.per)
            with d.Fori(0, NI) as i:
                for s in range(2):
                    d.wait_ge(gathered[s], i * (16 * G) + (16 * G + gbase))
                    stats(nc, x, s, st).then_inc(vec, 1)
                for s in range(2):
                    wait_apart(d, k, vec, V.at(i, "stats", s))
                    aggregate(nc, s, st, mv).then_inc(vec, 1)
                for s in range(2):
                    d.wait_ge(act, A.at(i, "sd", s))
                    nc.vector.reciprocal(rs[:, s, :], sd[:, s, :]).then_inc(vec, 1)
                for s in range(2):
                    d.wait_ge(vec, V.at(i, "rs", s))
                    nc.vector.tensor_tensor(rs[:, s, :], rs[:, s, :], cols(k.norm_out, i, s, 0, G), ALU.mult).then_inc(vec, 1)
                for s in range(2):
                    d.wait_ge(vec, V.at(i, "rsn", s))
                    normalise(nc, x, s, mv, rs, h).then_inc(vec, 1)
                for s in range(2):
                    d.wait_ge(act, A.at(i, "relu", s))
                    d.wait_ge(stored[s], i * 16)
                    running_sum(nc, k, d, vec, V, i, s, h, sums)
            d.wait_ge(vec, V.last())
            d.tensor_copy(k.tail[:, :], tile(sums, 1, G - 1))

        @block.scalar
        def _(a):
            a.sem_inc(act, A.per)
            with a.Fori(0, NI) as i:
                for s in range(2):
                    a.wait_ge(vec, V.at(i, "aggr", s))
                    deviation(nc, k, s, mv, sd).then_inc(act, 1)
                for s in range(2):
                    a.wait_ge(vec, V.at(i, "norm", s))
                    nc.scalar.activation(slot(h, s), slot(h, s), ACT.Relu).then_inc(act, 1)


def conv1_nodes(nc, k):
    V = Steps("scaled")
    A = Steps("moved", "relu")
    M = Steps("turned", "product")
    with Phase(nc, k, "c1n") as ph:
        vec, act, pe = (ph.sem(n) for n in ("vector_steps", "scalar_steps", "tensor_steps"))
        loaded, stored = ph.sem2("loaded"), ph.sem2("stored")
        va, vT, y = ph.ring("va"), ph.ring("vT"), ph.ring("y")
        block = ph.block()

        @block.sync
        def _(sp):
            def load(i):
                for s in range(2):
                    sp.wait_ge(pe, M.at(i - 1, "turned", s))
                    sp.dma_start(slot(va, s), part(k.V0, i, s)).then_inc(loaded[s], 16)

            def store(i):
                for s in range(2):
                    sp.wait_ge(act, A.at(i, "relu", s))
                    sp.dma_start(part(k.T1, i, s), slot(y, s)).then_inc(stored[s], 16)
            load(0)
            with sp.Fori(1, NI) as i:
                load(i)
                store(i - 1)
            store(NI - 1)
            for s in range(2):
                sp.wait_ge(stored[s], NI * 16)

        @block.tensor
        def _(t):
            t.sem_inc(pe, M.per)
            with t.Fori(0, NI) as i:
                for s in range(2):
                    t.wait_ge(loaded[s], i * 16 + 16)
                    t.wait_ge(act, A.at(i - 1, "moved", s))
                    transposed(nc, k, va, s, pair(k, 2 * s)).then_inc(pe, 1)
                for s in range(2):
                    t.wait_ge(act, A.at(i, "moved", s))
                    t.wait_ge(vec, V.at(i - 1, "scaled", s))
                    times_rows(nc, vT, s, k.w0[:, 0, :], pair(k, 2 * s + 1)).then_inc(pe, 1)

        @block.scalar
        def _(a):
            a.sem_inc(act, A.per)
            with a.Fori(0, NI) as i:
                for s in range(2):
                    a.wait_ge(pe, M.at(i, "turned", s))
                    nc.scalar.activation(slot(vT, s), pair(k, 2 * s), ACT.Copy).then_inc(act, 1)
                for s in range(2):
                    a.wait_ge(vec, V.at(i, "scaled", s))
                    nc.scalar.activation(slot(y, s), slot(y, s), ACT.Relu).then_inc(act, 1)

        @block.vector
        def _(d):
            d.sem_inc(vec, V.per)
            with d.Fori(0, NI) as i:
                for s in range(2):
                    d.wait_ge(pe, M.at(i, "product", s))
                    d.wait_ge(stored[s], i * 16)
                    for c in range(G):
                        o = pair(k, 2 * s + 1)[:, c * D:(c + 1) * D]
                        last = nc.vector.scalar_tensor_tensor(tile(y, s, c), o, cols(k.norm_in, i, s, c),
                                                              k.b1_0[:, :], ALU.mult, ALU.add)
                    last.then_inc(vec, 1)


def conv2_edges(nc, k):
    V = Steps(*slotwise(*SUMS))
    A = Steps("scaled")
    with Phase(nc, k, "c2e") as ph:
        vec, act, staged, cleared = (ph.sem(n) for n in ("vector_steps", "scalar_steps", "staged", "cleared"))
        gathered, gbase = ph.moves("gathered", NI * 16 * G)
        stored = ph.sem2("stored")
        ring = ph.sb("ring", [P, 2 * G], I32)
        y, m, sums = ph.ring("y"), ph.ring("m"), ph.ring("sums")
        block = ph.block()

        @block.gpsimd
        def _(g):
            g.sem_inc(staged, 2)
            with g.Fori(0, NI) as i:
                for s in range(2):
                    wait_apart(g, k, act, A.at(i - 1, "scaled", s))
                    gather_columns(nc, k, g, i, s, k.slot_i, ring, staged, k.T1, y, D, gathered)

        @block.scalar
        def _(a):
            a.sem_inc(act, A.per)
            with a.Fori(0, NI) as i:
                for s in range(2):
                    a.wait_ge(gathered[s], i * (16 * G) + (16 * G + gbase))
                    a.wait_ge(vec, V.at(i - 1, SUMS[-1], s))
                    for c in range(G):
                        last = nc.scalar.activation(tile(m, s, c), tile(y, s, c), ACT.Copy, scale=cols(k.norm_out, i, s, c))
                    last.then_inc(act, 1)

        @block.vector
        def _(d):
            d.memset(tile(sums, 1, G - 1), 0.0).then_inc(cleared, 1)
            d.wait_ge(cleared, 1)
            d.sem_inc(vec, V.per)
            with d.Fori(0, NI) as i:
                for s in range(2):
                    d.wait_ge(act, A.at(i, "scaled", s))
                    d.wait_ge(stored[s], i * 16)
                    running_sum(nc, k, d, vec, V, i, s, m, sums)
            d.wait_ge(vec, V.last())
            d.tensor_copy(k.tail[:, :], tile(sums, 1, G - 1))

        @block.sync
        def _(sp):
            with sp.Fori(0, NI) as i:
                for s in range(2):
                    sp.wait_ge(vec, V.at(i, SUMS[-1], s))
                    sp.dma_start(part(k.V1, i, s), slot(sums, s)).then_inc(stored[s], 16)
            for s in range(2):
                sp.wait_ge(stored[s], NI * 16)


def conv2_nodes(nc, k):
    V = Steps("out", "x1", "stats", "aggr", "rs", "norm", "weighted", "score")
    A = Steps("moved", "sd", "relu")
    M = Steps("turned", "product")
    with Phase(nc, k, "c2n") as ph:
        vec, act, pe, staged = (ph.sem(n) for n in ("vector_steps", "scalar_steps", "tensor_steps", "staged"))
        gathered, gbase = ph.moves("gathered", NI * 16 * G)
        loaded, stored = ph.sem2("loaded"), ph.sem2("stored")
        ring = ph.sb("ring", [P, 2 * G], I32)
        va, vT, y, x, x1, h, hw = (ph.ring(n) for n in ("va", "vT", "y", "x", "x1", "h", "hw"))
        st, mv = ph.sb("st", [P, 2, G, 6]), ph.sb("mv", [P, 2, G, 2])
        sd, rs = ph.sb("sd", [P, 2, G]), ph.sb("rs", [P, 2, G])
        block = ph.block()

        @block.gpsimd
        def _(g):
            g.sem_inc(staged, 2)
            with g.Fori(0, NI) as i:
                for s in range(2):
                    wait_apart(g, k, vec, V.at(i - 1, "x1", s))
                    gather_columns(nc, k, g, i, s, k.dst_i, ring, staged, k.x, x, D, gathered)

        @block.sync
        def _(sp):
            def load(i):
                for s in range(2):
                    sp.wait_ge(pe, M.at(i - 1, "turned", s))
                    sp.dma_start(slot(va, s), part(k.V1, i, s)).then_inc(loaded[s], 16)

            def store(i):
                for s in range(2):
                    sp.wait_ge(vec, V.at(i, "x1", s))
                    sp.dma_start(part(k.T2, i, s), slot(y, s)).then_inc(stored[s], 16)
                    sp.dma_start(part(k.XD, i, s), slot(x1, s)).then_inc(stored[s], 16)
            load(0)
            with sp.Fori(1, NI) as i:
                load(i)
                store(i - 1)
            store(NI - 1)
            for s in range(2):
                sp.wait_ge(stored[s], NI * 32)

        @block.tensor
        def _(t):
            t.sem_inc(pe, M.per)
            with t.Fori(0, NI) as i:
                for s in range(2):
                    t.wait_ge(loaded[s], i * 16 + 16)
                    t.wait_ge(act, A.at(i - 1, "moved", s))
                    transposed(nc, k, va, s, pair(k, 2 * s)).then_inc(pe, 1)
                for s in range(2):
                    t.wait_ge(act, A.at(i, "moved", s))
                    t.wait_ge(vec, V.at(i - 1, "out", s))
                    times_rows(nc, vT, s, k.w0[:, 1, :], pair(k, 2 * s + 1)).then_inc(pe, 1)

        @block.scalar
        def _(a):
            a.sem_inc(act, A.per)
            with a.Fori(0, NI) as i:
                for s in range(2):
                    a.wait_ge(pe, M.at(i, "turned", s))
                    nc.scalar.activation(slot(vT, s), pair(k, 2 * s), ACT.Copy).then_inc(act, 1)
                for s in range(2):
                    a.wait_ge(vec, V.at(i, "aggr", s))
                    deviation(nc, k, s, mv, sd).then_inc(act, 1)
                for s in range(2):
                    a.wait_ge(vec, V.at(i, "norm", s))
                    nc.scalar.activation(slot(h, s), slot(h, s), ACT.Relu).then_inc(act, 1)

        @block.vector
        def _(d):
            d.sem_inc(vec, V.per)
            with d.Fori(0, NI) as i:
                for s in range(2):
                    d.wait_ge(pe, M.at(i, "product", s))
                    d.wait_ge(stored[s], i * 32)
                    for c in range(G):
                        o = pair(k, 2 * s + 1)[:, c * D:(c + 1) * D]
                        last = nc.vector.scalar_tensor_tensor(tile(y, s, c), o, cols(k.norm_in, i, s, c),
                                                              k.b2_0[:, :], ALU.mult, ALU.add)
                    last.then_inc(vec, 1)
                for s in range(2):
                    d.wait_ge(gathered[s], i * (16 * G) + (16 * G + gbase))
                    d.wait_ge(vec, V.at(i, "out", s))
                    nc.vector.tensor_tensor(slot(x1, s), slot(x, s), slot(y, s), ALU.add).then_inc(vec, 1)
                for s in range(2):
                    d.wait_ge(vec, V.at(i, "x1", s))
                    stats(nc, x1, s, st).then_inc(vec, 1)
                for s in range(2):
                    wait_apart(d, k, vec, V.at(i, "stats", s))
                    aggregate(nc, s, st, mv).then_inc(vec, 1)
                for s in range(2):
                    d.wait_ge(act, A.at(i, "sd", s))
                    nc.vector.reciprocal(rs[:, s, :], sd[:, s, :]).then_inc(vec, 1)
                for s in range(2):
                    d.wait_ge(vec, V.at(i, "rs", s))
                    normalise(nc, x1, s, mv, rs, h).then_inc(vec, 1)
                for s in range(2):
                    d.wait_ge(act, A.at(i, "relu", s))
                    nc.vector.tensor_tensor(by_tile(slot(hw, s)), by_tile(slot(h, s)), every(k.attn_r[:, :]), ALU.mult).then_inc(vec, 1)
                for s in range(2):
                    d.wait_ge(vec, V.at(i, "weighted", s))
                    nc.vector.tensor_reduce(small(k.sr, i, s), slot(hw, s).rearrange("p (k h e) -> p k h e", h=H8, e=D // H8),
                                            AX.X, ALU.add).then_inc(vec, 1)


def small(arr, i, s):
    return arr[:, :, bass.ds(i * (2 * G) + s * G, G)].rearrange("p f c -> p c f")


def relational_edges(nc, k, name, base, table, kept, first, groups, width, weights, scores):
    second = not first
    adds = ("x",) if first else ("ax", "bx", "x")
    V = Steps(*adds, "stats", "aggr", "rs", "norm", *(("u",) if second else ()), *slotwise("masked", "scores"))
    A = Steps("sd", "relu", *slotwise("moved", "message"))
    M = Steps(*slotwise(*(("turned", "base", "product") if first else ("turned", "product"))))
    rel_rows = k.relT8 if first else k.relT4
    with Phase(nc, k, name) as ph:
        vec, act, pe, staged = (ph.sem(n) for n in ("vector_steps", "scalar_steps", "tensor_steps", "staged"))
        gathered, gbase = ph.moves("gathered", NI * 16 * G)
        loaded, stored, told = ph.sem2("loaded"), ph.sem2("stored"), ph.sem2("message_stored")
        ring = ph.sb("ring", [P, 2 * G], I32)
        a_in, x_in, x1, h, rel, msg = (ph.ring(n) for n in ("a_in", "x_in", "x1", "h", "rel", "msg"))
        hT = ph.sb("hT", [P, W])
        masked = ph.sb("masked", [P, 4, W])
        ax = ph.ring("ax") if second else None
        st, mv = ph.sb("st", [P, 2, G, 6]), ph.sb("mv", [P, 2, G, 2])
        sd, rs = ph.sb("sd", [P, 2, G]), ph.sb("rs", [P, 2, G])
        block = ph.block()
        nstore = 32 if second else 16

        @block.gpsimd
        def _(g):
            g.sem_inc(staged, 2)
            with g.Fori(0, NI) as i:
                for s in range(2):
                    wait_apart(g, k, vec, V.at(i - 1, adds[0], s))
                    gather_columns(nc, k, g, i, s, k.slot_i, ring, staged, table, a_in, D, gathered)

        @block.sync
        def _(sp):
            def load(i):
                for s in range(2):
                    sp.wait_ge(vec, V.at(i - 1, "x", s))
                    sp.dma_start(slot(x_in, s), part(k.XS, i, s)).then_inc(loaded[s], 16)
                    sp.wait_ge(vec, V.at(i - 1, "masked", s))
                    t0 = i * (2 * G) + s * G
                    rows = rel_rows[bass.ds(t0, G), :].rearrange("(a t) p -> a (t p)", a=1).to_broadcast([P, W])
                    sp.dma_start(slot(rel, s), rows).then_inc(loaded[s], 16)

            def store(i):
                for s in range(2):
                    sp.wait_ge(vec, V.at(i, "x", s))
                    sp.dma_start(part(k.XS, i, s), slot(x1, s)).then_inc(stored[s], 16)
                if second:
                    for s in range(2):
                        sp.wait_ge(vec, V.at(i, "u", s))
                        sp.dma_start(part(k.HS, i, s), slot(ax, s)).then_inc(stored[s], 16)
                for s in range(2):
                    sp.wait_ge(act, A.at(i, "message", s))
                    sp.dma_start(part(k.MSG, i, s), slot(msg, s)).then_inc(told[s], 16)
            load(0)
            with sp.Fori(1, NI) as i:
                load(i)
                store(i - 1)
            store(NI - 1)
            for s in range(2):
                sp.wait_ge(stored[s], NI * nstore)
                sp.wait_ge(told[s], NI * 16)

        @block.vector
        def _(d):
            d.sem_inc(vec, V.per)
            with d.Fori(0, NI) as i:
                for s in range(2):
                    d.wait_ge(gathered[s], i * (16 * G) + (16 * G + gbase))
                    if first:
                        d.wait_ge(loaded[s], i * 32 + 32)
                        d.wait_ge(stored[s], i * nstore)
                        nc.vector.tensor_tensor(slot(x1, s), slot(a_in, s), slot(x_in, s), ALU.add).then_inc(vec, 1)
                    else:
                        d.wait_ge(stored[s], i * nstore)
                        nc.vector.tensor_tensor(by_tile(slot(ax, s)), by_tile(slot(a_in, s)), every(k.bn_a[:, :]), ALU.mult).then_inc(vec, 1)
                if second:
                    for s in range(2):
                        d.wait_ge(vec, V.at(i, "ax", s))
                        nc.vector.tensor_tensor(by_tile(slot(ax, s)), by_tile(slot(ax, s)), every(k.bn_b[:, :]), ALU.add).then_inc(vec, 1)
                    for s in range(2):
                        d.wait_ge(loaded[s], i * 32 + 32)
                        d.wait_ge(vec, V.at(i, "bx", s))
                        nc.vector.tensor_tensor(slot(x1, s), slot(ax, s), slot(x_in, s), ALU.add).then_inc(vec, 1)
                for s in range(2):
                    d.wait_ge(vec, V.at(i, "x", s))
                    stats(nc, x1, s, st).then_inc(vec, 1)
                for s in range(2):
                    wait_apart(d, k, vec, V.at(i, "stats", s))
                    aggregate(nc, s, st, mv).then_inc(vec, 1)
                for s in range(2):
                    d.wait_ge(act, A.at(i, "sd", s))
                    nc.vector.reciprocal(rs[:, s, :], sd[:, s, :]).then_inc(vec, 1)
                for s in range(2):
                    d.wait_ge(vec, V.at(i, "rs", s))
                    d.wait_ge(pe, M.at(i - 1, "turned", s))
                    normalise(nc, x1, s, mv, rs, h).then_inc(vec, 1)
                if second:
                    for s in range(2):
                        d.wait_ge(act, A.at(i, "relu", s))
                        nc.vector.tensor_tensor(by_tile(slot(ax, s)), by_tile(slot(h, s)), every(k.bias2[:, :]), ALU.add).then_inc(vec, 1)
                for s in range(2):
                    d.wait_ge(pe, M.at(i if s else i - 1, "product", 1 - s))
                    if first:
                        d.wait_ge(pe, M.at(i, "base", s))
                        right = pair(k, 1)
                    else:
                        d.wait_ge(act, A.at(i, "moved", s))
                        right = hT[:, :]
                    for c in range(4):
                        which = k.rel_of[:, c:c + 1] if first else float(c)
                        last = nc.vector.scalar_tensor_tensor(masked[:, c, :], slot(rel, s), which, right, ALU.is_equal, ALU.mult)
                    last.then_inc(vec, 1)
                    d.wait_ge(act, A.at(i, "message", s))
                    for c in range(G):
                        last = nc.vector.tensor_copy(scores[:, :, bass.ds(i * (2 * G) + (s * G + c), 1)].rearrange("p f c -> p (f c)"),
                                                     wide(k, 2, c, width)[:, D:width])
                    last.then_inc(vec, 1)

        @block.scalar
        def _(a):
            a.sem_inc(act, A.per)
            with a.Fori(0, NI) as i:
                for s in range(2):
                    a.wait_ge(vec, V.at(i, "aggr", s))
                    deviation(nc, k, s, mv, sd).then_inc(act, 1)
                for s in range(2):
                    a.wait_ge(vec, V.at(i, "norm", s))
                    nc.scalar.activation(slot(h, s), slot(h, s), ACT.Relu).then_inc(act, 1)
                for s in range(2):
                    a.wait_ge(pe, M.at(i, "turned", s))
                    if first:
                        a.wait_ge(pe, M.at(i if s else i - 1, "base", 1 - s))
                    else:
                        a.wait_ge(vec, V.at(i if s else i - 1, "masked", 1 - s))
                    nc.scalar.activation(hT[:, :], pair(k, 0), ACT.Copy).then_inc(act, 1)
                    a.wait_ge(pe, M.at(i, "product", s))
                    a.wait_ge(told[s], i * 16)
                    for c in range(G):
                        last = nc.scalar.activation(tile(msg, s, c), wide(k, 2, c, width)[:, 0:D], ACT.Copy)
                    last.then_inc(act, 1)

        @block.tensor
        def _(t):
            t.sem_inc(pe, M.per)
            with t.Fori(0, NI) as i:
                for s in range(2):
                    t.wait_ge(act, A.at(i, "relu", s))
                    t.wait_ge(act, A.at(i if s else i - 1, "moved", 1 - s))
                    transposed(nc, k, h, s, pair(k, 0)).then_inc(pe, 1)
                    if first:
                        t.wait_ge(act, A.at(i, "moved", s))
                        t.wait_ge(vec, V.at(i if s else i - 1, "masked", 1 - s))
                        nc.tensor.matmul(pair(k, 1)[:, 0:512], k.q2[:, :], hT[:, 0:512], start=True, stop=True)
                        nc.tensor.matmul(pair(k, 1)[:, 512:W], k.q2[:, :], hT[:, 512:W], start=True, stop=True).then_inc(pe, 1)
                    t.wait_ge(vec, V.at(i, "masked", s))
                    t.wait_ge(vec, V.at(i if s else i - 1, "scores", 1 - s))
                    t.wait_ge(act, A.at(i if s else i - 1, "message", 1 - s))
                    for c in range(G):
                        for r in range(4):
                            last = nc.tensor.matmul(wide(k, 2, c, width), masked[:, r, c * D:(c + 1) * D], weights[:, r, :],
                                                    start=(r == 0), stop=(r == 3))
                    last.then_inc(pe, 1)


class Chain:

    def __init__(self, eng, sem):
        self.eng, self.sem, self.n = eng, sem, 0

    def __call__(self, ins):
        self.n += 1
        ins.then_inc(self.sem, 1)
        self.eng.wait_ge(self.sem, self.n)


def fetch_back(nc, k, d, chain, to_pe, from_pe, n, ends, work, firsts, rest, F):
    chain(nc.vector.tensor_tensor(work, ends, k.fix[:, :].unsqueeze(1).to_broadcast([P, F, T]), ALU.mult))
    chain(nc.vector.tensor_reduce(firsts, work, AX.X, ALU.add))
    d.sem_inc(to_pe, 1)
    d.wait_ge(from_pe, n)
    chain(nc.vector.tensor_copy(rest, k.psum[:, 0:F]))
    chain(nc.vector.tensor_tensor(work, ends, k.end[:, :].unsqueeze(1).to_broadcast([P, F, T]), ALU.mult))
    for f in range(F):
        last = nc.vector.tensor_tensor_scan(ends[:, f, ::-1], k.more[:, ::-1], work[:, f, ::-1], rest[:, f:f + 1], ALU.mult, ALU.add)
    chain(last)


def weigh_heads1(nc, k):
    with Phase(nc, k, "att1") as ph:
        v, to_pe, from_pe, act = (ph.sem(n) for n in ("vector_done", "firsts_ready", "rest_ready", "exp_done"))
        work = ph.sb("work", [P, H8, T])
        firsts, rest = ph.sb("firsts", [P, H8]), ph.sb("rest", [P, H8])
        top = ph.sb("top", [P, T])
        block = ph.block()

        @block.vector
        def _(d):
            chain = Chain(d, v)
            fetch_back(nc, k, d, chain, to_pe, from_pe, 1, k.sr, work[:, :, :], firsts[:, :], rest[:, :], H8)
            chain(d.tensor_tensor(work[:, :, :], k.sl, k.sr, ALU.add))
            chain(d.scalar_tensor_tensor(k.sl, work[:, :, :], SLOPE, work[:, :, :], ALU.mult, ALU.max))
            chain(d.tensor_reduce(top[:, :], k.sl.rearrange("p h t -> p t h"), AX.X, ALU.max))
            chain(d.tensor_tensor(k.sl, k.sl, top[:, :].unsqueeze(1).to_broadcast([P, H8, T]), ALU.subtract))
            assert chain.n == 9
            d.wait_ge(act, 1)
            chain(d.tensor_reduce(top[:, :], k.sl.rearrange("p h t -> p t h"), AX.X, ALU.add))
            chain(d.reciprocal(top[:, :], top[:, :]))
            d.tensor_tensor(k.sl, k.sl, top[:, :].unsqueeze(1).to_broadcast([P, H8, T]), ALU.mult)

        @block.tensor
        def _(t):
            t.wait_ge(to_pe, 1)
            t.wait_ge(v, 2)
            nc.tensor.matmul(k.psum[:, 0:H8], k.back[:, :], firsts[:, :], start=True, stop=True).then_inc(from_pe, 1)

        @block.scalar
        def _(a):
            a.wait_ge(v, 9)
            nc.scalar.activation(k.sl, k.sl, ACT.Exp).then_inc(act, 1)


def weigh_edges2(nc, k):
    with Phase(nc, k, "att2") as ph:
        v, to_pe, from_pe, act = (ph.sem(n) for n in ("vector_done", "asked", "answered", "exp_done"))
        F = R4 * H4
        full = [P, R4, H4, T]
        is_rel = ph.sb("is_rel", [P, R4, T])
        val, acc, work = ph.sb("val", full), ph.sb("acc", full), ph.sb("work", full)
        tails = ph.sb("tails", [P, 3, F])
        own = ph.sb("own", [P, H4, T])
        spread = ph.sb("spread", [P, F, P])
        block = ph.block()
        rel_b = is_rel[:, :, :].unsqueeze(2).to_broadcast(full)
        flat = lambda b: b[:, :, :, :].rearrange("p r h t -> p (r h) t")

        @block.vector
        def _(d):
            chain = Chain(d, v)

            def own_of(arr4):
                chain(d.tensor_tensor(work[:, :, :, :], arr4, rel_b, ALU.mult))
                chain(d.tensor_reduce(own[:, :, :], work[:, :, :, :].rearrange("p r h t -> p h t r"), AX.X, ALU.add))

            def scan(op):
                for f in range(F):
                    last = d.tensor_tensor_scan(flat(acc)[:, f, :], k.cont[:, :], flat(val)[:, f, :], 0.0, ALU.mult, op)
                chain(last)
                chain(d.tensor_copy(tails[:, 0, :], flat(acc)[:, :, T - 1]))

            for r in range(R4):
                chain(d.tensor_scalar(is_rel[:, r, :], k.rel4[:, :], float(r), None, ALU.is_equal))
            fetch_back(nc, k, d, chain, to_pe, from_pe, 1, k.ed, flat(work), tails[:, 0, :], tails[:, 1, :], F)
            assert chain.n == 9
            own_of(k.ed.rearrange("p (r h) t -> p r h t", h=H4))
            chain(d.tensor_tensor(own[:, :, :], own[:, :, :], k.es, ALU.add))
            chain(d.scalar_tensor_tensor(k.es, own[:, :, :], SLOPE, own[:, :, :], ALU.mult, ALU.max))
            chain(d.tensor_tensor(val[:, :, :, :], k.es.unsqueeze(1).to_broadcast(full), rel_b, ALU.mult))
            scan(ALU.max)
            chain(d.tensor_tensor(spread[:, :, :], tails[:, 0, :].unsqueeze(2).to_broadcast([P, F, P]),
                                  k.ident[:, :].unsqueeze(1).to_broadcast([P, F, P]), ALU.mult))
            assert chain.n == 17
            d.sem_inc(to_pe, 1)
            d.wait_ge(from_pe, 2)
            chain(d.tensor_tensor(spread[:, :, :], k.psum[:, 0:F * P].rearrange("p (f q) -> p f q", q=P),
                                  k.intoT[:, :].unsqueeze(1).to_broadcast([P, F, P]), ALU.mult))
            chain(d.tensor_reduce(tails[:, 2, :], spread[:, :, :], AX.X, ALU.max))
            for f in range(F):
                last = d.scalar_tensor_tensor(flat(acc)[:, f, :], k.fix[:, :], tails[:, 2, f:f + 1], flat(acc)[:, f, :], ALU.mult, ALU.max)
            chain(last)
            fetch_back(nc, k, d, chain, to_pe, from_pe, 3, flat(acc), flat(work), tails[:, 0, :], tails[:, 1, :], F)
            assert chain.n == 25
            own_of(acc[:, :, :, :])
            chain(d.tensor_tensor(k.es, k.es, own[:, :, :], ALU.subtract))
            assert chain.n == 28
            d.wait_ge(act, 1)
            chain(d.tensor_tensor(val[:, :, :, :], k.es.unsqueeze(1).to_broadcast(full), rel_b, ALU.mult))
            scan(ALU.add)
            assert chain.n == 31
            d.sem_inc(to_pe, 1)
            d.wait_ge(from_pe, 4)
            chain(d.tensor_copy(tails[:, 2, :], k.psum[:, 0:F]))
            for f in range(F):
                last = d.scalar_tensor_tensor(flat(acc)[:, f, :], k.fix[:, :], tails[:, 2, f:f + 1], flat(acc)[:, f, :], ALU.mult, ALU.add)
            chain(last)
            fetch_back(nc, k, d, chain, to_pe, from_pe, 5, flat(acc), flat(work), tails[:, 0, :], tails[:, 1, :], F)
            assert chain.n == 38
            own_of(acc[:, :, :, :])
            chain(d.tensor_scalar(own[:, :, :], own[:, :, :], 1e-8, None, ALU.add))
            chain(d.reciprocal(own[:, :, :], own[:, :, :]))
            chain(d.tensor_tensor(k.es, k.es, own[:, :, :], ALU.mult))

        @block.scalar
        def _(a):
            a.wait_ge(v, 28)
            nc.scalar.activation(k.es, k.es, ACT.Exp).then_inc(act, 1)

        @block.tensor
        def _(t):
            def product(n, steps, weights, m):
                t.wait_ge(to_pe, n)
                t.wait_ge(v, steps)
                nc.tensor.matmul(k.psum[:, 0:F], weights[:, :], tails[:, m, :], start=True, stop=True).then_inc(from_pe, 1)
            product(1, 6, k.back, 0)
            t.wait_ge(to_pe, 2)
            t.wait_ge(v, 17)
            for c in range(4):
                last = nc.tensor.matmul(k.psum[:, c * 512:(c + 1) * 512], k.ones[:, :],
                                        spread[:, 4 * c:4 * c + 4, :].rearrange("p f q -> p (f q)"), start=True, stop=True)
            last.then_inc(from_pe, 1)
            product(3, 22, k.back, 0)
            product(4, 31, k.into, 0)
            product(5, 35, k.back, 0)


def weighted_edges(nc, k, name, heads, att, V_table):
    V = Steps("weighted", *slotwise(*SUMS))
    with Phase(nc, k, name) as ph:
        vec, cleared = ph.sem("vector_steps"), ph.sem("cleared")
        loaded, stored = ph.sem2("loaded"), ph.sem2("stored")
        m, w, sums = ph.ring("m"), ph.ring("w"), ph.ring("sums")
        block = ph.block()

        @block.sync
        def _(sp):
            def load(i):
                for s in range(2):
                    sp.wait_ge(vec, V.at(i - 1, "weighted", s))
                    sp.dma_start(slot(m, s), part(k.MSG, i, s)).then_inc(loaded[s], 16)

            def store(i):
                for s in range(2):
                    sp.wait_ge(vec, V.at(i, SUMS[-1], s))
                    sp.dma_start(part(V_table, i, s), slot(sums, s)).then_inc(stored[s], 16)
            load(0)
            with sp.Fori(1, NI) as i:
                load(i)
                store(i - 1)
            store(NI - 1)
            for s in range(2):
                sp.wait_ge(stored[s], NI * 16)

        @block.vector
        def _(d):
            d.memset(tile(sums, 1, G - 1), 0.0).then_inc(cleared, 1)
            d.wait_ge(cleared, 1)
            d.sem_inc(vec, V.per)
            with d.Fori(0, NI) as i:
                for s in range(2):
                    d.wait_ge(loaded[s], i * 16 + 16)
                    d.wait_ge(vec, V.at(i - 1, SUMS[-1], s))
                    e = D // heads
                    view = lambda b: slot(b, s).rearrange("p (k h e) -> p k h e", h=heads, e=e)
                    for c in range(G):
                        wt = att[:, :, bass.ds(i * (2 * G) + (s * G + c), 1)].to_broadcast([P, heads, e])
                        last = nc.vector.tensor_tensor(view(w)[:, c, :, :], view(m)[:, c, :, :], wt, ALU.mult)
                    last.then_inc(vec, 1)
                for s in range(2):
                    d.wait_ge(vec, V.at(i, "weighted", s))
                    d.wait_ge(stored[s], i * 16)
                    running_sum(nc, k, d, vec, V, i, s, w, sums)
            d.wait_ge(vec, V.last())
            d.tensor_copy(k.tail[:, :], tile(sums, 1, G - 1))


def batch_stats(nc, k):
    A = Steps("squared")
    M = Steps("summed")
    with Phase(nc, k, "bn") as ph:
        act, pe, v, tdone, ready = (ph.sem(n) for n in ("scalar_steps", "tensor_steps", "vector_done", "tensor_done", "sqrt_done"))
        loaded = ph.sem2("loaded")
        va, sq = ph.ring("va"), ph.ring("sq")
        c = ph.sb("c", [P, 6])
        dg = ph.sb("dg", [P, 2, P])
        block = ph.block()

        @block.sync
        def _(sp):
            with sp.Fori(0, NI) as i:
                for s in range(2):
                    sp.wait_ge(pe, M.at(i - 1, "summed", s))
                    sp.dma_start(slot(va, s), part(k.V2, i, s)).then_inc(loaded[s], 16)

        @block.scalar
        def _(a):
            a.sem_inc(act, A.per)
            with a.Fori(0, NI) as i:
                for s in range(2):
                    a.wait_ge(loaded[s], i * 16 + 16)
                    a.wait_ge(pe, M.at(i - 1, "summed", s))
                    nc.scalar.activation(slot(sq, s), slot(va, s), ACT.Square).then_inc(act, 1)
            a.wait_ge(v, 4)
            nc.scalar.activation(c[:, 3:4], c[:, 2:3], ACT.Sqrt, bias=k.eps[:, 0:1]).then_inc(ready, 1)

        @block.tensor
        def _(t):
            S, Q = k.psum[:, 0:1], k.psum[:, 512:513]
            nc.tensor.matmul(S, k.zeros[:, :], k.ones[:, 0:1], start=True, stop=False, skip_group_check=True)
            nc.tensor.matmul(Q, k.zeros[:, :], k.ones[:, 0:1], start=True, stop=False, skip_group_check=True)
            t.sem_inc(pe, M.per)
            with t.Fori(0, NI) as i:
                for s in range(2):
                    t.wait_ge(loaded[s], i * 16 + 16)
                    t.wait_ge(act, A.at(i, "squared", s))
                    for j in range(G):
                        nc.tensor.matmul(S, tile(va, s, j), cols(k.real_end, i, s, j), start=False, stop=False, skip_group_check=True)
                        last = nc.tensor.matmul(Q, tile(sq, s, j), cols(k.real_end, i, s, j), start=False, stop=False, skip_group_check=True)
                    last.then_inc(pe, 1)
            t.wait_ge(v, 10)
            nc.tensor.matmul(k.psum[:, 1024:1024 + 2 * P], k.ones[:, :], dg[:, :, :].rearrange("p a q -> p (a q)"),
                             start=True, stop=True).then_inc(tdone, 1)

        @block.vector
        def _(d):
            chain = Chain(d, v)
            d.wait_ge(pe, M.last())
            chain(d.tensor_scalar(c[:, 0:1], k.psum[:, 0:1], 1.0 / NODES, None, ALU.mult))
            chain(d.tensor_scalar(c[:, 1:2], k.psum[:, 512:513], 1.0 / NODES, None, ALU.mult))
            chain(d.tensor_tensor(c[:, 2:3], c[:, 0:1], c[:, 0:1], ALU.mult))
            chain(d.tensor_tensor(c[:, 2:3], c[:, 1:2], c[:, 2:3], ALU.subtract))
            d.wait_ge(ready, 1)
            chain(d.reciprocal(c[:, 3:4], c[:, 3:4]))
            chain(d.tensor_tensor(c[:, 3:4], c[:, 3:4], k.gb[:, 0:1], ALU.mult))
            chain(d.tensor_tensor(c[:, 4:5], c[:, 0:1], c[:, 3:4], ALU.mult))
            chain(d.tensor_tensor(c[:, 4:5], k.gb[:, 1:2], c[:, 4:5], ALU.subtract))
            chain(d.tensor_scalar(dg[:, 0, :], k.ident[:, :], c[:, 3:4], None, ALU.mult))
            chain(d.tensor_scalar(dg[:, 1, :], k.ident[:, :], c[:, 4:5], None, ALU.mult))
            d.wait_ge(tdone, 1)
            chain(d.tensor_copy(k.bn_a[:, :], k.psum[:, 1024:1024 + P]))
            chain(d.tensor_copy(k.bn_b[:, :], k.psum[:, 1024 + P:1024 + 2 * P]))
            chain(d.tensor_tensor(k.plain[:, :], k.bn_b[:, :], k.b2_0[:, :], ALU.add))


def layer2_nodes(nc, k):
    V = Steps("ax", "bx", "x", "stats", "aggr", "rs", "norm", "u", "scores")
    A = Steps("sd", "relu", "moved")
    M = Steps("turned", "product")
    F = R4 * H4
    with Phase(nc, k, "n2") as ph:
        vec, act, pe = (ph.sem(n) for n in ("vector_steps", "scalar_steps", "tensor_steps"))
        loaded, stored = ph.sem2("loaded"), ph.sem2("stored")
        a_in, x_in, ax, x1, h, hT = (ph.ring(n) for n in ("a_in", "x_in", "ax", "x1", "h", "hT"))
        st, mv = ph.sb("st", [P, 2, G, 6]), ph.sb("mv", [P, 2, G, 2])
        sd, rs = ph.sb("sd", [P, 2, G]), ph.sb("rs", [P, 2, G])
        block = ph.block()

        @block.sync
        def _(sp):
            def load(i):
                for s in range(2):
                    sp.wait_ge(vec, V.at(i - 1, "x", s))
                    sp.dma_start(slot(a_in, s), part(k.V2, i, s)).then_inc(loaded[s], 16)
                    sp.dma_start(slot(x_in, s), part(k.XD, i, s)).then_inc(loaded[s], 16)

            def store(i):
                for s in range(2):
                    sp.wait_ge(vec, V.at(i, "x", s))
                    sp.dma_start(part(k.XD, i, s), slot(x1, s)).then_inc(stored[s], 16)
                for s in range(2):
                    sp.wait_ge(vec, V.at(i, "u", s))
                    sp.dma_start(part(k.HD, i, s), slot(ax, s)).then_inc(stored[s], 16)
            load(0)
            with sp.Fori(1, NI) as i:
                load(i)
                store(i - 1)
            store(NI - 1)
            for s in range(2):
                sp.wait_ge(stored[s], NI * 32)

        @block.vector
        def _(d):
            d.sem_inc(vec, V.per)
            with d.Fori(0, NI) as i:
                for s in range(2):
                    d.wait_ge(loaded[s], i * 32 + 32)
                    d.wait_ge(stored[s], i * 32)
                    nc.vector.tensor_tensor(by_tile(slot(ax, s)), by_tile(slot(a_in, s)), every(k.bn_a[:, :]), ALU.mult).then_inc(vec, 1)
                for s in range(2):
                    d.wait_ge(vec, V.at(i, "ax", s))
                    nc.vector.tensor_tensor(by_tile(slot(ax, s)), by_tile(slot(ax, s)), every(k.bn_b[:, :]), ALU.add).then_inc(vec, 1)
                for s in range(2):
                    d.wait_ge(vec, V.at(i, "bx", s))
                    nc.vector.tensor_tensor(slot(x1, s), slot(ax, s), slot(x_in, s), ALU.add).then_inc(vec, 1)
                for s in range(2):
                    d.wait_ge(vec, V.at(i, "x", s))
                    stats(nc, x1, s, st).then_inc(vec, 1)
                for s in range(2):
                    wait_apart(d, k, vec, V.at(i, "stats", s))
                    aggregate(nc, s, st, mv).then_inc(vec, 1)
                for s in range(2):
                    d.wait_ge(act, A.at(i, "sd", s))
                    nc.vector.reciprocal(rs[:, s, :], sd[:, s, :]).then_inc(vec, 1)
                for s in range(2):
                    d.wait_ge(vec, V.at(i, "rs", s))
                    d.wait_ge(pe, M.at(i - 1, "turned", s))
                    normalise(nc, x1, s, mv, rs, h).then_inc(vec, 1)
                for s in range(2):
                    d.wait_ge(act, A.at(i, "relu", s))
                    nc.vector.tensor_tensor(by_tile(slot(ax, s)), by_tile(slot(h, s)), every(k.bias2[:, :]), ALU.add).then_inc(vec, 1)
                for s in range(2):
                    d.wait_ge(pe, M.at(i, "product", s))
                    got = pair(k, 2 * s + 1)[:, 0:G * F].rearrange("p (c f) -> p c f", f=F)
                    nc.vector.tensor_copy(small(k.ed, i, s), got).then_inc(vec, 1)

        @block.scalar
        def _(a):
            a.sem_inc(act, A.per)
            with a.Fori(0, NI) as i:
                for s in range(2):
                    a.wait_ge(vec, V.at(i, "aggr", s))
                    deviation(nc, k, s, mv, sd).then_inc(act, 1)
                for s in range(2):
                    a.wait_ge(vec, V.at(i, "norm", s))
                    nc.scalar.activation(slot(h, s), slot(h, s), ACT.Relu).then_inc(act, 1)
                for s in range(2):
                    a.wait_ge(pe, M.at(i, "turned", s))
                    nc.scalar.activation(slot(hT, s), pair(k, 2 * s), ACT.Copy).then_inc(act, 1)

        @block.tensor
        def _(t):
            t.sem_inc(pe, M.per)
            with t.Fori(0, NI) as i:
                for s in range(2):
                    t.wait_ge(act, A.at(i, "relu", s))
                    t.wait_ge(act, A.at(i - 1, "moved", s))
                    transposed(nc, k, h, s, pair(k, 2 * s)).then_inc(pe, 1)
                for s in range(2):
                    t.wait_ge(act, A.at(i, "moved", s))
                    t.wait_ge(vec, V.at(i - 1, "scores", s))
                    for c in range(G):
                        last = nc.tensor.matmul(pair(k, 2 * s + 1)[:, c * F:(c + 1) * F], tile(hT, s, c), k.vdst[:, :], start=True, stop=True)
                    last.then_inc(pe, 1)


def layer3_inputs(nc, k, name, edges):
    V = Steps("o", "stats", "aggr", "rs", "norm", "scaled", "shifted", "x", "stats2", "aggr2", "rs2", "norm2",
              *(slotwise(*SUMS) if edges else ()))
    A = Steps("sd", "sd2", "relu")
    x_table, u_table = (k.XS, k.HS) if edges else (k.XD, k.HD)
    with Phase(nc, k, name) as ph:
        vec, act, staged, cleared = (ph.sem(n) for n in ("vector_steps", "scalar_steps", "staged", "cleared"))
        gathered, gbase = ph.moves("gathered", NI * 16 * G if edges else 0)
        loaded, stored = ph.sem2("loaded"), ph.sem2("stored")
        summed = ph.sem2("sums_stored")
        ring = ph.sb("ring", [P, 2 * G], I32)
        a_in, u_in, x_in, o, y, x3, h = (ph.ring(n) for n in ("a_in", "u_in", "x_in", "o", "y", "x3", "h"))
        sums = ph.ring("sums") if edges else None
        st, mv = ph.sb("st", [P, 2, G, 6]), ph.sb("mv", [P, 2, G, 2])
        sd, rs = ph.sb("sd", [P, 2, G]), ph.sb("rs", [P, 2, G])
        block = ph.block()
        nload = 32 if edges else 48
        nstore = 16 if edges else 32

        if edges:
            @block.gpsimd
            def _(g):
                g.sem_inc(staged, 2)
                with g.Fori(0, NI) as i:
                    for s in range(2):
                        wait_apart(g, k, vec, V.at(i - 1, "o", s))
                        gather_columns(nc, k, g, i, s, k.slot_i, ring, staged, k.V3, a_in, D, gathered)

        @block.sync
        def _(sp):
            def load(i):
                for s in range(2):
                    sp.wait_ge(vec, V.at(i - 1, "x", s))
                    if not edges:
                        sp.dma_start(slot(a_in, s), part(k.V3, i, s)).then_inc(loaded[s], 16)
                    sp.dma_start(slot(u_in, s), part(u_table, i, s)).then_inc(loaded[s], 16)
                    sp.dma_start(slot(x_in, s), part(x_table, i, s)).then_inc(loaded[s], 16)

            def store(i):
                if not edges:
                    for s in range(2):
                        sp.wait_ge(vec, V.at(i, "x", s))
                        sp.dma_start(part(k.XD, i, s), slot(x3, s)).then_inc(stored[s], 16)
                for s in range(2):
                    sp.wait_ge(act, A.at(i, "relu", s))
                    sp.dma_start(part(u_table, i, s), slot(h, s)).then_inc(stored[s], 16)
                if edges:
                    for s in range(2):
                        sp.wait_ge(vec, V.at(i, SUMS[-1], s))
                        sp.dma_start(part(k.V4, i, s), slot(sums, s)).then_inc(summed[s], 16)
            load(0)
            with sp.Fori(1, NI) as i:
                load(i)
                store(i - 1)
            store(NI - 1)
            for s in range(2):
                sp.wait_ge(stored[s], NI * nstore)
                if edges:
                    sp.wait_ge(summed[s], NI * 16)

        @block.vector
        def _(d):
            if edges:
                d.memset(tile(sums, 1, G - 1), 0.0).then_inc(cleared, 1)
                d.wait_ge(cleared, 1)
            d.sem_inc(vec, V.per)
            with d.Fori(0, NI) as i:
                for s in range(2):
                    if edges:
                        d.wait_ge(gathered[s], i * (16 * G) + (16 * G + gbase))
                    d.wait_ge(loaded[s], i * nload + nload)
                    nc.vector.tensor_tensor(slot(o, s), slot(a_in, s), slot(u_in, s), ALU.add).then_inc(vec, 1)
                for s in range(2):
                    d.wait_ge(vec, V.at(i, "o", s))
                    stats(nc, o, s, st).then_inc(vec, 1)
                for s in range(2):
                    wait_apart(d, k, vec, V.at(i, "stats", s))
                    aggregate(nc, s, st, mv).then_inc(vec, 1)
                for s in range(2):
                    d.wait_ge(act, A.at(i, "sd", s))
                    nc.vector.reciprocal(rs[:, s, :], sd[:, s, :]).then_inc(vec, 1)
                for s in range(2):
                    d.wait_ge(vec, V.at(i, "rs", s))
                    normalise(nc, o, s, mv, rs, y).then_inc(vec, 1)
                for s in range(2):
                    d.wait_ge(vec, V.at(i, "norm", s))
                    nc.vector.tensor_tensor(by_tile(slot(y, s)), by_tile(slot(y, s)), every(k.ln_g[:, :]), ALU.mult).then_inc(vec, 1)
                for s in range(2):
                    d.wait_ge(vec, V.at(i, "scaled", s))
                    nc.vector.tensor_tensor(by_tile(slot(y, s)), by_tile(slot(y, s)), every(k.ln_b[:, :]), ALU.add).then_inc(vec, 1)
                for s in range(2):
                    d.wait_ge(vec, V.at(i, "shifted", s))
                    d.wait_ge(stored[s], i * nstore)
                    nc.vector.tensor_tensor(slot(x3, s), slot(y, s), slot(x_in, s), ALU.add).then_inc(vec, 1)
                for s in range(2):
                    d.wait_ge(vec, V.at(i, "x", s))
                    stats(nc, x3, s, st).then_inc(vec, 1)
                for s in range(2):
                    wait_apart(d, k, vec, V.at(i, "stats2", s))
                    aggregate(nc, s, st, mv).then_inc(vec, 1)
                for s in range(2):
                    d.wait_ge(act, A.at(i, "sd2", s))
                    nc.vector.reciprocal(rs[:, s, :], sd[:, s, :]).then_inc(vec, 1)
                for s in range(2):
                    d.wait_ge(vec, V.at(i, "rs2", s))
                    normalise(nc, x3, s, mv, rs, h).then_inc(vec, 1)
                if edges:
                    for s in range(2):
                        d.wait_ge(act, A.at(i, "relu", s))
                        d.wait_ge(summed[s], i * 16)
                        running_sum(nc, k, d, vec, V, i, s, h, sums)
            if edges:
                d.wait_ge(vec, V.last())
                d.tensor_copy(k.tail[:, :], tile(sums, 1, G - 1))

        @block.scalar
        def _(a):
            a.sem_inc(act, A.per)
            with a.Fori(0, NI) as i:
                for s in range(2):
                    a.wait_ge(vec, V.at(i, "aggr", s))
                    deviation(nc, k, s, mv, sd).then_inc(act, 1)
                for s in range(2):
                    a.wait_ge(vec, V.at(i, "aggr2", s))
                    deviation(nc, k, s, mv, sd).then_inc(act, 1)
                for s in range(2):
                    a.wait_ge(vec, V.at(i, "norm2", s))
                    nc.scalar.activation(slot(h, s), slot(h, s), ACT.Relu).then_inc(act, 1)


def graph_mlp(nc, k, name, edges, layer):
    final = layer == 1
    V = Steps("z", "biased", *(("out",) if final else ()), *(slotwise(*SUMS) if edges else ()))
    A = Steps("moved", "hidden", *(() if final else ("relu",)))
    M = Steps("turned", "inner", "product")
    sum_table = k.V5 if final else k.V4
    with Phase(nc, k, name) as ph:
        vec, act, pe, staged, cleared = (ph.sem(n) for n in ("vector_steps", "scalar_steps", "tensor_steps", "staged", "cleared"))
        gathered, gbase = ph.moves("gathered", NI * 16 * G if edges else 0)
        scattered, sbase = ph.moves("scattered", NI * 16 * G if final else 0)
        loaded, stored = ph.sem2("loaded"), ph.sem2("stored")
        ring = ph.sb("ring", [P, 2 * G], I32)
        a_in, h_in, z, zT, hidden, y = (ph.ring(n) for n in ("a_in", "h_in", "z", "zT", "hidden", "y"))
        x_in = ph.ring("x_in") if final else None
        sums = ph.ring("sums") if edges else None
        block = ph.block()
        nload = 16 + 16 * (not edges) + 16 * final
        w_in, w_out = k.w3[:, 2 * layer, :], k.w3[:, 2 * layer + 1, :]
        b_in, b_out = k.b3[:, 2 * layer:2 * layer + 1], k.b3_row[:, layer, :]

        @block.gpsimd
        def _(g):
            if edges or final:
                g.sem_inc(staged, 2)
                with g.Fori(0, NI) as i:
                    for s in range(2):
                        if edges:
                            wait_apart(g, k, vec, V.at(i - 1, "z", s))
                            gather_columns(nc, k, g, i, s, k.slot_i, ring, staged, k.V4, a_in, D, gathered)
                        else:
                            wait_apart(g, k, scattered[s], i * (16 * G) + sbase)
                            g.tensor_copy(ring[:, s * G:(s + 1) * G], cols(k.out_i, i, s, 0, G)).then_inc(staged, 1)
                            wait_apart(g, k, staged, i * 2 + (s + 3))
                            wait_apart(g, k, vec, V.at(i, "out", s))
                            for c in range(G):
                                at = bass.IndirectOffsetOnAxis(ap=ring[:, s * G + c:s * G + c + 1], axis=0)
                                g.indirect_dma_start(k.out, at, tile(y, s, c), None, bounds_check=NODES - 1,
                                                     oob_is_err=False).then_inc(scattered[s], 16)
                if final:
                    for s in range(2):
                        g.wait_ge(scattered[s], NI * 16 * G + sbase)

        @block.sync
        def _(sp):
            def load(i):
                for s in range(2):
                    sp.wait_ge(vec, V.at(i - 1, "z", s))
                    if not edges:
                        sp.dma_start(slot(a_in, s), part(sum_table, i, s)).then_inc(loaded[s], 16)
                    sp.dma_start(slot(h_in, s), part(k.HS if edges else k.HD, i, s)).then_inc(loaded[s], 16)
                    if final:
                        sp.wait_ge(vec, V.at(i - 1, "out", s))
                        sp.dma_start(slot(x_in, s), part(k.XD, i, s)).then_inc(loaded[s], 16)

            def store(i):
                for s in range(2):
                    if edges:
                        sp.wait_ge(vec, V.at(i, SUMS[-1], s))
                        sp.dma_start(part(k.V5, i, s), slot(sums, s)).then_inc(stored[s], 16)
                    elif not final:
                        sp.wait_ge(act, A.at(i, "relu", s))
                        sp.dma_start(part(k.HD, i, s), slot(y, s)).then_inc(stored[s], 16)
            load(0)
            with sp.Fori(1, NI) as i:
                load(i)
                store(i - 1)
            store(NI - 1)
            if not final:
                for s in range(2):
                    sp.wait_ge(stored[s], NI * 16)

        @block.vector
        def _(d):
            if edges:
                d.memset(tile(sums, 1, G - 1), 0.0).then_inc(cleared, 1)
                d.wait_ge(cleared, 1)
            d.sem_inc(vec, V.per)
            with d.Fori(0, NI) as i:
                for s in range(2):
                    if edges:
                        d.wait_ge(gathered[s], i * (16 * G) + (16 * G + gbase))
                    d.wait_ge(loaded[s], i * nload + nload)
                    d.wait_ge(pe, M.at(i - 1, "turned", s))
                    nc.vector.tensor_tensor(slot(z, s), slot(a_in, s), slot(h_in, s), ALU.add).then_inc(vec, 1)
                for s in range(2):
                    d.wait_ge(pe, M.at(i, "product", s))
                    if final:
                        d.wait_ge(scattered[s], i * (16 * G) + sbase)
                    elif edges:
                        d.wait_ge(vec, V.at(i - 1, SUMS[-1], s))
                    else:
                        d.wait_ge(stored[s], i * 16)
                    nc.vector.tensor_tensor(by_tile(slot(y, s)), by_tile(pair(k, 2 * s)), every(b_out), ALU.add).then_inc(vec, 1)
                if final:
                    for s in range(2):
                        d.wait_ge(vec, V.at(i, "biased", s))
                        nc.vector.scalar_tensor_tensor(slot(y, s), slot(y, s), 0.0, slot(x_in, s), ALU.max, ALU.add).then_inc(vec, 1)
                if edges:
                    for s in range(2):
                        d.wait_ge(act, A.at(i, "relu", s))
                        d.wait_ge(stored[s], i * 16)
                        running_sum(nc, k, d, vec, V, i, s, y, sums)
            if edges:
                d.wait_ge(vec, V.last())
                d.tensor_copy(k.tail[:, :], tile(sums, 1, G - 1))

        @block.scalar
        def _(a):
            a.sem_inc(act, A.per)
            with a.Fori(0, NI) as i:
                for s in range(2):
                    a.wait_ge(pe, M.at(i, "turned", s))
                    nc.scalar.activation(slot(zT, s), pair(k, 2 * s), ACT.Copy).then_inc(act, 1)
                for s in range(2):
                    a.wait_ge(pe, M.at(i, "inner", s))
                    nc.scalar.activation(slot(hidden, s), pair(k, 2 * s + 1), ACT.Relu, bias=b_in).then_inc(act, 1)
                if not final:
                    for s in range(2):
                        a.wait_ge(vec, V.at(i, "biased", s))
                        nc.scalar.activation(slot(y, s), slot(y, s), ACT.Relu).then_inc(act, 1)

        @block.tensor
        def _(t):
            t.sem_inc(pe, M.per)
            with t.Fori(0, NI) as i:
                for s in range(2):
                    t.wait_ge(vec, V.at(i, "z", s))
                    t.wait_ge(vec, V.at(i - 1, "biased", s))
                    transposed(nc, k, z, s, pair(k, 2 * s)).then_inc(pe, 1)
                for s in range(2):
                    t.wait_ge(act, A.at(i, "moved", s))
                    times_cols(nc, zT, s, w_in, pair(k, 2 * s + 1)).then_inc(pe, 1)
                for s in range(2):
                    t.wait_ge(act, A.at(i, "hidden", s))
                    times_rows(nc, hidden, s, w_out, pair(k, 2 * s)).then_inc(pe, 1)


def all_nodes(nc, k):
    ROWS = P * G
    V = Steps("x2", "stats", "aggr", "rs", "norm", "u", "stats2", "aggr2", "rs2", "norm2", "scaled", "shifted", "x3",
              "stats3", "aggr3", "rs3", "norm3", "biased", "out")
    A = Steps("sd", "relu", "sd2", "sd3", "moved", "hidden1", "hidden2", "hidden3")
    M = Steps("turned", "inner1", "inner2", "inner3", "product")
    N = -(-NODES // ROWS) // 2
    with Phase(nc, k, "all") as ph:
        vec, act, pe = (ph.sem(n) for n in ("vector_steps", "scalar_steps", "tensor_steps"))
        loaded, stored = ph.sem2("loaded"), ph.sem2("stored")
        x_in, x, h, u, y, x3, hT, aT, out = (ph.ring(n) for n in ("x_in", "x", "h", "u", "y", "x3", "hT", "aT", "out"))
        st, mv = ph.sb("st", [P, 2, G, 6]), ph.sb("mv", [P, 2, G, 2])
        sd, rs = ph.sb("sd", [P, 2, G]), ph.sb("rs", [P, 2, G])
        block = ph.block()

        def rows(table, i, s):
            first = NODES - ROWS if (isinstance(i, int) and i == N - 1 and s == 1) else i * (2 * ROWS) + s * ROWS
            return table[bass.ds(first, ROWS), :].rearrange("(p k) f -> p (k f)", k=G)

        @block.sync
        def _(sp):
            def load(i):
                for s in range(2):
                    sp.wait_ge(vec, V.at(i - 1, "x2", s))
                    sp.dma_start(slot(x_in, s), rows(k.x, i, s)).then_inc(loaded[s], 16)

            def store(i):
                for s in range(2):
                    sp.wait_ge(vec, V.at(i, "out", s))
                    if isinstance(i, int) and i == N - 1 and s == 1:
                        sp.wait_ge(stored[0], N * 16)
                    sp.dma_start(rows(k.out, i, s), slot(out, s)).then_inc(stored[s], 16)
            load(0)
            with sp.Fori(1, N - 1) as i:
                load(i)
                store(i - 1)
            load(N - 1)
            store(N - 2)
            store(N - 1)
            for s in range(2):
                sp.wait_ge(stored[s], N * 16)

        @block.vector
        def _(d):
            d.sem_inc(vec, V.per)
            with d.Fori(0, N) as i:
                def norm(src, dst, n, before=None):
                    for s in range(2):
                        d.wait_ge(vec, V.at(i, before, s))
                        stats(nc, src, s, st).then_inc(vec, 1)
                    for s in range(2):
                        wait_apart(d, k, vec, V.at(i, "stats" + n, s))
                        aggregate(nc, s, st, mv).then_inc(vec, 1)
                    for s in range(2):
                        d.wait_ge(act, A.at(i, "sd" + n, s))
                        nc.vector.reciprocal(rs[:, s, :], sd[:, s, :]).then_inc(vec, 1)
                    for s in range(2):
                        d.wait_ge(vec, V.at(i, "rs" + n, s))
                        d.wait_ge(pe, M.at(i - 1, "turned", s))
                        normalise(nc, src, s, mv, rs, dst).then_inc(vec, 1)

                for s in range(2):
                    d.wait_ge(loaded[s], i * 16 + 16)
                    nc.vector.tensor_tensor(by_tile(slot(x, s)), by_tile(slot(x_in, s)), every(k.plain[:, :]), ALU.add).then_inc(vec, 1)
                norm(x, h, "", "x2")
                for s in range(2):
                    d.wait_ge(act, A.at(i, "relu", s))
                    nc.vector.tensor_tensor(by_tile(slot(u, s)), by_tile(slot(h, s)), every(k.bias2[:, :]), ALU.add).then_inc(vec, 1)
                norm(u, y, "2", "u")
                for s in range(2):
                    d.wait_ge(vec, V.at(i, "norm2", s))
                    nc.vector.tensor_tensor(by_tile(slot(y, s)), by_tile(slot(y, s)), every(k.ln_g[:, :]), ALU.mult).then_inc(vec, 1)
                for s in range(2):
                    d.wait_ge(vec, V.at(i, "scaled", s))
                    nc.vector.tensor_tensor(by_tile(slot(y, s)), by_tile(slot(y, s)), every(k.ln_b[:, :]), ALU.add).then_inc(vec, 1)
                for s in range(2):
                    d.wait_ge(vec, V.at(i, "shifted", s))
                    nc.vector.tensor_tensor(slot(x3, s), slot(y, s), slot(x, s), ALU.add).then_inc(vec, 1)
                norm(x3, h, "3", "x3")
                for s in range(2):
                    d.wait_ge(pe, M.at(i, "product", s))
                    d.wait_ge(stored[s], i * 16)
                    nc.vector.tensor_tensor(by_tile(slot(out, s)), by_tile(pair(k, 2 * s)), every(k.b3_row[:, 1, :]), ALU.add).then_inc(vec, 1)
                for s in range(2):
                    d.wait_ge(vec, V.at(i, "biased", s))
                    nc.vector.scalar_tensor_tensor(slot(out, s), slot(out, s), 0.0, slot(x3, s), ALU.max, ALU.add).then_inc(vec, 1)

        @block.scalar
        def _(a):
            a.sem_inc(act, A.per)
            with a.Fori(0, N) as i:
                for s in range(2):
                    a.wait_ge(vec, V.at(i, "aggr", s))
                    deviation(nc, k, s, mv, sd).then_inc(act, 1)
                for s in range(2):
                    a.wait_ge(vec, V.at(i, "norm", s))
                    nc.scalar.activation(slot(h, s), slot(h, s), ACT.Relu).then_inc(act, 1)
                for n in ("2", "3"):
                    for s in range(2):
                        a.wait_ge(vec, V.at(i, "aggr" + n, s))
                        deviation(nc, k, s, mv, sd).then_inc(act, 1)
                for s in range(2):
                    a.wait_ge(pe, M.at(i, "turned", s))
                    nc.scalar.activation(slot(hT, s), pair(k, 2 * s), ACT.Relu).then_inc(act, 1)
                for n, (src, dst) in enumerate(((1, aT), (0, hT), (1, aT))):
                    for s in range(2):
                        a.wait_ge(pe, M.at(i, f"inner{n + 1}", s))
                        nc.scalar.activation(slot(dst, s), pair(k, 2 * s + src), ACT.Relu, bias=k.b3[:, n:n + 1]).then_inc(act, 1)

        @block.tensor
        def _(t):
            t.sem_inc(pe, M.per)
            with t.Fori(0, N) as i:
                for s in range(2):
                    t.wait_ge(vec, V.at(i, "norm3", s))
                    t.wait_ge(vec, V.at(i - 1, "biased", s))
                    transposed(nc, k, h, s, pair(k, 2 * s)).then_inc(pe, 1)
                for s in range(2):
                    t.wait_ge(act, A.at(i, "moved", s))
                    times_cols(nc, hT, s, k.w3[:, 0, :], pair(k, 2 * s + 1)).then_inc(pe, 1)
                for s in range(2):
                    t.wait_ge(act, A.at(i, "hidden1", s))
                    times_cols(nc, aT, s, k.w3[:, 1, :], pair(k, 2 * s)).then_inc(pe, 1)
                for s in range(2):
                    t.wait_ge(act, A.at(i, "hidden2", s))
                    times_cols(nc, hT, s, k.w3[:, 2, :], pair(k, 2 * s + 1)).then_inc(pe, 1)
                for s in range(2):
                    t.wait_ge(act, A.at(i, "hidden3", s))
                    times_rows(nc, aT, s, k.w3[:, 3, :], pair(k, 2 * s)).then_inc(pe, 1)


def build(nc, x, src, dst, et4, et8, w, out, upto=99):
    with ExitStack() as ctx:
        k = Shared()
        k.x, k.src, k.dst, k.et4, k.et8, k.w, k.out = x, src, dst, et4, et8, w, out

        def dram(name, shape, dt=F32):
            return nc.dram_tensor(name, shape, dt, kind="Internal").ap()

        def sb(name, shape, dt=F32):
            return ctx.enter_context(nc.sbuf_tensor(name, shape, dt))

        k.slot_table, k.pair_table = dram("slot_table", (P * HI, 1), I32), dram("pair_table", (P * HI, 2))
        k.relT4, k.relT8 = dram("relT4", (T, P)), dram("relT8", (T, P))
        for_rows = (EPAD + P, D)
        k.T1, k.T2, k.V2, k.V3, k.V4 = (dram(n, for_rows) for n in ("T1", "T2", "V2", "V3", "V4"))
        k.V0, k.V1, k.V5, k.XS, k.XD, k.HS, k.HD, k.MSG = (
            dram(n, (EPAD, D)) for n in ("V0", "V1", "V5", "XS", "XD", "HS", "HD", "MSG"))

        k.dstf = sb("dstf", [P, T + 2])
        for_edges = [P, T]
        k.lo, k.hi, k.cont, k.end, k.real_end, k.more, k.fix, k.rel4, k.rel8, k.norm_out, k.norm_in = (
            sb(n, for_edges) for n in ("lo", "hi", "cont", "end", "real_end", "more", "fix", "rel4", "rel8", "norm_out", "norm_in"))
        k.src_i, k.dst_i, k.src_tab, k.slot_at, k.out_i, k.pos_i, k.slot_i = (
            sb(n, for_edges, I32) for n in ("src_i", "dst_i", "src_tab", "slot_at", "out_i", "pos_i", "slot_i"))
        k.fix_i = sb("fix_i", [P, 1], I32)
        k.ident, k.into, k.intoT, k.back = (sb(n, [P, P]) for n in ("ident", "into", "intoT", "back"))
        k.tail, k.bn_a, k.bn_b, k.plain = (sb(n, [P, D]) for n in ("tail", "bn_a", "bn_b", "plain"))
        k.small = sb("small", [P, 36, T])
        k.sl, k.sr, k.es, k.ed = k.small[:, 0:8, :], k.small[:, 8:16, :], k.small[:, 16:20, :], k.small[:, 20:36, :]
        k.zeros, k.ones, k.eps, k.p_col = sb("zeros", [P, D]), sb("ones", [P, P]), sb("eps", [P, 1]), sb("p_col", [P, 1])
        k.hi_row = sb("hi_row", [P, HI], FP16)
        k.w0, k.w3 = sb("w0", [P, 2, D]), sb("w3", [P, 4, D])
        k.wf, k.w2 = sb("wf", [P, 4, D + H8]), sb("w2", [P, R4, D + H4])
        k.vdst, k.q2, k.rel_of = sb("vdst", [P, R4 * H4]), sb("q2", [P, P]), sb("rel_of", [P, 4])
        k.b3, k.gb, k.b3_row = sb("b3", [P, 3]), sb("gb", [P, 2]), sb("b3_row", [P, 2, D])
        k.b1_0, k.b2_0, k.attn_r, k.bias2, k.ln_g, k.ln_b = (sb(n, [P, D]) for n in ("b1_0", "b2_0", "attn_r", "bias2", "ln_g", "ln_b"))
        k.hm8, k.hm4, k.al, k.a4 = sb("hm8", [P, H8]), sb("hm4", [P, H4]), sb("al", [P, H8]), sb("a4", [P, 2, R4, H4])
        k.psum = ctx.enter_context(nc.psum_tensor("psum", [P, 4096], F32))
        k.setup_rows = SQUARES + 5
        k.gpsimd_sems = {n: [ctx.enter_context(nc.semaphore(f"{n}{s}")) for s in range(2)]
                         for n in ("gathered", "scattered", "fetched")}
        k.passed = ctx.enter_context(nc.semaphore("passed"))
        k.raised = dict.fromkeys(k.gpsimd_sems, 0)
        phases = [setup, out_degrees, lookups,
                  conv1_edges, lambda nc, k: join_partitions(nc, k, k.V0, "j0"), conv1_nodes,
                  conv2_edges, lambda nc, k: join_partitions(nc, k, k.V1, "j1"), conv2_nodes,
                  lambda nc, k: relational_edges(nc, k, "r1", None, k.T2, None, True, 4, D + H8, k.wf, k.sl),
                  weigh_heads1,
                  lambda nc, k: weighted_edges(nc, k, "w1", H8, k.sl, k.V2),
                  lambda nc, k: join_partitions(nc, k, k.V2, "j2"),
                  batch_stats,
                  layer2_nodes,
                  lambda nc, k: relational_edges(nc, k, "r2", None, k.V2, None, False, 4, D + H4, k.w2, k.es),
                  weigh_edges2,
                  lambda nc, k: weighted_edges(nc, k, "w2", H4, k.es, k.V3),
                  lambda nc, k: join_partitions(nc, k, k.V3, "j3"),
                  lambda nc, k: layer3_inputs(nc, k, "n3", False),
                  lambda nc, k: layer3_inputs(nc, k, "e3", True),
                  lambda nc, k: join_partitions(nc, k, k.V4, "j4"),
                  lambda nc, k: graph_mlp(nc, k, "m1n", False, 0),
                  lambda nc, k: graph_mlp(nc, k, "m1e", True, 0),
                  lambda nc, k: join_partitions(nc, k, k.V5, "j5"),
                  all_nodes,
                  lambda nc, k: graph_mlp(nc, k, "m2n", False, 1)]
        for n, phase in enumerate(phases):
            if n <= upto:
                phase(nc, k)


def kernel(**inputs):
    import numpy as np
    import concourse.bacc as bacc
    from concourse.bass_utils import run_bass_kernel_spmd

    nc = bacc.Bacc("TRN2", target_bir_lowering=False, num_devices=1)
    arrays = {name: np.ascontiguousarray(a) for name, a in inputs.items()}
    aps = {name: nc.dram_tensor(name, a.shape, mybir.dt.from_np(a.dtype), kind="ExternalInput").ap() for name, a in arrays.items()}
    out = nc.dram_tensor("out", (NODES, D), F32, kind="ExternalOutput").ap()
    build(nc, aps["x"], aps["src"], aps["dst"], aps["edge_type_4"], aps["edge_type_8"], aps, out)
    r = run_bass_kernel_spmd(nc, [arrays], core_ids=[0])
    return r.results[0]["out"]
```

```python
import concourse.bass as bass
from concourse import mybir
from contextlib import ExitStack

F32 = mybir.dt.float32
BF16 = mybir.dt.bfloat16
FP16 = mybir.dt.float16
I32 = mybir.dt.int32
ALU = mybir.AluOpType
ACT = mybir.ActivationFunctionType
AX = mybir.AxisListType

P = 128
D = 128
NODES = 100000
EDGES = 25000
T = 196
EPAD = P * T
REAL_LAST = EDGES - (P - 1) * T
G = 7
W = G * D
NI = T // (2 * G)
HI = 784
PAD_NODE = 2**24 - 1
SKIP = 1 << 20
NONE = EPAD
AHEAD = 1
EPS = 1e-5
R8, H8 = 8, 8
R4, H4 = 4, 4
SLOPE = 0.2


class Shared:
    pass


class Steps:

    def __init__(self, *names, lag=None):
        self.order, self.lag = [], lag or {}
        for n in names:
            self.order += [n] if isinstance(n, tuple) else [(n, 0), (n, 1)]
        self.per = len(self.order)

    def at(self, i, name, s=0):
        return (i + (1 + self.lag.get(name, 0))) * self.per + (self.order.index((name, s)) + 1)

    def last(self, n=NI):
        return (n + 1) * self.per


def slotwise(*names):
    return [(n, s) for s in range(2) for n in names]


SUMS = tuple(f"sum{c}" for c in range(G))


def place(s, k=0):
    return s * W + k * D


def slot(buf, s):
    return buf[:, s * W:(s + 1) * W]


def tile(buf, s, k):
    return buf[:, s * W + k * D:s * W + (k + 1) * D]


def by_tile(ap):
    return ap.rearrange("p (k f) -> p k f", f=D)


def every(row, count=G):
    return row.unsqueeze(1).to_broadcast([P, count, D])


def cols(arr, i, s, k=0, n=1):
    return arr[:, bass.ds(i * (2 * G) + (s * G + k), n)]


def part(table, i, s):
    return table[0:EPAD, :].rearrange("(p t) f -> p (t f)", p=P)[:, bass.ds(i * (2 * W) + s * W, W)]



def stats(nc, x, s, st):
    for k in range(G):
        last = nc.vector.bn_stats(st[:, s, k, :], tile(x, s, k))
    return last


def aggregate(nc, s, st, mv):
    for c in range(G):
        last = nc.vector.bn_aggr(mv[:, s, c, :], st[:, s, c, :])
    return last


def deviation(nc, k, s, mv, sd):
    return nc.scalar.activation(sd[:, s, :], mv[:, s, :, 1], ACT.Sqrt, bias=k.eps[:, 0:1])


def normalise(nc, x, s, mv, rs, out):
    for k in range(G):
        last = nc.vector.tensor_scalar(tile(out, s, k), tile(x, s, k), mv[:, s, k, 0:1], rs[:, s, k:k + 1],
                                       ALU.subtract, ALU.mult)
    return last


def transposed(nc, k, x, s, psum):
    for c in range(G):
        last = nc.tensor.transpose(psum[:, c * D:(c + 1) * D], tile(x, s, c), k.ident[:, :])
    return last


def times_rows(nc, xT, s, w, psum):
    for c in range(G):
        last = nc.tensor.matmul(psum[:, c * D:(c + 1) * D], tile(xT, s, c), w, start=True, stop=True)
    return last


def times_rows_plus(nc, k, xT, s, w, psum):
    bias = k.b2b[0:1, :].unsqueeze(1)
    nc.tensor.matmul(psum[:, 0:512], k.ones[0:1, :], bias.to_broadcast([1, 4, D]), start=True, stop=False, skip_group_check=True)
    nc.tensor.matmul(psum[:, 512:W], k.ones[0:1, :], bias.to_broadcast([1, G - 4, D]), start=True, stop=False, skip_group_check=True)
    for c in range(G):
        last = nc.tensor.matmul(psum[:, c * D:(c + 1) * D], tile(xT, s, c), w, start=False, stop=True, skip_group_check=True)
    return last


def times_cols(nc, xT, s, w, psum):
    v = slot(xT, s)
    nc.tensor.matmul(psum[:, 0:512], w, v[:, 0:512], start=True, stop=True)
    return nc.tensor.matmul(psum[:, 512:W], w, v[:, 512:W], start=True, stop=True)


class Phase:

    def __init__(self, nc, k, name):
        self.nc, self.k, self.name = nc, k, name

    def __enter__(self):
        self.ctx = ExitStack()
        self.ctx.__enter__()
        self.sems = []
        return self

    def sb(self, name, shape, dt=F32):
        return self.ctx.enter_context(self.nc.sbuf_tensor(f"{self.name}_{name}", shape, dt))

    def ring(self, name):
        return self.sb(name, [P, 2 * W])

    def sem(self, name):
        s = self.ctx.enter_context(self.nc.semaphore(f"{self.name}_{name}"))
        self.sems.append(s)
        return s

    def sem2(self, name):
        return [self.sem(f"{name}{s}") for s in range(2)]

    def moves(self, name, raised):
        base = self.k.raised[name]
        self.k.raised[name] += raised
        return self.k.gpsimd_sems[name], base

    def block(self):
        self.open = self.nc.Block()
        return self.open.__enter__()

    def __exit__(self, *a):
        if a[0] is None:
            self.open.__exit__(None, None, None)
            for s in self.sems:
                self.nc.gpsimd.sem_clear(s)
            self.nc.all_engine_barrier()
        return self.ctx.__exit__(*a)


def order_edges(nc, k):
    BLOCK = T // 4
    with Phase(nc, k, "order") as ph:
        filled, loaded, edge_cols, v, pe, told, ranked = (
            ph.sem(n) for n in ("filled", "loaded", "edge_cols", "vector_done", "tensor_done", "flag_read", "ranked"))
        row_loaded, row_used, listed, iotas, staged, back = (
            ph.sem(n) for n in ("row_loaded", "row_used", "list_stored", "iotas", "staged", "sorted_back"))
        placed = k.placed
        dst_i, src_t, rel_i = k.dst_list, k.src_list, k.rel_list
        dstf = ph.sb("dstf", [P, T + 2])
        wrong, wrong_sum = ph.sb("wrong", [P, T]), ph.sb("wrong_sum", [P, 1])
        ones = ph.sb("ones", [P, 1])
        flag = ph.sb("flag", [1, 1], I32)
        cols_of, half = ph.sb("cols_of", [P, T]), ph.sb("half", [P, P])
        p_col = ph.sb("p_col", [P, 1])
        row, mine = ph.sb("row", [P, T]), ph.sb("mine", [P, T])
        smaller = ph.sb("smaller", [P, BLOCK, T])
        found = ph.sb("found", [P, BLOCK])
        rank, rank_i = ph.sb("rank", [P, T]), ph.sb("rank_i", [P, T], I32)
        record = ph.sb("record", [P, T, 4], I32)
        at, what = ph.sb("at", [P, 2 * G], I32), ph.sb("what", [P, 2 * G, 4], I32)
        head = (P - 1) * T
        block = ph.block()

        def edge_columns(sp, dst):
            with nc.allow_non_contiguous_dma(reason="two columns of the edge list"):
                sp.dma_start(dst_i[1:P, 0:1], dst[0:head].rearrange("(p t) -> p t", t=T)[:, T - 1:T]).then_inc(edge_cols, 16)
                sp.dma_start(dst_i[0:P - 2, T + 1:T + 2], dst[T:head].rearrange("(p t) -> p t", t=T)[:, 0:1]).then_inc(edge_cols, 16)
                sp.dma_start(dst_i[P - 2:P - 1, T + 1:T + 2], dst[head:head + 1].rearrange("(a t) -> a t", a=1)).then_inc(edge_cols, 16)

        def unsorted(eng):
            eng.wait_ge(v, FLAG)
            return eng.value_load(flag[0:1, 0:1], min_val=0, max_val=EPAD)

        @block.sync
        def _(sp):
            sp.wait_ge(filled, 1)
            for to, one in ((dst_i[:, 1:T + 1], k.dst), (src_t[:, :], k.src), (rel_i[:, 0, :], k.et4), (rel_i[:, 1, :], k.et8)):
                sp.dma_start(to[0:P - 1, :], one[0:head].rearrange("(p t) -> p t", t=T)).then_inc(loaded, 16)
                sp.dma_start(to[P - 1:P, 0:REAL_LAST], one[head:EDGES].rearrange("(a t) -> a t", a=1)).then_inc(loaded, 16)
            edge_columns(sp, k.dst)
            with sp.If(unsorted(sp) > 0):
                sp.dma_start(k.dst_rows, dstf[:, 1:T + 1]).then_inc(listed, 16)
                sp.wait_ge(listed, 16)
                sp.sem_inc(row_used, 1)
                with sp.Fori(0, P) as q:
                    sp.wait_ge(row_used, q + 1)
                    sp.dma_start(row[:, :], k.dst_rows[bass.ds(q, 1), :].to_broadcast([P, T])).then_inc(row_loaded, 16)
                sp.wait_ge(ranked, 2)
                places = k.sorted_edges.rearrange("n c -> (n c)")
                sp.dma_start(record[0:P - 1, :, :], places[0:head * 4].rearrange("(p t c) -> p t c", t=T, c=4)).then_inc(back, 16)
                sp.dma_start(record[P - 1:P, 0:REAL_LAST, :], places[head * 4:EDGES * 4].rearrange("(a t c) -> a t c", a=1, c=4)).then_inc(back, 16)
                edge_columns(sp, k.sorted_edges[:, 0:1].rearrange("n c -> (n c)"))
                sp.wait_ge(edge_cols, 96)

        @block.gpsimd
        def _(g):
            g.memset(dst_i[:, 0:1], -1)
            g.memset(dst_i[:, 1:T + 1], PAD_NODE)
            g.memset(dst_i[:, T + 1:T + 2], -1)
            g.memset(src_t[:, :], 0)
            g.memset(rel_i[:, :, :], 0).then_inc(filled, 1)
            g.iota(cols_of[:, :], pattern=[[1, T]], base=0, channel_multiplier=0, allow_small_or_imprecise_dtypes=True)
            g.iota(p_col[:, :], pattern=[[0, 1]], base=0, channel_multiplier=1, allow_small_or_imprecise_dtypes=True).then_inc(iotas, 1)
            with g.If(unsorted(g) > 0):
                g.wait_ge(ranked, 1)
                with g.Fori(0, NI) as i:
                    c = bass.ds(i * (2 * G), 2 * G)
                    g.tensor_copy(at[:, :], rank_i[:, c]).then_inc(staged, 1)
                    g.tensor_copy(what[:, :, :], record[:, c, :]).then_inc(staged, 1)
                    wait_apart(g, k, staged, i * 2 + 2)
                    for n in range(2 * G):
                        g.indirect_dma_start(k.sorted_edges, bass.IndirectOffsetOnAxis(ap=at[:, n:n + 1], axis=0),
                                             what[:, n, :], None, bounds_check=EDGES - 1, oob_is_err=False).then_inc(placed, 16)
                    wait_apart(g, k, placed, i * (2 * G * 16) + 2 * G * 16)
                g.sem_inc(ranked, 1)

        @block.vector
        def _(d):
            n = [0]

            def chain(ins):
                n[0] += 1
                ins.then_inc(v, 1)
                d.wait_ge(v, n[0])
            d.wait_ge(loaded, 16 * 8)
            d.wait_ge(edge_cols, 48)
            chain(d.memset(ones[:, :], 1.0))
            chain(d.tensor_copy(dstf[:, :], dst_i[:, :]))
            chain(d.tensor_tensor(wrong[:, :], dstf[:, 1:T + 1], dstf[:, 2:T + 2], ALU.is_gt))
            chain(d.tensor_scalar(mine[:, :], dstf[:, 1:T + 1], float(NODES), None, ALU.is_lt))
            chain(d.tensor_tensor(wrong[:, :], wrong[:, :], mine[:, :], ALU.mult))
            chain(d.tensor_reduce(wrong_sum[:, :], wrong[:, :], AX.X, ALU.add))
            assert n[0] == FLAG - 1
            d.wait_ge(pe, 1)
            chain(d.tensor_copy(flag[:, :], k.psum[0:1, 0:1]))
            with d.If(unsorted(d) > 0):
                d.wait_ge(iotas, 1)
                for c, one in enumerate((dst_i[:, 1:T + 1], src_t[:, :], rel_i[:, 0, :], rel_i[:, 1, :])):
                    chain(d.tensor_copy(record[:, :, c], one))
                chain(d.tensor_scalar(half[:, :], cols_of[:, 0:P], p_col[:, 0:1], 0.5, ALU.is_lt, ALU.mult))
                base = n[0]
                with d.Fori(0, T) as t:
                    d.tensor_scalar(mine[:, :], cols_of[:, :], cols_of[:, bass.ds(t, 1)], None, ALU.is_lt).then_inc(v, 1)
                    wait_apart(d, k, v, t * 3 + (base + 1))
                    d.scalar_tensor_tensor(wrong[:, :], dstf[:, 1:T + 1], dstf[:, bass.ds(t + 1, 1)], mine[:, :],
                                           ALU.is_equal, ALU.mult).then_inc(v, 1)
                    wait_apart(d, k, v, t * 3 + (base + 2))
                    d.tensor_reduce(rank[:, bass.ds(t, 1)], wrong[:, :], AX.X, ALU.add).then_inc(v, 1)
                    wait_apart(d, k, v, t * 3 + (base + 3))
                base += 3 * T
                steps = 1 + 3 * 4
                with d.Fori(0, P) as q:
                    done = [0]

                    def next_step(ins):
                        done[0] += 1
                        ins.then_inc(v, 1)
                        wait_apart(d, k, v, q * steps + (base + done[0]))
                    wait_apart(d, k, row_loaded, q * 16 + 16)
                    next_step(d.tensor_scalar(mine[:, :], row[:, :], half[:, bass.ds(q, 1)], None, ALU.subtract))
                    d.sem_inc(row_used, 1)
                    for b in range(4):
                        own = slice(b * BLOCK, (b + 1) * BLOCK)
                        next_step(d.tensor_tensor(smaller[:, :, :], mine[:, :].unsqueeze(1).to_broadcast([P, BLOCK, T]),
                                                  dstf[:, 1 + own.start:1 + own.stop].unsqueeze(2).to_broadcast([P, BLOCK, T]), ALU.is_lt))
                        next_step(d.tensor_reduce(found[:, :], smaller[:, :, :], AX.X, ALU.add))
                        next_step(d.tensor_tensor(rank[:, own], rank[:, own], found[:, :], ALU.add))
                n[0] = base + P * steps
                chain(d.tensor_scalar(mine[:, :], dstf[:, 1:T + 1], float(NODES), float(SKIP), ALU.is_ge, ALU.mult))
                chain(d.tensor_tensor(rank[:, :], rank[:, :], mine[:, :], ALU.add))
                chain(d.tensor_copy(rank_i[:, :], rank[:, :]))
                d.sem_inc(ranked, 1)
                d.wait_ge(back, 32)
                last = slice(0, REAL_LAST)
                for c, one in enumerate((dst_i[:, 1:T + 1], src_t[:, :], rel_i[:, 0, :], rel_i[:, 1, :])):
                    chain(d.tensor_copy(one, record[:, :, c]))

        @block.tensor
        def _(t):
            t.wait_ge(v, FLAG - 1)
            nc.tensor.matmul(k.psum[0:1, 0:1], wrong_sum[:, :], ones[:, :], start=True, stop=True).then_inc(pe, 1)


FLAG = 7


def setup(nc, k):
    with Phase(nc, k, "setup") as ph:
        consts, v, weights = (ph.sem(n) for n in ("consts", "vector_done", "weights_loaded"))
        pe_done, act_done, stored = ph.sem("tensor_done"), ph.sem("scalar_done"), ph.sem("stored")
        dst_i, src_t, rel_i = k.dst_list, k.src_list, k.rel_list
        tmp_i = ph.sb("tmp_i", [P, T], I32)
        tmp = ph.sb("tmp", [P, T])
        tmp2 = ph.sb("tmp2", [P, T])
        pos = ph.sb("pos", [P, T])
        sq = ph.sb("sq", [P, 4, P])
        hasfix = ph.sb("hasfix", [P, 2])
        upper = ph.sb("upper", [P, P])
        lower = ph.sb("lower", [P, P])
        relT = ph.sb("relT", [98, 4, P])
        row = ph.sb("row", [P, 8, D])
        none_rows = ph.sb("none_rows", [P, D])
        wv = ph.sb("wv", [P, 2, R4, D])
        wT = ph.sb("wT", [P, R4, D])
        att = ph.sb("att", [P, 2, R4, H4])
        wfT = ph.sb("wfT", [P, 4, D])
        attl = ph.sb("attl", [P, H8])
        compb = ph.sb("compb", [P, 32])
        jdx = ph.sb("jdx", [P, 2, 128])
        qm = ph.sb("qm", [P, 3, 64])
        big_none = ph.sb("big_none", [P, HI], I32)
        block = ph.block()
        PS = k.psum

        @block.sync
        def _(sp):
            sp.wait_ge(v, 5)
            sp.dma_start(k.slot_table.rearrange("(p j) a -> p (j a)", p=P), big_none[:, :]).then_inc(stored, 16)
            sp.wait_ge(act_done, 1)
            for h in range(2):
                sp.dma_start(k.relT8[98 * h:98 * h + 98, :], relT[:, h, :]).then_inc(stored, 16)
                sp.dma_start(k.relT4[98 * h:98 * h + 98, :], relT[:, 2 + h, :]).then_inc(stored, 16)
            sp.wait_ge(v, k.setup_rows)
            sp.dma_start(k.T1[EPAD:EPAD + P, :], none_rows[:, :]).then_inc(stored, 16)
            sp.dma_start(k.T2[EPAD:EPAD + P, :], k.b2_0[:, :]).then_inc(stored, 16)
            for t in (k.V2, k.V3, k.V4):
                sp.dma_start(t[EPAD:EPAD + P, :], k.zeros[:, 0:D]).then_inc(stored, 16)
            sp.wait_ge(stored, 16 * 10)

        @block.gpsimd
        def _(g):
            g.memset(k.ident[:, :], 0.0)
            g.memset(upper[:, :], 1.0)
            g.memset(lower[:, :], 1.0)
            g.memset(k.zeros[:, :], 0.0)
            g.memset(k.ones[:, :], 1.0)
            g.memset(k.eps[:, :], EPS)
            g.memset(qm[:, 0, :], 0.0)
            g.iota(tmp_i[:, :], pattern=[[1, T]], base=0, channel_multiplier=T)
            g.iota(k.hi_row[:, :], pattern=[[1, HI]], base=0, channel_multiplier=0, allow_small_or_imprecise_dtypes=True)
            g.iota(k.p_col[:, :], pattern=[[0, 1]], base=0, channel_multiplier=1, allow_small_or_imprecise_dtypes=True)\
                .then_inc(consts, 4)
            g.wait_ge(consts, 4)
            g.affine_select(out=k.ident[:, :], in_=k.ident[:, :], compare_op=ALU.not_equal, fill=1.0,
                            base=0, pattern=[[-1, P]], channel_multiplier=1)
            g.affine_select(out=upper[:, :], in_=upper[:, :], compare_op=ALU.is_gt, fill=0.0,
                            base=0, pattern=[[1, P]], channel_multiplier=-1)
            g.affine_select(out=lower[:, :], in_=lower[:, :], compare_op=ALU.is_gt, fill=0.0,
                            base=0, pattern=[[-1, P]], channel_multiplier=1)
            g.memset(qm[:, 1, :], 1.0).then_inc(consts, 1)
            g.wait_ge(consts, 5)
            q3 = qm[:, 1, :].rearrange("p (j b) -> p j b", b=4)
            g.affine_select(out=q3, in_=q3, compare_op=ALU.is_ge, fill=0.0,
                            base=0, pattern=[[-8, 16], [0, 4]], channel_multiplier=1).then_inc(consts, 1)
            g.wait_ge(consts, 6)
            g.affine_select(out=q3, in_=q3, compare_op=ALU.is_ge, fill=0.0,
                            base=7, pattern=[[8, 16], [0, 4]], channel_multiplier=-1).then_inc(consts, 1)

        @block.scalar
        def _(a):
            def rows(dst, src):
                a.dma_start(dst, src).then_inc(weights, 16)
            bc = lambda ap: ap.rearrange("(a n) -> a n", a=1).to_broadcast([P, D])
            rows(k.w0[:, 0, :], k.w['L0_gnn_W1'])
            rows(k.w0[:, 1, :], k.w['L0_gnn_W2'])
            rows(k.wf[:, :, 0:D], k.w['L1_gnn_weight'].rearrange("b i o -> (b i) o").rearrange("(c k) o -> k c o", k=P))
            rows(k.w2[:, :, 0:D], k.w['L2_gnn_W'].rearrange("r i o -> i r o"))
            for n, name in enumerate(('L3_gnn_W1a', 'L3_gnn_W1b', 'L3_gnn_W2a', 'L3_gnn_W2b')):
                rows(k.w3[:, n, :], k.w[name])
            with nc.allow_non_contiguous_dma(reason="bias columns and attention vectors"):
                for n, name in enumerate(('L3_gnn_b1a', 'L3_gnn_b1b', 'L3_gnn_b2a')):
                    rows(k.b3[:, n:n + 1], k.w[name].rearrange("(n a) -> n a", a=1))
                rows(k.gb[:, 0:1], k.w['L1_gnn_gamma'].rearrange("(n a) -> n a", a=1))
                rows(k.gb[:, 1:2], k.w['L1_gnn_beta'].rearrange("(n a) -> n a", a=1))
                rows(attl[:, 0:1], k.w['L1_gnn_attn_l'].rearrange("h (d a) -> (h d) a", a=1))
                for m, name in enumerate(('L2_gnn_attn_src', 'L2_gnn_attn_dst')):
                    rows(att[:, m, :, 0:1], k.w[name].rearrange("r h (d a) -> (h d) r a", a=1))
                for n in range(16):
                    rows(compb[8 * n:8 * n + 8, 0:4], k.w['L1_gnn_w_comp'])
            rows(k.b1_0[:, :], bc(k.w['L0_gnn_b1']))
            rows(k.b2_0[:, :], bc(k.w['L0_gnn_b2']))
            rows(k.attn_r[:, :], k.w['L1_gnn_attn_r'].rearrange("h d -> (h d)").rearrange("(a n) -> a n", a=1).to_broadcast([P, D]))
            rows(k.bias2[:, :], bc(k.w['L2_gnn_bias']))
            rows(k.ln_g[:, :], bc(k.w['L2_gnn_ln_gamma']))
            rows(k.ln_b[:, :], bc(k.w['L2_gnn_ln_beta']))
            rows(k.b3_row[:, 0, :], bc(k.w['L3_gnn_b1b']))
            rows(k.b3_row[:, 1, :], bc(k.w['L3_gnn_b2b']))
            a.wait_ge(pe_done, 2)
            a.activation(relT[:, :, :], PS[0:98, 0:4 * P], ACT.Copy).then_inc(act_done, 1)
            a.wait_ge(pe_done, 4)
            a.activation(wfT[:, :, :], PS[:, 2048:2560], ACT.Copy).then_inc(act_done, 1)
            a.activation(wT[:, :, :], PS[:, 2560:3072], ACT.Copy).then_inc(act_done, 1)
            a.wait_ge(pe_done, 6)
            a.activation(k.wf[:, :, D:D + H8], PS[:, 3072:3072 + 32].rearrange("p (c h) -> p c h", h=H8), ACT.Copy).then_inc(act_done, 1)
            pv = PS[:, 3584:3584 + 32].rearrange("p (m r h) -> p m r h", m=2, h=H4)
            a.activation(k.intoT[:, :], PS[:, 768:896], ACT.Copy)
            a.activation(k.w2[:, :, D:D + H4], pv[:, 0, :, :], ACT.Copy)
            a.activation(k.vdst[:, :].rearrange("p (r h) -> p r h", h=H4), pv[:, 1, :, :], ACT.Copy).then_inc(act_done, 1)

        @block.vector
        def _(d):
            n = [0]

            def chain(ins):
                n[0] += 1
                ins.then_inc(v, 1)
                d.wait_ge(v, n[0])

            chain(d.tensor_copy(k.dstf[:, :], dst_i[:, :]))
            chain(d.tensor_copy(k.src_i[:, :], src_t[:, :]))
            d.wait_ge(consts, 7)
            chain(d.tensor_copy(pos[:, :], tmp_i[:, :]))
            chain(d.memset(tmp[:, :], float(NONE)))
            chain(d.tensor_copy(big_none[:, :], tmp[:, 0:1].to_broadcast([P, HI])))
            chain(d.tensor_copy(k.rel4[:, :], rel_i[:, 0, :]))
            chain(d.tensor_copy(k.rel8[:, :], rel_i[:, 1, :]))
            chain(d.tensor_scalar(tmp_i[:, :], src_t[:, :], 127, None, ALU.bitwise_and))
            chain(d.tensor_copy(k.lo[:, :], tmp_i[:, :]))
            chain(d.tensor_scalar(tmp_i[:, :], src_t[:, :], 7, None, ALU.arith_shift_right))
            chain(d.tensor_copy(k.hi[:, :], tmp_i[:, :]))
            chain(d.scalar_tensor_tensor(tmp[:, :], k.lo[:, :], float(HI), k.hi[:, :], ALU.mult, ALU.add))
            chain(d.tensor_copy(k.src_tab[:, :], tmp[:, :]))
            chain(d.tensor_scalar(tmp2[:, :], pos[:, :], float(EDGES), 1.0, ALU.is_lt, ALU.mult))
            chain(d.scalar_tensor_tensor(k.lo[:, :], k.lo[:, :], 1.0, tmp2[:, :], ALU.add, ALU.mult))
            chain(d.tensor_scalar(k.lo[:, :], k.lo[:, :], 1.0, None, ALU.subtract))
            chain(d.tensor_tensor(k.cont[:, :], k.dstf[:, 1:T + 1], k.dstf[:, 0:T], ALU.is_equal))
            chain(d.memset(k.cont[:, 0:1], 0.0))
            chain(d.tensor_tensor(k.end[:, :], k.dstf[:, 1:T + 1], k.dstf[:, 2:T + 2], ALU.not_equal))
            chain(d.tensor_tensor(k.real_end[:, :], k.end[:, :], tmp2[:, :], ALU.mult))
            chain(d.tensor_scalar(k.more[:, :], k.end[:, :], -1.0, 1.0, ALU.mult, ALU.add))
            chain(d.tensor_scalar(k.fix[:, :], k.dstf[:, 1:T + 1], k.dstf[:, 1:2], None, ALU.is_equal))
            chain(d.tensor_tensor(k.fix[:, :], k.fix[:, :], k.end[:, :], ALU.mult))
            chain(d.tensor_reduce(hasfix[:, 0:1], k.fix[:, :], AX.X, ALU.add))
            chain(d.tensor_tensor(tmp[:, :], k.fix[:, :], pos[:, :], ALU.mult))
            chain(d.tensor_reduce(hasfix[:, 1:2], tmp[:, :], AX.X, ALU.add))
            chain(d.scalar_tensor_tensor(hasfix[:, 1:2], hasfix[:, 0:1], -float(SKIP), hasfix[:, 1:2], ALU.mult, ALU.add))
            chain(d.tensor_scalar(hasfix[:, 1:2], hasfix[:, 1:2], float(SKIP), None, ALU.add))
            chain(d.tensor_copy(k.fix_i[:, :], hasfix[:, 1:2]))
            chain(d.tensor_copy(tmp_i[:, :], k.dstf[:, 1:T + 1]))
            chain(d.tensor_scalar(tmp[:, :], k.dstf[:, 1:T + 1], -float(SKIP), None, ALU.add))
            chain(d.tensor_tensor(tmp[:, :], tmp[:, :], k.end[:, :], ALU.mult))
            chain(d.tensor_scalar(tmp[:, :], tmp[:, :], float(SKIP), None, ALU.add))
            chain(d.tensor_copy(k.out_i[:, :], tmp[:, :]))
            chain(d.tensor_scalar(rel_i[:, 0, :], tmp_i[:, :], 127, None, ALU.bitwise_and))
            chain(d.tensor_scalar(rel_i[:, 1, :], tmp_i[:, :], 7, None, ALU.arith_shift_right))
            chain(d.tensor_copy(tmp[:, :], rel_i[:, 0, :]))
            chain(d.tensor_copy(tmp2[:, :], rel_i[:, 1, :]))
            chain(d.scalar_tensor_tensor(tmp[:, :], tmp[:, :], float(HI), tmp2[:, :], ALU.mult, ALU.add))
            chain(d.tensor_scalar(tmp[:, :], tmp[:, :], -float(SKIP), None, ALU.add))
            chain(d.tensor_tensor(tmp[:, :], tmp[:, :], k.end[:, :], ALU.mult))
            chain(d.tensor_scalar(tmp[:, :], tmp[:, :], float(SKIP), None, ALU.add))
            chain(d.tensor_copy(k.slot_at[:, :], tmp[:, :]))
            chain(d.tensor_copy(k.pos_i[:, :], pos[:, :]))
            chain(d.tensor_scalar(tmp[:, :], k.dstf[:, 1:T + 1], float(NODES), None, ALU.is_lt))
            chain(d.tensor_tensor(tmp[:, :], tmp[:, :], k.dstf[:, 1:T + 1], ALU.mult))
            chain(d.tensor_copy(k.dst_i[:, :], tmp[:, :]))
            chain(d.tensor_copy(sq[:, 0, :], k.dstf[:, 1:2].to_broadcast([P, P])))
            chain(d.tensor_copy(sq[:, 1, :], k.dstf[:, T:T + 1].to_broadcast([P, P])))
            assert n[0] == SQUARES
            d.wait_ge(pe_done, 1)
            chain(d.tensor_scalar(sq[:, 2, :], PS[:, 512:640], k.dstf[:, T:T + 1], None, ALU.is_equal))
            chain(d.tensor_tensor(k.into[:, :], sq[:, 2, :], upper[:, :], ALU.mult))
            chain(d.tensor_scalar(sq[:, 3, :], PS[:, 640:768], k.dstf[:, 1:2], hasfix[:, 0:1], ALU.is_equal, ALU.mult))
            chain(d.tensor_tensor(k.back[:, :], sq[:, 3, :], lower[:, :], ALU.mult))
            d.wait_ge(weights, 16 * NWEIGHTS)
            chain(d.tensor_scalar(none_rows[:, :], k.b1_0[:, :], 0.0, None, ALU.max))
            assert n[0] == k.setup_rows
            q4 = k.q2[:, :].rearrange("p (c j b) -> p c j b", c=2, b=4)
            m3 = qm[:, 1, :].rearrange("p (j b) -> p j b", b=4)
            cb = compb[:, 0:4].unsqueeze(1).to_broadcast([P, 16, 4])
            chain(d.tensor_tensor(q4[:, 0, :, :], m3, cb, ALU.mult))
            chain(d.tensor_tensor(q4[:, 1, :, :], m3, cb, ALU.mult))
            for c in range(4):
                chain(d.memset(k.rel_of[0:64, c:c + 1], float(2 * c)))
                chain(d.memset(k.rel_of[64:P, c:c + 1], float(2 * c + 1)))
            hm8 = k.hm8[:, :]
            hm4 = k.hm4[:, :]
            chain(d.tensor_reduce(hm8, k.ident[:, :].rearrange("p (h e) -> p h e", h=H8), AX.X, ALU.add))
            chain(d.tensor_reduce(hm4, k.ident[:, :].rearrange("p (h e) -> p h e", h=H4), AX.X, ALU.add))
            chain(d.tensor_scalar(k.al[:, :], hm8, attl[:, 0:1], None, ALU.mult))
            for m in range(2):
                for r in range(R4):
                    chain(d.tensor_scalar(k.a4[:, m, r, :], hm4, att[:, m, r, 0:1], None, ALU.mult))
            assert n[0] == ATTENTION

        @block.tensor
        def _(t):
            t.wait_ge(v, SQUARES)
            nc.tensor.transpose(PS[:, 512:640], sq[:, 0, :], k.ident[:, :])
            nc.tensor.transpose(PS[:, 640:768], sq[:, 1, :], k.ident[:, :]).then_inc(pe_done, 1)
            for h in range(2):
                nc.tensor.transpose(PS[0:98, h * P:(h + 1) * P], k.rel8[:, 98 * h:98 * h + 98], k.ident[:, :])
                last = nc.tensor.transpose(PS[0:98, (h + 2) * P:(h + 3) * P], k.rel4[:, 98 * h:98 * h + 98], k.ident[:, :])
            last.then_inc(pe_done, 1)
            t.wait_ge(weights, 16 * NWEIGHTS)
            for c in range(4):
                last = nc.tensor.transpose(PS[:, 2048 + c * D:2048 + (c + 1) * D], k.wf[:, c, 0:D], k.ident[:, :])
            last.then_inc(pe_done, 1)
            for r in range(R4):
                last = nc.tensor.transpose(PS[:, 2560 + r * D:2560 + (r + 1) * D], k.w2[:, r, 0:D], k.ident[:, :])
            last.then_inc(pe_done, 1)
            t.wait_ge(act_done, 3)
            t.wait_ge(v, ATTENTION)
            for c in range(4):
                last = nc.tensor.matmul(PS[:, 3072 + c * H8:3072 + (c + 1) * H8], wfT[:, c, :], k.al[:, :], start=True, stop=True)
            last.then_inc(pe_done, 1)
            nc.tensor.transpose(PS[:, 768:896], k.into[:, :], k.ident[:, :])
            for m in range(2):
                for r in range(R4):
                    o = 3584 + (m * R4 + r) * H4
                    last = nc.tensor.matmul(PS[:, o:o + H4], wT[:, r, :], k.a4[:, m, r, :], start=True, stop=True)
            last.then_inc(pe_done, 1)


SQUARES = 49
ATTENTION = SQUARES + 5 + 2 + 8 + 3 + 8
NWEIGHTS = 4 + 4 + 3 + 2 + 1 + 2 + 16 + 8


def out_degrees(nc, k):
    S = Steps("hot")
    M = Steps("counted")
    with Phase(nc, k, "deg") as ph:
        vec, pe, staged, done, tab, act = (ph.sem(n) for n in ("vector_steps", "tensor_steps", "staged", "vector_done", "table_moved", "scalar_done"))
        scattered, sbase = ph.moves("scattered", NI * 16 * G)
        lo_hot = ph.sb("lo_hot", [P, 2, G, P], BF16)
        hi_hot = ph.sb("hi_hot", [P, 2, G, HI], BF16)
        at = ph.sb("at", [P, 2 * G], I32)
        what = ph.sb("what", [P, 2 * G], I32)
        deg = ph.sb("deg", [P, HI])
        slots = ph.sb("slots", [P, HI], I32)
        pair = ph.sb("pair", [P, HI, 2])
        zero = ph.sb("zero", [P, 512], BF16)
        block = ph.block()
        PS = k.psum

        @block.gpsimd
        def _(g):
            def scatter(i):
                for s in range(2):
                    if not isinstance(i, int):
                        wait_apart(g, k, scattered[s], i * (16 * G) + sbase)
                    g.tensor_copy(at[:, s * G:(s + 1) * G], cols(k.slot_at, i, s, 0, G)).then_inc(staged, 1)
                    g.tensor_copy(what[:, s * G:(s + 1) * G], cols(k.pos_i, i, s, 0, G)).then_inc(staged, 1)
                    wait_apart(g, k, staged, i * 4 + (2 * s + 2))
                    for c in range(s * G, (s + 1) * G):
                        g.indirect_dma_start(k.slot_table, bass.IndirectOffsetOnAxis(ap=at[:, c:c + 1], axis=0),
                                             what[:, c:c + 1], None, bounds_check=P * HI - 1,
                                             oob_is_err=False).then_inc(scattered[s], 16)
            scatter(0)
            with g.Fori(1, NI) as i:
                scatter(i)

        @block.vector
        def _(d):
            d.memset(zero[:, :], 0.0).then_inc(done, 1)
            d.sem_inc(vec, S.per)
            with d.Fori(0, NI) as i:
                for s in range(2):
                    d.wait_ge(pe, M.at(i - 1, "counted", s))
                    for c in range(G):
                        nc.vector.tensor_scalar(lo_hot[:, s, c, :], k.hi_row[:, 0:P], cols(k.lo, i, s, c), None, ALU.is_equal)
                        last = nc.vector.tensor_scalar(hi_hot[:, s, c, :], k.hi_row[:, :], cols(k.hi, i, s, c), None, ALU.is_equal)
                    last.then_inc(vec, 1)
            d.wait_ge(pe, M.last())
            d.tensor_scalar(deg[:, 0:HI // 2], PS[:, 0:HI // 2], 1.0, None, ALU.max)
            d.tensor_scalar(deg[:, HI // 2:HI], PS[:, 512:512 + HI // 2], 1.0, None, ALU.max).then_inc(done, 1)
            d.wait_ge(act, 1)
            d.reciprocal(pair[:, :, 1], deg[:, :]).then_inc(done, 1)
            d.wait_ge(tab, 16)
            d.tensor_copy(pair[:, :, 0], slots[:, :]).then_inc(done, 1)

        @block.scalar
        def _(a):
            a.wait_ge(done, 2)
            a.activation(deg[:, :], deg[:, :], ACT.Sqrt).then_inc(act, 1)

        @block.tensor
        def _(t):
            t.wait_ge(done, 1)
            nc.tensor.matmul(PS[:, 0:HI // 2], zero[:, 0:P], zero[:, 0:HI // 2], start=True, stop=False, skip_group_check=True)
            nc.tensor.matmul(PS[:, 512:512 + HI // 2], zero[:, 0:P], zero[:, 0:HI // 2], start=True, stop=False, skip_group_check=True)
            t.sem_inc(pe, M.per)
            with t.Fori(0, NI) as i:
                for s in range(2):
                    t.wait_ge(vec, S.at(i, "hot", s))
                    for c in range(G):
                        nc.tensor.matmul(PS[:, 0:HI // 2], lo_hot[:, s, c, :], hi_hot[:, s, c, 0:HI // 2],
                                         start=False, stop=False, skip_group_check=True)
                        last = nc.tensor.matmul(PS[:, 512:512 + HI // 2], lo_hot[:, s, c, :], hi_hot[:, s, c, HI // 2:HI],
                                                start=False, stop=False, skip_group_check=True)
                    last.then_inc(pe, 1)

        @block.sync
        def _(sp):
            for s in range(2):
                sp.wait_ge(scattered[s], NI * 16 * G + sbase)
            sp.dma_start(slots[:, :], k.slot_table.rearrange("(p j) a -> p (j a)", p=P)).then_inc(tab, 16)
            sp.wait_ge(done, 4)
            sp.dma_start(k.pair_table.rearrange("(p j) a -> p (j a)", p=P), pair[:, :, :].rearrange("p j a -> p (j a)")).then_inc(tab, 16)
            sp.wait_ge(tab, 32)


def start_ahead(eng, *sems):
    for pair_of_slots in sems:
        for sem in pair_of_slots:
            eng.sem_inc(sem, AHEAD)


def wait_apart(eng, k, sem, value):
    eng.wait_ge(sem, value)
    eng.sem_inc(k.passed, 1)


def gather_columns(nc, k, g, i, s, index, ring, staged, table, out, width, gathered):
    g.tensor_copy(ring[:, s * G:(s + 1) * G], cols(index, i, s, 0, G)).then_inc(staged, 1)
    wait_apart(g, k, staged, i * 2 + (s + 3))
    for c in range(G):
        o = (s * G + c) * width
        g.indirect_dma_start(out[:, o:o + width], None, table,
                             bass.IndirectOffsetOnAxis(ap=ring[:, s * G + c:s * G + c + 1], axis=0)).then_inc(gathered[s], 16)


def lookups(nc, k):
    S = Steps("kept")
    with Phase(nc, k, "look") as ph:
        vec, staged, v, pe, act = (ph.sem(n) for n in ("vector_steps", "staged", "vector_done", "tensor_done", "scalar_done"))
        gathered, gbase = ph.moves("gathered", NI * 16 * G)
        ring = ph.sb("ring", [P, 2 * G], I32)
        pairs = ph.sb("pairs", [P, 2 * G * 2])
        slotf = ph.sb("slotf", [P, T])
        none = ph.sb("none", [P, T])
        count = ph.sb("count", [P, T])
        carry = ph.sb("carry", [P, 1])
        block = ph.block()

        @block.gpsimd
        def _(g):
            g.sem_inc(staged, 2)
            with g.Fori(0, NI) as i:
                for s in range(2):
                    wait_apart(g, k, vec, S.at(i - 1, "kept", s))
                    gather_columns(nc, k, g, i, s, k.src_tab, ring, staged, k.pair_table, pairs, 2, gathered)

        @block.vector
        def _(d):
            d.sem_inc(vec, S.per)
            with d.Fori(0, NI) as i:
                for s in range(2):
                    d.wait_ge(gathered[s], i * (16 * G) + (16 * G + gbase))
                    got = pairs[:, s * 2 * G:(s + 1) * 2 * G].rearrange("p (c a) -> p c a", a=2)
                    nc.vector.tensor_copy(cols(slotf, i, s, 0, G), got[:, :, 0])
                    nc.vector.tensor_copy(cols(k.norm_out, i, s, 0, G), got[:, :, 1]).then_inc(vec, 1)
            n = [0]

            def chain(ins):
                n[0] += 1
                ins.then_inc(v, 1)
                d.wait_ge(v, n[0])
            d.wait_ge(vec, S.last())
            chain(d.tensor_scalar(none[:, :], slotf[:, :], float(NONE), k.p_col[:, 0:1], ALU.is_equal, ALU.mult))
            chain(d.tensor_tensor(slotf[:, :], slotf[:, :], none[:, :], ALU.add))
            chain(d.tensor_copy(k.slot_i[:, :], slotf[:, :]))
            chain(d.tensor_tensor_scan(count[:, :], k.cont[:, :], k.ones[:, 0:1].to_broadcast([P, T]), 0.0, ALU.mult, ALU.add))
            d.wait_ge(pe, 1)
            chain(d.tensor_copy(carry[:, :], k.psum[:, 0:1]))
            chain(d.scalar_tensor_tensor(count[:, :], k.fix[:, :], carry[:, 0:1], count[:, :], ALU.mult, ALU.add))
            d.wait_ge(act, 1)
            chain(d.reciprocal(k.norm_in[:, :], count[:, :]))

        @block.tensor
        def _(t):
            t.wait_ge(v, 4)
            nc.tensor.matmul(k.psum[:, 0:1], k.into[:, :], count[:, T - 1:T], start=True, stop=True).then_inc(pe, 1)

        @block.scalar
        def _(a):
            a.wait_ge(v, 6)
            a.activation(count[:, :], count[:, :], ACT.Sqrt).then_inc(act, 1)


def pair(k, j):
    return k.psum[:, j * 1024:j * 1024 + W]


def wide(k, j, c, n):
    o = j * 1024 + (c // 3) * 512 + (c % 3) * n
    return k.psum[:, o:o + n]


def running_sum(nc, k, d, vec, S, i, s, message, sums):
    for c in range(G):
        before = (tile(sums, s, c - 1), i, f"sum{c - 1}", s) if c else \
                 (tile(sums, 1 - s, G - 1), i if s else i - 1, SUMS[-1], 1 - s)
        d.wait_ge(vec, S.at(*before[1:]))
        nc.vector.scalar_tensor_tensor(tile(sums, s, c), before[0], cols(k.cont, i, s, c), tile(message, s, c),
                                       ALU.mult, ALU.add).then_inc(vec, 1)


def join_partitions(nc, k, V, name):
    with Phase(nc, k, name) as ph:
        pe, v, zeroed = (ph.sem(n) for n in ("tensor_done", "vector_done", "zeroed"))
        (fetched, _), fbase = ph.moves("fetched", 32)
        rows = ph.sb("rows", [P, D])
        block = ph.block()

        @block.tensor
        def _(t):
            nc.tensor.matmul(k.psum[:, 0:D], k.into[:, :], k.tail[:, :], start=True, stop=True).then_inc(pe, 1)

        @block.gpsimd
        def _(g):
            g.memset(rows[:, :], 0.0).then_inc(zeroed, 1)
            g.wait_ge(zeroed, 1)
            at = bass.IndirectOffsetOnAxis(ap=k.fix_i[:, 0:1], axis=0)
            g.indirect_dma_start(rows[:, :], None, V, at, bounds_check=EPAD - 1, oob_is_err=False).then_inc(fetched, 16)
            g.wait_ge(v, 1)
            g.indirect_dma_start(V, at, rows[:, :], None, bounds_check=EPAD - 1, oob_is_err=False).then_inc(fetched, 16)
            g.wait_ge(fetched, fbase + 32)

        @block.vector
        def _(d):
            d.wait_ge(fetched, fbase + 16)
            d.wait_ge(pe, 1)
            nc.vector.tensor_tensor(rows[:, :], rows[:, :], k.psum[:, 0:D], ALU.add).then_inc(v, 1)


def conv1_edges(nc, k):
    V = Steps("stats", "aggr", "rs", "rsn", "norm", *slotwise(*SUMS))
    A = Steps("sd", "relu")
    with Phase(nc, k, "c1e") as ph:
        vec, act, staged, cleared = (ph.sem(n) for n in ("vector_steps", "scalar_steps", "staged", "cleared"))
        gathered, gbase = ph.moves("gathered", NI * 16 * G)
        kept, stored = ph.sem2("kept"), ph.sem2("stored")
        ring = ph.sb("ring", [P, 2 * G], I32)
        x, h, sums = ph.ring("x"), ph.ring("h"), ph.ring("sums")
        st, mv = ph.sb("st", [P, 2, G, 6]), ph.sb("mv", [P, 2, G, 2])
        sd, rs = ph.sb("sd", [P, 2, G]), ph.sb("rs", [P, 2, G])
        block = ph.block()

        @block.gpsimd
        def _(g):
            g.sem_inc(staged, 2)
            with g.Fori(0, NI) as i:
                for s in range(2):
                    wait_apart(g, k, vec, V.at(i - 1, "norm", s))
                    wait_apart(g, k, kept[s], i * 16 + AHEAD)
                    gather_columns(nc, k, g, i, s, k.src_i, ring, staged, k.x, x, D, gathered)

        @block.sync
        def _(sp):
            start_ahead(sp, kept, stored)
            with sp.Fori(0, NI) as i:
                for s in range(2):
                    sp.wait_ge(gathered[s], i * (16 * G) + (16 * G + gbase))
                    sp.dma_start(part(k.XS, i, s), slot(x, s)).then_inc(kept[s], 16)
                for s in range(2):
                    sp.wait_ge(vec, V.at(i, SUMS[-1], s))
                    sp.dma_start(part(k.V0, i, s), slot(sums, s)).then_inc(stored[s], 16)
            for s in range(2):
                sp.wait_ge(kept[s], NI * 16 + AHEAD)
                sp.wait_ge(stored[s], NI * 16 + AHEAD)

        @block.vector
        def _(d):
            d.memset(tile(sums, 1, G - 1), 0.0).then_inc(cleared, 1)
            d.wait_ge(cleared, 1)
            d.sem_inc(vec, V.per)
            with d.Fori(0, NI) as i:
                for s in range(2):
                    d.wait_ge(gathered[s], i * (16 * G) + (16 * G + gbase))
                    stats(nc, x, s, st).then_inc(vec, 1)
                for s in range(2):
                    wait_apart(d, k, vec, V.at(i, "stats", s))
                    aggregate(nc, s, st, mv).then_inc(vec, 1)
                for s in range(2):
                    d.wait_ge(act, A.at(i, "sd", s))
                    nc.vector.reciprocal(rs[:, s, :], sd[:, s, :]).then_inc(vec, 1)
                for s in range(2):
                    d.wait_ge(vec, V.at(i, "rs", s))
                    nc.vector.tensor_tensor(rs[:, s, :], rs[:, s, :], cols(k.norm_out, i, s, 0, G), ALU.mult).then_inc(vec, 1)
                for s in range(2):
                    d.wait_ge(vec, V.at(i, "rsn", s))
                    normalise(nc, x, s, mv, rs, h).then_inc(vec, 1)
                for s in range(2):
                    d.wait_ge(act, A.at(i, "relu", s))
                    d.wait_ge(stored[s], i * 16 + AHEAD)
                    running_sum(nc, k, d, vec, V, i, s, h, sums)
            d.wait_ge(vec, V.last())
            d.tensor_copy(k.tail[:, :], tile(sums, 1, G - 1))

        @block.scalar
        def _(a):
            a.sem_inc(act, A.per)
            with a.Fori(0, NI) as i:
                for s in range(2):
                    a.wait_ge(vec, V.at(i, "aggr", s))
                    deviation(nc, k, s, mv, sd).then_inc(act, 1)
                for s in range(2):
                    a.wait_ge(vec, V.at(i, "norm", s))
                    nc.scalar.activation(slot(h, s), slot(h, s), ACT.Relu).then_inc(act, 1)


def conv1_nodes(nc, k):
    V = Steps("scaled")
    A = Steps("moved", "relu")
    M = Steps("turned", "product")
    with Phase(nc, k, "c1n") as ph:
        vec, act, pe = (ph.sem(n) for n in ("vector_steps", "scalar_steps", "tensor_steps"))
        loaded, stored = ph.sem2("loaded"), ph.sem2("stored")
        va, vT, y = ph.ring("va"), ph.ring("vT"), ph.ring("y")
        block = ph.block()

        @block.sync
        def _(sp):
            start_ahead(sp, stored)
            def load(i):
                for s in range(2):
                    sp.wait_ge(pe, M.at(i - 1, "turned", s))
                    sp.dma_start(slot(va, s), part(k.V0, i, s)).then_inc(loaded[s], 16)

            def store(i):
                for s in range(2):
                    sp.wait_ge(act, A.at(i, "relu", s))
                    sp.dma_start(part(k.T1, i, s), slot(y, s)).then_inc(stored[s], 16)
            load(0)
            with sp.Fori(1, NI) as i:
                load(i)
                store(i - 1)
            store(NI - 1)
            for s in range(2):
                sp.wait_ge(stored[s], NI * 16 + AHEAD)

        @block.tensor
        def _(t):
            t.sem_inc(pe, M.per)
            with t.Fori(0, NI) as i:
                for s in range(2):
                    t.wait_ge(loaded[s], i * 16 + 16)
                    t.wait_ge(act, A.at(i - 1, "moved", s))
                    transposed(nc, k, va, s, pair(k, 2 * s)).then_inc(pe, 1)
                for s in range(2):
                    t.wait_ge(act, A.at(i, "moved", s))
                    t.wait_ge(vec, V.at(i - 1, "scaled", s))
                    times_rows(nc, vT, s, k.w0[:, 0, :], pair(k, 2 * s + 1)).then_inc(pe, 1)

        @block.scalar
        def _(a):
            a.sem_inc(act, A.per)
            with a.Fori(0, NI) as i:
                for s in range(2):
                    a.wait_ge(pe, M.at(i, "turned", s))
                    nc.scalar.activation(slot(vT, s), pair(k, 2 * s), ACT.Copy).then_inc(act, 1)
                for s in range(2):
                    a.wait_ge(vec, V.at(i, "scaled", s))
                    nc.scalar.activation(slot(y, s), slot(y, s), ACT.Relu).then_inc(act, 1)

        @block.vector
        def _(d):
            d.sem_inc(vec, V.per)
            with d.Fori(0, NI) as i:
                for s in range(2):
                    d.wait_ge(pe, M.at(i, "product", s))
                    d.wait_ge(stored[s], i * 16 + AHEAD)
                    for c in range(G):
                        o = pair(k, 2 * s + 1)[:, c * D:(c + 1) * D]
                        last = nc.vector.scalar_tensor_tensor(tile(y, s, c), o, cols(k.norm_in, i, s, c),
                                                              k.b1_0[:, :], ALU.mult, ALU.add)
                    last.then_inc(vec, 1)


def conv2_edges(nc, k):
    V = Steps(*slotwise(*SUMS))
    A = Steps("scaled")
    with Phase(nc, k, "c2e") as ph:
        vec, act, staged, cleared = (ph.sem(n) for n in ("vector_steps", "scalar_steps", "staged", "cleared"))
        gathered, gbase = ph.moves("gathered", NI * 16 * G)
        stored = ph.sem2("stored")
        ring = ph.sb("ring", [P, 2 * G], I32)
        y, m, sums = ph.ring("y"), ph.ring("m"), ph.ring("sums")
        block = ph.block()

        @block.gpsimd
        def _(g):
            g.sem_inc(staged, 2)
            with g.Fori(0, NI) as i:
                for s in range(2):
                    wait_apart(g, k, act, A.at(i - 1, "scaled", s))
                    gather_columns(nc, k, g, i, s, k.slot_i, ring, staged, k.T1, y, D, gathered)

        @block.scalar
        def _(a):
            a.sem_inc(act, A.per)
            with a.Fori(0, NI) as i:
                for s in range(2):
                    a.wait_ge(gathered[s], i * (16 * G) + (16 * G + gbase))
                    a.wait_ge(vec, V.at(i - 1, SUMS[-1], s))
                    for c in range(G):
                        last = nc.scalar.activation(tile(m, s, c), tile(y, s, c), ACT.Copy, scale=cols(k.norm_out, i, s, c))
                    last.then_inc(act, 1)

        @block.vector
        def _(d):
            d.memset(tile(sums, 1, G - 1), 0.0).then_inc(cleared, 1)
            d.wait_ge(cleared, 1)
            d.sem_inc(vec, V.per)
            with d.Fori(0, NI) as i:
                for s in range(2):
                    d.wait_ge(act, A.at(i, "scaled", s))
                    d.wait_ge(stored[s], i * 16 + AHEAD)
                    running_sum(nc, k, d, vec, V, i, s, m, sums)
            d.wait_ge(vec, V.last())
            d.tensor_copy(k.tail[:, :], tile(sums, 1, G - 1))

        @block.sync
        def _(sp):
            start_ahead(sp, stored)
            with sp.Fori(0, NI) as i:
                for s in range(2):
                    sp.wait_ge(vec, V.at(i, SUMS[-1], s))
                    sp.dma_start(part(k.V1, i, s), slot(sums, s)).then_inc(stored[s], 16)
            for s in range(2):
                sp.wait_ge(stored[s], NI * 16 + AHEAD)


def conv2_nodes(nc, k):
    V = Steps("out", "x1", "stats", "aggr", "rs", "norm", "weighted", "score")
    A = Steps("moved", "sd", "relu")
    M = Steps("turned", "product")
    with Phase(nc, k, "c2n") as ph:
        vec, act, pe, staged = (ph.sem(n) for n in ("vector_steps", "scalar_steps", "tensor_steps", "staged"))
        gathered, gbase = ph.moves("gathered", NI * 16 * G)
        loaded, stored = ph.sem2("loaded"), ph.sem2("stored")
        ring = ph.sb("ring", [P, 2 * G], I32)
        va, vT, y, x, x1, h, hw = (ph.ring(n) for n in ("va", "vT", "y", "x", "x1", "h", "hw"))
        st, mv = ph.sb("st", [P, 2, G, 6]), ph.sb("mv", [P, 2, G, 2])
        sd, rs = ph.sb("sd", [P, 2, G]), ph.sb("rs", [P, 2, G])
        block = ph.block()

        @block.gpsimd
        def _(g):
            g.sem_inc(staged, 2)
            with g.Fori(0, NI) as i:
                for s in range(2):
                    wait_apart(g, k, vec, V.at(i - 1, "x1", s))
                    gather_columns(nc, k, g, i, s, k.dst_i, ring, staged, k.x, x, D, gathered)

        @block.sync
        def _(sp):
            start_ahead(sp, stored)
            def load(i):
                for s in range(2):
                    sp.wait_ge(pe, M.at(i - 1, "turned", s))
                    sp.dma_start(slot(va, s), part(k.V1, i, s)).then_inc(loaded[s], 16)

            def store(i):
                for s in range(2):
                    sp.wait_ge(vec, V.at(i, "x1", s))
                    sp.dma_start(part(k.T2, i, s), slot(y, s)).then_inc(stored[s], 16)
                    sp.dma_start(part(k.XD, i, s), slot(x1, s)).then_inc(stored[s], 16)
            load(0)
            with sp.Fori(1, NI) as i:
                load(i)
                store(i - 1)
            store(NI - 1)
            for s in range(2):
                sp.wait_ge(stored[s], NI * 32 + AHEAD)

        @block.tensor
        def _(t):
            t.sem_inc(pe, M.per)
            with t.Fori(0, NI) as i:
                for s in range(2):
                    t.wait_ge(loaded[s], i * 16 + 16)
                    t.wait_ge(act, A.at(i - 1, "moved", s))
                    transposed(nc, k, va, s, pair(k, 2 * s)).then_inc(pe, 1)
                for s in range(2):
                    t.wait_ge(act, A.at(i, "moved", s))
                    t.wait_ge(vec, V.at(i - 1, "out", s))
                    times_rows(nc, vT, s, k.w0[:, 1, :], pair(k, 2 * s + 1)).then_inc(pe, 1)

        @block.scalar
        def _(a):
            a.sem_inc(act, A.per)
            with a.Fori(0, NI) as i:
                for s in range(2):
                    a.wait_ge(pe, M.at(i, "turned", s))
                    nc.scalar.activation(slot(vT, s), pair(k, 2 * s), ACT.Copy).then_inc(act, 1)
                for s in range(2):
                    a.wait_ge(vec, V.at(i, "aggr", s))
                    deviation(nc, k, s, mv, sd).then_inc(act, 1)
                for s in range(2):
                    a.wait_ge(vec, V.at(i, "norm", s))
                    nc.scalar.activation(slot(h, s), slot(h, s), ACT.Relu).then_inc(act, 1)

        @block.vector
        def _(d):
            d.sem_inc(vec, V.per)
            with d.Fori(0, NI) as i:
                for s in range(2):
                    d.wait_ge(pe, M.at(i, "product", s))
                    d.wait_ge(stored[s], i * 32 + AHEAD)
                    for c in range(G):
                        o = pair(k, 2 * s + 1)[:, c * D:(c + 1) * D]
                        last = nc.vector.scalar_tensor_tensor(tile(y, s, c), o, cols(k.norm_in, i, s, c),
                                                              k.b2_0[:, :], ALU.mult, ALU.add)
                    last.then_inc(vec, 1)
                for s in range(2):
                    d.wait_ge(gathered[s], i * (16 * G) + (16 * G + gbase))
                    d.wait_ge(vec, V.at(i, "out", s))
                    nc.vector.tensor_tensor(slot(x1, s), slot(x, s), slot(y, s), ALU.add).then_inc(vec, 1)
                for s in range(2):
                    d.wait_ge(vec, V.at(i, "x1", s))
                    stats(nc, x1, s, st).then_inc(vec, 1)
                for s in range(2):
                    wait_apart(d, k, vec, V.at(i, "stats", s))
                    aggregate(nc, s, st, mv).then_inc(vec, 1)
                for s in range(2):
                    d.wait_ge(act, A.at(i, "sd", s))
                    nc.vector.reciprocal(rs[:, s, :], sd[:, s, :]).then_inc(vec, 1)
                for s in range(2):
                    d.wait_ge(vec, V.at(i, "rs", s))
                    normalise(nc, x1, s, mv, rs, h).then_inc(vec, 1)
                for s in range(2):
                    d.wait_ge(act, A.at(i, "relu", s))
                    nc.vector.tensor_tensor(by_tile(slot(hw, s)), by_tile(slot(h, s)), every(k.attn_r[:, :]), ALU.mult).then_inc(vec, 1)
                for s in range(2):
                    d.wait_ge(vec, V.at(i, "weighted", s))
                    nc.vector.tensor_reduce(small(k.sr, i, s), slot(hw, s).rearrange("p (k h e) -> p k h e", h=H8, e=D // H8),
                                            AX.X, ALU.add).then_inc(vec, 1)


def small(arr, i, s):
    return arr[:, :, bass.ds(i * (2 * G) + s * G, G)].rearrange("p f c -> p c f")


def relational_edges(nc, k, name, base, table, kept, first, groups, width, weights, scores):
    second = not first
    adds = ("x",) if first else ("ax", "bx", "x")
    V = Steps(*adds, "stats", "aggr", "rs", "norm", *(("u",) if second else ()), "masked", "scores")
    A = Steps("sd", "relu", "moved", "message")
    M = Steps(*slotwise(*(("turned", "base") if first else ("turned",))), "product")
    rel_rows = k.relT8 if first else k.relT4
    with Phase(nc, k, name) as ph:
        vec, act, pe, staged = (ph.sem(n) for n in ("vector_steps", "scalar_steps", "tensor_steps", "staged"))
        gathered, gbase = ph.moves("gathered", NI * 16 * G)
        loaded, stored, told = ph.sem2("loaded"), ph.sem2("stored"), ph.sem2("message_stored")
        ring = ph.sb("ring", [P, 2 * G], I32)
        a_in, x_in, x1, h, rel, msg = (ph.ring(n) for n in ("a_in", "x_in", "x1", "h", "rel", "msg"))
        hT = ph.ring("hT")
        masked = ph.sb("masked", [P, 2, 4, W])
        ax = ph.ring("ax") if second else None
        st, mv = ph.sb("st", [P, 2, G, 6]), ph.sb("mv", [P, 2, G, 2])
        sd, rs = ph.sb("sd", [P, 2, G]), ph.sb("rs", [P, 2, G])
        block = ph.block()
        nstore = 32 if second else 16

        @block.gpsimd
        def _(g):
            g.sem_inc(staged, 2)
            with g.Fori(0, NI) as i:
                for s in range(2):
                    wait_apart(g, k, vec, V.at(i - 1, adds[0], s))
                    gather_columns(nc, k, g, i, s, k.slot_i, ring, staged, table, a_in, D, gathered)

        @block.sync
        def _(sp):
            start_ahead(sp, stored, told)
            def load(i):
                for s in range(2):
                    sp.wait_ge(vec, V.at(i - 1, "x", s))
                    sp.dma_start(slot(x_in, s), part(k.XS, i, s)).then_inc(loaded[s], 16)
                    sp.wait_ge(vec, V.at(i - 1, "masked", s))
                    t0 = i * (2 * G) + s * G
                    rows = rel_rows[bass.ds(t0, G), :].rearrange("(a t) p -> a (t p)", a=1).to_broadcast([P, W])
                    sp.dma_start(slot(rel, s), rows).then_inc(loaded[s], 16)

            def store(i):
                for s in range(2):
                    sp.wait_ge(vec, V.at(i, "x", s))
                    sp.dma_start(part(k.XS, i, s), slot(x1, s)).then_inc(stored[s], 16)
                if second:
                    for s in range(2):
                        sp.wait_ge(vec, V.at(i, "u", s))
                        sp.dma_start(part(k.HS, i, s), slot(ax, s)).then_inc(stored[s], 16)
                for s in range(2):
                    sp.wait_ge(act, A.at(i, "message", s))
                    sp.dma_start(part(k.MSG, i, s), slot(msg, s)).then_inc(told[s], 16)
            load(0)
            with sp.Fori(1, NI) as i:
                load(i)
                store(i - 1)
            store(NI - 1)
            for s in range(2):
                sp.wait_ge(stored[s], NI * nstore + AHEAD)
                sp.wait_ge(told[s], NI * 16 + AHEAD)

        @block.vector
        def _(d):
            d.sem_inc(vec, V.per)
            with d.Fori(0, NI) as i:
                for s in range(2):
                    d.wait_ge(gathered[s], i * (16 * G) + (16 * G + gbase))
                    if first:
                        d.wait_ge(loaded[s], i * 32 + 32)
                        d.wait_ge(stored[s], i * nstore + AHEAD)
                        nc.vector.tensor_tensor(slot(x1, s), slot(a_in, s), slot(x_in, s), ALU.add).then_inc(vec, 1)
                    else:
                        d.wait_ge(stored[s], i * nstore + AHEAD)
                        nc.vector.tensor_tensor(by_tile(slot(ax, s)), by_tile(slot(a_in, s)), every(k.bn_a[:, :]), ALU.mult).then_inc(vec, 1)
                if second:
                    for s in range(2):
                        d.wait_ge(vec, V.at(i, "ax", s))
                        nc.vector.tensor_tensor(by_tile(slot(ax, s)), by_tile(slot(ax, s)), every(k.bn_b[:, :]), ALU.add).then_inc(vec, 1)
                    for s in range(2):
                        d.wait_ge(loaded[s], i * 32 + 32)
                        d.wait_ge(vec, V.at(i, "bx", s))
                        nc.vector.tensor_tensor(slot(x1, s), slot(ax, s), slot(x_in, s), ALU.add).then_inc(vec, 1)
                for s in range(2):
                    d.wait_ge(vec, V.at(i, "x", s))
                    stats(nc, x1, s, st).then_inc(vec, 1)
                for s in range(2):
                    wait_apart(d, k, vec, V.at(i, "stats", s))
                    aggregate(nc, s, st, mv).then_inc(vec, 1)
                for s in range(2):
                    d.wait_ge(act, A.at(i, "sd", s))
                    nc.vector.reciprocal(rs[:, s, :], sd[:, s, :]).then_inc(vec, 1)
                for s in range(2):
                    d.wait_ge(vec, V.at(i, "rs", s))
                    d.wait_ge(pe, M.at(i - 1, "turned", s))
                    normalise(nc, x1, s, mv, rs, h).then_inc(vec, 1)
                if second:
                    for s in range(2):
                        d.wait_ge(act, A.at(i, "relu", s))
                        nc.vector.tensor_tensor(by_tile(slot(ax, s)), by_tile(slot(h, s)), every(k.bias2[:, :]), ALU.add).then_inc(vec, 1)
                for s in range(2):
                    d.wait_ge(pe, M.at(i - 1, "product", s))
                    if first:
                        d.wait_ge(pe, M.at(i, "base", s))
                        right = pair(k, 1)
                    else:
                        d.wait_ge(act, A.at(i, "moved", s))
                        right = slot(hT, s)
                    for c in range(4):
                        which = k.rel_of[:, c:c + 1] if first else float(c)
                        last = nc.vector.scalar_tensor_tensor(masked[:, s, c, :], slot(rel, s), which, right, ALU.is_equal, ALU.mult)
                    last.then_inc(vec, 1)
                for s in range(2):
                    d.wait_ge(act, A.at(i, "message", s))
                    for c in range(G):
                        last = nc.vector.tensor_copy(scores[:, :, bass.ds(i * (2 * G) + (s * G + c), 1)].rearrange("p f c -> p (f c)"),
                                                     wide(k, 2, c, width)[:, D:width])
                    last.then_inc(vec, 1)

        @block.scalar
        def _(a):
            a.sem_inc(act, A.per)
            with a.Fori(0, NI) as i:
                for s in range(2):
                    a.wait_ge(vec, V.at(i, "aggr", s))
                    deviation(nc, k, s, mv, sd).then_inc(act, 1)
                for s in range(2):
                    a.wait_ge(vec, V.at(i, "norm", s))
                    nc.scalar.activation(slot(h, s), slot(h, s), ACT.Relu).then_inc(act, 1)
                for s in range(2):
                    a.wait_ge(pe, M.at(i, "turned", s))
                    if first:
                        a.wait_ge(pe, M.at(i - 1, "base", s))
                    else:
                        a.wait_ge(vec, V.at(i - 1, "masked", s))
                    nc.scalar.activation(slot(hT, s), pair(k, 0), ACT.Copy).then_inc(act, 1)
                for s in range(2):
                    a.wait_ge(pe, M.at(i, "product", s))
                    a.wait_ge(told[s], i * 16 + AHEAD)
                    for c in range(G):
                        last = nc.scalar.activation(tile(msg, s, c), wide(k, 2, c, width)[:, 0:D], ACT.Copy)
                    last.then_inc(act, 1)

        @block.tensor
        def _(t):
            t.sem_inc(pe, M.per)
            with t.Fori(0, NI) as i:
                for s in range(2):
                    t.wait_ge(act, A.at(i, "relu", s))
                    t.wait_ge(act, A.at(i if s else i - 1, "moved", 1 - s))
                    transposed(nc, k, h, s, pair(k, 0)).then_inc(pe, 1)
                    if first:
                        t.wait_ge(act, A.at(i, "moved", s))
                        t.wait_ge(vec, V.at(i if s else i - 1, "masked", 1 - s))
                        nc.tensor.matmul(pair(k, 1)[:, 0:512], k.q2[:, :], slot(hT, s)[:, 0:512], start=True, stop=True)
                        nc.tensor.matmul(pair(k, 1)[:, 512:W], k.q2[:, :], slot(hT, s)[:, 512:W], start=True, stop=True).then_inc(pe, 1)
                for s in range(2):
                    t.wait_ge(vec, V.at(i, "masked", s))
                    t.wait_ge(vec, V.at(i if s else i - 1, "scores", 1 - s))
                    t.wait_ge(act, A.at(i if s else i - 1, "message", 1 - s))
                    for c in range(G):
                        for r in range(4):
                            last = nc.tensor.matmul(wide(k, 2, c, width), masked[:, s, r, c * D:(c + 1) * D], weights[:, r, :],
                                                    start=(r == 0), stop=(r == 3))
                    last.then_inc(pe, 1)


class Chain:

    def __init__(self, eng, sem):
        self.eng, self.sem, self.n = eng, sem, 0

    def __call__(self, ins):
        self.n += 1
        ins.then_inc(self.sem, 1)
        self.eng.wait_ge(self.sem, self.n)


def fetch_back(nc, k, d, chain, to_pe, from_pe, n, ends, work, firsts, rest, F):
    chain(nc.vector.tensor_tensor(work, ends, k.fix[:, :].unsqueeze(1).to_broadcast([P, F, T]), ALU.mult))
    chain(nc.vector.tensor_reduce(firsts, work, AX.X, ALU.add))
    d.sem_inc(to_pe, 1)
    d.wait_ge(from_pe, n)
    chain(nc.vector.tensor_copy(rest, k.psum[:, 0:F]))
    chain(nc.vector.tensor_tensor(work, ends, k.end[:, :].unsqueeze(1).to_broadcast([P, F, T]), ALU.mult))
    for f in range(F):
        last = nc.vector.tensor_tensor_scan(ends[:, f, ::-1], k.more[:, ::-1], work[:, f, ::-1], rest[:, f:f + 1], ALU.mult, ALU.add)
    chain(last)


def weigh_heads1(nc, k):
    with Phase(nc, k, "att1") as ph:
        v, to_pe, from_pe, act = (ph.sem(n) for n in ("vector_done", "firsts_ready", "rest_ready", "exp_done"))
        work = ph.sb("work", [P, H8, T])
        firsts, rest = ph.sb("firsts", [P, H8]), ph.sb("rest", [P, H8])
        top = ph.sb("top", [P, T])
        block = ph.block()

        @block.vector
        def _(d):
            chain = Chain(d, v)
            fetch_back(nc, k, d, chain, to_pe, from_pe, 1, k.sr, work[:, :, :], firsts[:, :], rest[:, :], H8)
            chain(d.tensor_tensor(work[:, :, :], k.sl, k.sr, ALU.add))
            chain(d.scalar_tensor_tensor(k.sl, work[:, :, :], SLOPE, work[:, :, :], ALU.mult, ALU.max))
            chain(d.tensor_reduce(top[:, :], k.sl.rearrange("p h t -> p t h"), AX.X, ALU.max))
            chain(d.tensor_tensor(k.sl, k.sl, top[:, :].unsqueeze(1).to_broadcast([P, H8, T]), ALU.subtract))
            assert chain.n == 9
            d.wait_ge(act, 1)
            chain(d.tensor_reduce(top[:, :], k.sl.rearrange("p h t -> p t h"), AX.X, ALU.add))
            chain(d.reciprocal(top[:, :], top[:, :]))
            d.tensor_tensor(k.sl, k.sl, top[:, :].unsqueeze(1).to_broadcast([P, H8, T]), ALU.mult)

        @block.tensor
        def _(t):
            t.wait_ge(to_pe, 1)
            t.wait_ge(v, 2)
            nc.tensor.matmul(k.psum[:, 0:H8], k.back[:, :], firsts[:, :], start=True, stop=True).then_inc(from_pe, 1)

        @block.scalar
        def _(a):
            a.wait_ge(v, 9)
            nc.scalar.activation(k.sl, k.sl, ACT.Exp).then_inc(act, 1)


def weigh_edges2(nc, k):
    with Phase(nc, k, "att2") as ph:
        v, to_pe, from_pe, act = (ph.sem(n) for n in ("vector_done", "asked", "answered", "exp_done"))
        F = R4 * H4
        full = [P, R4, H4, T]
        is_rel = ph.sb("is_rel", [P, R4, T])
        val, acc, work = ph.sb("val", full), ph.sb("acc", full), ph.sb("work", full)
        tails = ph.sb("tails", [P, 3, F])
        own = ph.sb("own", [P, H4, T])
        spread = ph.sb("spread", [P, F, P])
        block = ph.block()
        rel_b = is_rel[:, :, :].unsqueeze(2).to_broadcast(full)
        flat = lambda b: b[:, :, :, :].rearrange("p r h t -> p (r h) t")

        @block.vector
        def _(d):
            chain = Chain(d, v)

            def own_of(arr4):
                chain(d.tensor_tensor(work[:, :, :, :], arr4, rel_b, ALU.mult))
                chain(d.tensor_reduce(own[:, :, :], work[:, :, :, :].rearrange("p r h t -> p h t r"), AX.X, ALU.add))

            def scan(op):
                for f in range(F):
                    last = d.tensor_tensor_scan(flat(acc)[:, f, :], k.cont[:, :], flat(val)[:, f, :], 0.0, ALU.mult, op)
                chain(last)
                chain(d.tensor_copy(tails[:, 0, :], flat(acc)[:, :, T - 1]))

            for r in range(R4):
                chain(d.tensor_scalar(is_rel[:, r, :], k.rel4[:, :], float(r), None, ALU.is_equal))
            fetch_back(nc, k, d, chain, to_pe, from_pe, 1, k.ed, flat(work), tails[:, 0, :], tails[:, 1, :], F)
            assert chain.n == 9
            own_of(k.ed.rearrange("p (r h) t -> p r h t", h=H4))
            chain(d.tensor_tensor(own[:, :, :], own[:, :, :], k.es, ALU.add))
            chain(d.scalar_tensor_tensor(k.es, own[:, :, :], SLOPE, own[:, :, :], ALU.mult, ALU.max))
            chain(d.tensor_tensor(val[:, :, :, :], k.es.unsqueeze(1).to_broadcast(full), rel_b, ALU.mult))
            scan(ALU.max)
            chain(d.tensor_tensor(spread[:, :, :], tails[:, 0, :].unsqueeze(2).to_broadcast([P, F, P]),
                                  k.ident[:, :].unsqueeze(1).to_broadcast([P, F, P]), ALU.mult))
            assert chain.n == 17
            d.sem_inc(to_pe, 1)
            d.wait_ge(from_pe, 2)
            chain(d.tensor_tensor(spread[:, :, :], k.psum[:, 0:F * P].rearrange("p (f q) -> p f q", q=P),
                                  k.intoT[:, :].unsqueeze(1).to_broadcast([P, F, P]), ALU.mult))
            chain(d.tensor_reduce(tails[:, 2, :], spread[:, :, :], AX.X, ALU.max))
            for f in range(F):
                last = d.scalar_tensor_tensor(flat(acc)[:, f, :], k.fix[:, :], tails[:, 2, f:f + 1], flat(acc)[:, f, :], ALU.mult, ALU.max)
            chain(last)
            fetch_back(nc, k, d, chain, to_pe, from_pe, 3, flat(acc), flat(work), tails[:, 0, :], tails[:, 1, :], F)
            assert chain.n == 25
            own_of(acc[:, :, :, :])
            chain(d.tensor_tensor(k.es, k.es, own[:, :, :], ALU.subtract))
            assert chain.n == 28
            d.wait_ge(act, 1)
            chain(d.tensor_tensor(val[:, :, :, :], k.es.unsqueeze(1).to_broadcast(full), rel_b, ALU.mult))
            scan(ALU.add)
            assert chain.n == 31
            d.sem_inc(to_pe, 1)
            d.wait_ge(from_pe, 4)
            chain(d.tensor_copy(tails[:, 2, :], k.psum[:, 0:F]))
            for f in range(F):
                last = d.scalar_tensor_tensor(flat(acc)[:, f, :], k.fix[:, :], tails[:, 2, f:f + 1], flat(acc)[:, f, :], ALU.mult, ALU.add)
            chain(last)
            fetch_back(nc, k, d, chain, to_pe, from_pe, 5, flat(acc), flat(work), tails[:, 0, :], tails[:, 1, :], F)
            assert chain.n == 38
            own_of(acc[:, :, :, :])
            chain(d.tensor_scalar(own[:, :, :], own[:, :, :], 1e-8, None, ALU.add))
            chain(d.reciprocal(own[:, :, :], own[:, :, :]))
            chain(d.tensor_tensor(k.es, k.es, own[:, :, :], ALU.mult))

        @block.scalar
        def _(a):
            a.wait_ge(v, 28)
            nc.scalar.activation(k.es, k.es, ACT.Exp).then_inc(act, 1)

        @block.tensor
        def _(t):
            def product(n, steps, weights, m):
                t.wait_ge(to_pe, n)
                t.wait_ge(v, steps)
                nc.tensor.matmul(k.psum[:, 0:F], weights[:, :], tails[:, m, :], start=True, stop=True).then_inc(from_pe, 1)
            product(1, 6, k.back, 0)
            t.wait_ge(to_pe, 2)
            t.wait_ge(v, 17)
            for c in range(4):
                last = nc.tensor.matmul(k.psum[:, c * 512:(c + 1) * 512], k.ones[:, :],
                                        spread[:, 4 * c:4 * c + 4, :].rearrange("p f q -> p (f q)"), start=True, stop=True)
            last.then_inc(from_pe, 1)
            product(3, 22, k.back, 0)
            product(4, 31, k.into, 0)
            product(5, 35, k.back, 0)


def weighted_edges(nc, k, name, heads, att, V_table):
    V = Steps("weighted", *slotwise(*SUMS))
    with Phase(nc, k, name) as ph:
        vec, cleared = ph.sem("vector_steps"), ph.sem("cleared")
        loaded, stored = ph.sem2("loaded"), ph.sem2("stored")
        m, w, sums = ph.ring("m"), ph.ring("w"), ph.ring("sums")
        block = ph.block()

        @block.sync
        def _(sp):
            start_ahead(sp, stored)
            def load(i):
                for s in range(2):
                    sp.wait_ge(vec, V.at(i - 1, "weighted", s))
                    sp.dma_start(slot(m, s), part(k.MSG, i, s)).then_inc(loaded[s], 16)

            def store(i):
                for s in range(2):
                    sp.wait_ge(vec, V.at(i, SUMS[-1], s))
                    sp.dma_start(part(V_table, i, s), slot(sums, s)).then_inc(stored[s], 16)
            load(0)
            with sp.Fori(1, NI) as i:
                load(i)
                store(i - 1)
            store(NI - 1)
            for s in range(2):
                sp.wait_ge(stored[s], NI * 16 + AHEAD)

        @block.vector
        def _(d):
            d.memset(tile(sums, 1, G - 1), 0.0).then_inc(cleared, 1)
            d.wait_ge(cleared, 1)
            d.sem_inc(vec, V.per)
            with d.Fori(0, NI) as i:
                for s in range(2):
                    d.wait_ge(loaded[s], i * 16 + 16)
                    d.wait_ge(vec, V.at(i - 1, SUMS[-1], s))
                    e = D // heads
                    view = lambda b: slot(b, s).rearrange("p (k h e) -> p k h e", h=heads, e=e)
                    for c in range(G):
                        wt = att[:, :, bass.ds(i * (2 * G) + (s * G + c), 1)].to_broadcast([P, heads, e])
                        last = nc.vector.tensor_tensor(view(w)[:, c, :, :], view(m)[:, c, :, :], wt, ALU.mult)
                    last.then_inc(vec, 1)
                for s in range(2):
                    d.wait_ge(vec, V.at(i, "weighted", s))
                    d.wait_ge(stored[s], i * 16 + AHEAD)
                    running_sum(nc, k, d, vec, V, i, s, w, sums)
            d.wait_ge(vec, V.last())
            d.tensor_copy(k.tail[:, :], tile(sums, 1, G - 1))


def batch_stats(nc, k):
    A = Steps("squared")
    M = Steps("summed")
    with Phase(nc, k, "bn") as ph:
        act, pe, v, tdone, ready = (ph.sem(n) for n in ("scalar_steps", "tensor_steps", "vector_done", "tensor_done", "sqrt_done"))
        loaded = ph.sem2("loaded")
        va, sq = ph.ring("va"), ph.ring("sq")
        c = ph.sb("c", [P, 6])
        dg = ph.sb("dg", [P, 2, P])
        block = ph.block()

        @block.sync
        def _(sp):
            with sp.Fori(0, NI) as i:
                for s in range(2):
                    sp.wait_ge(pe, M.at(i - 1, "summed", s))
                    sp.dma_start(slot(va, s), part(k.V2, i, s)).then_inc(loaded[s], 16)

        @block.scalar
        def _(a):
            a.sem_inc(act, A.per)
            with a.Fori(0, NI) as i:
                for s in range(2):
                    a.wait_ge(loaded[s], i * 16 + 16)
                    a.wait_ge(pe, M.at(i - 1, "summed", s))
                    nc.scalar.activation(slot(sq, s), slot(va, s), ACT.Square).then_inc(act, 1)
            a.wait_ge(v, 4)
            nc.scalar.activation(c[:, 3:4], c[:, 2:3], ACT.Sqrt, bias=k.eps[:, 0:1]).then_inc(ready, 1)

        @block.tensor
        def _(t):
            S, Q = k.psum[:, 0:1], k.psum[:, 512:513]
            nc.tensor.matmul(S, k.zeros[:, :], k.ones[:, 0:1], start=True, stop=False, skip_group_check=True)
            nc.tensor.matmul(Q, k.zeros[:, :], k.ones[:, 0:1], start=True, stop=False, skip_group_check=True)
            t.sem_inc(pe, M.per)
            with t.Fori(0, NI) as i:
                for s in range(2):
                    t.wait_ge(loaded[s], i * 16 + 16)
                    t.wait_ge(act, A.at(i, "squared", s))
                    for j in range(G):
                        nc.tensor.matmul(S, tile(va, s, j), cols(k.real_end, i, s, j), start=False, stop=False, skip_group_check=True)
                        last = nc.tensor.matmul(Q, tile(sq, s, j), cols(k.real_end, i, s, j), start=False, stop=False, skip_group_check=True)
                    last.then_inc(pe, 1)
            t.wait_ge(v, 10)
            nc.tensor.matmul(k.psum[:, 1024:1024 + 2 * P], k.ones[:, :], dg[:, :, :].rearrange("p a q -> p (a q)"),
                             start=True, stop=True).then_inc(tdone, 1)

        @block.vector
        def _(d):
            chain = Chain(d, v)
            d.wait_ge(pe, M.last())
            chain(d.tensor_scalar(c[:, 0:1], k.psum[:, 0:1], 1.0 / NODES, None, ALU.mult))
            chain(d.tensor_scalar(c[:, 1:2], k.psum[:, 512:513], 1.0 / NODES, None, ALU.mult))
            chain(d.tensor_tensor(c[:, 2:3], c[:, 0:1], c[:, 0:1], ALU.mult))
            chain(d.tensor_tensor(c[:, 2:3], c[:, 1:2], c[:, 2:3], ALU.subtract))
            d.wait_ge(ready, 1)
            chain(d.reciprocal(c[:, 3:4], c[:, 3:4]))
            chain(d.tensor_tensor(c[:, 3:4], c[:, 3:4], k.gb[:, 0:1], ALU.mult))
            chain(d.tensor_tensor(c[:, 4:5], c[:, 0:1], c[:, 3:4], ALU.mult))
            chain(d.tensor_tensor(c[:, 4:5], k.gb[:, 1:2], c[:, 4:5], ALU.subtract))
            chain(d.tensor_scalar(dg[:, 0, :], k.ident[:, :], c[:, 3:4], None, ALU.mult))
            chain(d.tensor_scalar(dg[:, 1, :], k.ident[:, :], c[:, 4:5], None, ALU.mult))
            d.wait_ge(tdone, 1)
            chain(d.tensor_copy(k.bn_a[:, :], k.psum[:, 1024:1024 + P]))
            chain(d.tensor_copy(k.bn_b[:, :], k.psum[:, 1024 + P:1024 + 2 * P]))
            chain(d.tensor_tensor(k.plain[:, :], k.bn_b[:, :], k.b2_0[:, :], ALU.add))


def layer2_nodes(nc, k):
    V = Steps("ax", "bx", "x", "stats", "aggr", "rs", "norm", "u", "scores")
    A = Steps("sd", "relu", "moved")
    M = Steps("turned", "product")
    F = R4 * H4
    with Phase(nc, k, "n2") as ph:
        vec, act, pe = (ph.sem(n) for n in ("vector_steps", "scalar_steps", "tensor_steps"))
        loaded, stored = ph.sem2("loaded"), ph.sem2("stored")
        a_in, x_in, ax, x1, h, hT = (ph.ring(n) for n in ("a_in", "x_in", "ax", "x1", "h", "hT"))
        st, mv = ph.sb("st", [P, 2, G, 6]), ph.sb("mv", [P, 2, G, 2])
        sd, rs = ph.sb("sd", [P, 2, G]), ph.sb("rs", [P, 2, G])
        block = ph.block()

        @block.sync
        def _(sp):
            start_ahead(sp, stored)
            def load(i):
                for s in range(2):
                    sp.wait_ge(vec, V.at(i - 1, "x", s))
                    sp.dma_start(slot(a_in, s), part(k.V2, i, s)).then_inc(loaded[s], 16)
                    sp.dma_start(slot(x_in, s), part(k.XD, i, s)).then_inc(loaded[s], 16)

            def store(i):
                for s in range(2):
                    sp.wait_ge(vec, V.at(i, "x", s))
                    sp.dma_start(part(k.XD, i, s), slot(x1, s)).then_inc(stored[s], 16)
                for s in range(2):
                    sp.wait_ge(vec, V.at(i, "u", s))
                    sp.dma_start(part(k.HD, i, s), slot(ax, s)).then_inc(stored[s], 16)
            load(0)
            with sp.Fori(1, NI) as i:
                load(i)
                store(i - 1)
            store(NI - 1)
            for s in range(2):
                sp.wait_ge(stored[s], NI * 32 + AHEAD)

        @block.vector
        def _(d):
            d.sem_inc(vec, V.per)
            with d.Fori(0, NI) as i:
                for s in range(2):
                    d.wait_ge(loaded[s], i * 32 + 32)
                    d.wait_ge(stored[s], i * 32 + AHEAD)
                    nc.vector.tensor_tensor(by_tile(slot(ax, s)), by_tile(slot(a_in, s)), every(k.bn_a[:, :]), ALU.mult).then_inc(vec, 1)
                for s in range(2):
                    d.wait_ge(vec, V.at(i, "ax", s))
                    nc.vector.tensor_tensor(by_tile(slot(ax, s)), by_tile(slot(ax, s)), every(k.bn_b[:, :]), ALU.add).then_inc(vec, 1)
                for s in range(2):
                    d.wait_ge(vec, V.at(i, "bx", s))
                    nc.vector.tensor_tensor(slot(x1, s), slot(ax, s), slot(x_in, s), ALU.add).then_inc(vec, 1)
                for s in range(2):
                    d.wait_ge(vec, V.at(i, "x", s))
                    stats(nc, x1, s, st).then_inc(vec, 1)
                for s in range(2):
                    wait_apart(d, k, vec, V.at(i, "stats", s))
                    aggregate(nc, s, st, mv).then_inc(vec, 1)
                for s in range(2):
                    d.wait_ge(act, A.at(i, "sd", s))
                    nc.vector.reciprocal(rs[:, s, :], sd[:, s, :]).then_inc(vec, 1)
                for s in range(2):
                    d.wait_ge(vec, V.at(i, "rs", s))
                    d.wait_ge(pe, M.at(i - 1, "turned", s))
                    normalise(nc, x1, s, mv, rs, h).then_inc(vec, 1)
                for s in range(2):
                    d.wait_ge(act, A.at(i, "relu", s))
                    nc.vector.tensor_tensor(by_tile(slot(ax, s)), by_tile(slot(h, s)), every(k.bias2[:, :]), ALU.add).then_inc(vec, 1)
                for s in range(2):
                    d.wait_ge(pe, M.at(i, "product", s))
                    got = pair(k, 2 * s + 1)[:, 0:G * F].rearrange("p (c f) -> p c f", f=F)
                    nc.vector.tensor_copy(small(k.ed, i, s), got).then_inc(vec, 1)

        @block.scalar
        def _(a):
            a.sem_inc(act, A.per)
            with a.Fori(0, NI) as i:
                for s in range(2):
                    a.wait_ge(vec, V.at(i, "aggr", s))
                    deviation(nc, k, s, mv, sd).then_inc(act, 1)
                for s in range(2):
                    a.wait_ge(vec, V.at(i, "norm", s))
                    nc.scalar.activation(slot(h, s), slot(h, s), ACT.Relu).then_inc(act, 1)
                for s in range(2):
                    a.wait_ge(pe, M.at(i, "turned", s))
                    nc.scalar.activation(slot(hT, s), pair(k, 2 * s), ACT.Copy).then_inc(act, 1)

        @block.tensor
        def _(t):
            t.sem_inc(pe, M.per)
            with t.Fori(0, NI) as i:
                for s in range(2):
                    t.wait_ge(act, A.at(i, "relu", s))
                    t.wait_ge(act, A.at(i - 1, "moved", s))
                    transposed(nc, k, h, s, pair(k, 2 * s)).then_inc(pe, 1)
                for s in range(2):
                    t.wait_ge(act, A.at(i, "moved", s))
                    t.wait_ge(vec, V.at(i - 1, "scores", s))
                    for c in range(G):
                        last = nc.tensor.matmul(pair(k, 2 * s + 1)[:, c * F:(c + 1) * F], tile(hT, s, c), k.vdst[:, :], start=True, stop=True)
                    last.then_inc(pe, 1)


def layer3_inputs(nc, k, name, edges):
    V = Steps("o", "stats", "aggr", "rs", "norm", "scaled", "shifted", "x", "stats2", "aggr2", "rs2", "norm2",
              *(slotwise(*SUMS) if edges else ()))
    A = Steps("sd", "sd2", "relu")
    x_table, u_table = (k.XS, k.HS) if edges else (k.XD, k.HD)
    with Phase(nc, k, name) as ph:
        vec, act, staged, cleared = (ph.sem(n) for n in ("vector_steps", "scalar_steps", "staged", "cleared"))
        gathered, gbase = ph.moves("gathered", NI * 16 * G if edges else 0)
        loaded, stored = ph.sem2("loaded"), ph.sem2("stored")
        summed = ph.sem2("sums_stored")
        ring = ph.sb("ring", [P, 2 * G], I32)
        a_in, u_in, x_in, o, y, x3, h = (ph.ring(n) for n in ("a_in", "u_in", "x_in", "o", "y", "x3", "h"))
        sums = ph.ring("sums") if edges else None
        st, mv = ph.sb("st", [P, 2, G, 6]), ph.sb("mv", [P, 2, G, 2])
        sd, rs = ph.sb("sd", [P, 2, G]), ph.sb("rs", [P, 2, G])
        block = ph.block()
        nload = 32 if edges else 48
        nstore = 16 if edges else 32

        if edges:
            @block.gpsimd
            def _(g):
                g.sem_inc(staged, 2)
                with g.Fori(0, NI) as i:
                    for s in range(2):
                        wait_apart(g, k, vec, V.at(i - 1, "o", s))
                        gather_columns(nc, k, g, i, s, k.slot_i, ring, staged, k.V3, a_in, D, gathered)

        @block.sync
        def _(sp):
            start_ahead(sp, stored, summed)
            def load(i):
                for s in range(2):
                    sp.wait_ge(vec, V.at(i - 1, "x", s))
                    if not edges:
                        sp.dma_start(slot(a_in, s), part(k.V3, i, s)).then_inc(loaded[s], 16)
                    sp.dma_start(slot(u_in, s), part(u_table, i, s)).then_inc(loaded[s], 16)
                    sp.dma_start(slot(x_in, s), part(x_table, i, s)).then_inc(loaded[s], 16)

            def store(i):
                if not edges:
                    for s in range(2):
                        sp.wait_ge(vec, V.at(i, "x", s))
                        sp.dma_start(part(k.XD, i, s), slot(x3, s)).then_inc(stored[s], 16)
                for s in range(2):
                    sp.wait_ge(act, A.at(i, "relu", s))
                    sp.dma_start(part(u_table, i, s), slot(h, s)).then_inc(stored[s], 16)
                if edges:
                    for s in range(2):
                        sp.wait_ge(vec, V.at(i, SUMS[-1], s))
                        sp.dma_start(part(k.V4, i, s), slot(sums, s)).then_inc(summed[s], 16)
            load(0)
            with sp.Fori(1, NI) as i:
                load(i)
                store(i - 1)
            store(NI - 1)
            for s in range(2):
                sp.wait_ge(stored[s], NI * nstore + AHEAD)
                if edges:
                    sp.wait_ge(summed[s], NI * 16 + AHEAD)

        @block.vector
        def _(d):
            if edges:
                d.memset(tile(sums, 1, G - 1), 0.0).then_inc(cleared, 1)
                d.wait_ge(cleared, 1)
            d.sem_inc(vec, V.per)
            with d.Fori(0, NI) as i:
                for s in range(2):
                    if edges:
                        d.wait_ge(gathered[s], i * (16 * G) + (16 * G + gbase))
                    d.wait_ge(loaded[s], i * nload + nload)
                    nc.vector.tensor_tensor(slot(o, s), slot(a_in, s), slot(u_in, s), ALU.add).then_inc(vec, 1)
                for s in range(2):
                    d.wait_ge(vec, V.at(i, "o", s))
                    stats(nc, o, s, st).then_inc(vec, 1)
                for s in range(2):
                    wait_apart(d, k, vec, V.at(i, "stats", s))
                    aggregate(nc, s, st, mv).then_inc(vec, 1)
                for s in range(2):
                    d.wait_ge(act, A.at(i, "sd", s))
                    nc.vector.reciprocal(rs[:, s, :], sd[:, s, :]).then_inc(vec, 1)
                for s in range(2):
                    d.wait_ge(vec, V.at(i, "rs", s))
                    normalise(nc, o, s, mv, rs, y).then_inc(vec, 1)
                for s in range(2):
                    d.wait_ge(vec, V.at(i, "norm", s))
                    nc.vector.tensor_tensor(by_tile(slot(y, s)), by_tile(slot(y, s)), every(k.ln_g[:, :]), ALU.mult).then_inc(vec, 1)
                for s in range(2):
                    d.wait_ge(vec, V.at(i, "scaled", s))
                    nc.vector.tensor_tensor(by_tile(slot(y, s)), by_tile(slot(y, s)), every(k.ln_b[:, :]), ALU.add).then_inc(vec, 1)
                for s in range(2):
                    d.wait_ge(vec, V.at(i, "shifted", s))
                    d.wait_ge(stored[s], i * nstore + AHEAD)
                    nc.vector.tensor_tensor(slot(x3, s), slot(y, s), slot(x_in, s), ALU.add).then_inc(vec, 1)
                for s in range(2):
                    d.wait_ge(vec, V.at(i, "x", s))
                    stats(nc, x3, s, st).then_inc(vec, 1)
                for s in range(2):
                    wait_apart(d, k, vec, V.at(i, "stats2", s))
                    aggregate(nc, s, st, mv).then_inc(vec, 1)
                for s in range(2):
                    d.wait_ge(act, A.at(i, "sd2", s))
                    nc.vector.reciprocal(rs[:, s, :], sd[:, s, :]).then_inc(vec, 1)
                for s in range(2):
                    d.wait_ge(vec, V.at(i, "rs2", s))
                    normalise(nc, x3, s, mv, rs, h).then_inc(vec, 1)
                if edges:
                    for s in range(2):
                        d.wait_ge(act, A.at(i, "relu", s))
                        d.wait_ge(summed[s], i * 16 + AHEAD)
                        running_sum(nc, k, d, vec, V, i, s, h, sums)
            if edges:
                d.wait_ge(vec, V.last())
                d.tensor_copy(k.tail[:, :], tile(sums, 1, G - 1))

        @block.scalar
        def _(a):
            a.sem_inc(act, A.per)
            with a.Fori(0, NI) as i:
                for s in range(2):
                    a.wait_ge(vec, V.at(i, "aggr", s))
                    deviation(nc, k, s, mv, sd).then_inc(act, 1)
                for s in range(2):
                    a.wait_ge(vec, V.at(i, "aggr2", s))
                    deviation(nc, k, s, mv, sd).then_inc(act, 1)
                for s in range(2):
                    a.wait_ge(vec, V.at(i, "norm2", s))
                    nc.scalar.activation(slot(h, s), slot(h, s), ACT.Relu).then_inc(act, 1)


def graph_mlp(nc, k, name, edges, layer):
    final = layer == 1
    V = Steps("z", "biased", *(("out",) if final else ()), *(slotwise(*SUMS) if edges else ()))
    A = Steps("moved", "hidden", *(() if final else ("relu",)))
    M = Steps("turned", "inner", "product")
    sum_table = k.V5 if final else k.V4
    with Phase(nc, k, name) as ph:
        vec, act, pe, staged, cleared = (ph.sem(n) for n in ("vector_steps", "scalar_steps", "tensor_steps", "staged", "cleared"))
        gathered, gbase = ph.moves("gathered", NI * 16 * G if edges else 0)
        scattered, sbase = ph.moves("scattered", NI * 16 * G if final else 0)
        loaded, stored = ph.sem2("loaded"), ph.sem2("stored")
        ring = ph.sb("ring", [P, 2 * G], I32)
        a_in, h_in, z, zT, hidden, y = (ph.ring(n) for n in ("a_in", "h_in", "z", "zT", "hidden", "y"))
        x_in = ph.ring("x_in") if final else None
        sums = ph.ring("sums") if edges else None
        block = ph.block()
        nload = 16 + 16 * (not edges) + 16 * final
        w_in, w_out = k.w3[:, 2 * layer, :], k.w3[:, 2 * layer + 1, :]
        b_in, b_out = k.b3[:, 2 * layer:2 * layer + 1], k.b3_row[:, layer, :]

        @block.gpsimd
        def _(g):
            if edges or final:
                g.sem_inc(staged, 2)
                with g.Fori(0, NI) as i:
                    for s in range(2):
                        if edges:
                            wait_apart(g, k, vec, V.at(i - 1, "z", s))
                            gather_columns(nc, k, g, i, s, k.slot_i, ring, staged, k.V4, a_in, D, gathered)
                        else:
                            wait_apart(g, k, scattered[s], i * (16 * G) + sbase)
                            g.tensor_copy(ring[:, s * G:(s + 1) * G], cols(k.out_i, i, s, 0, G)).then_inc(staged, 1)
                            wait_apart(g, k, staged, i * 2 + (s + 3))
                            wait_apart(g, k, vec, V.at(i, "out", s))
                            for c in range(G):
                                at = bass.IndirectOffsetOnAxis(ap=ring[:, s * G + c:s * G + c + 1], axis=0)
                                g.indirect_dma_start(k.out, at, tile(y, s, c), None, bounds_check=NODES - 1,
                                                     oob_is_err=False).then_inc(scattered[s], 16)
                if final:
                    for s in range(2):
                        g.wait_ge(scattered[s], NI * 16 * G + sbase)

        @block.sync
        def _(sp):
            start_ahead(sp, stored)
            def load(i):
                for s in range(2):
                    sp.wait_ge(vec, V.at(i - 1, "z", s))
                    if not edges:
                        sp.dma_start(slot(a_in, s), part(sum_table, i, s)).then_inc(loaded[s], 16)
                    sp.dma_start(slot(h_in, s), part(k.HS if edges else k.HD, i, s)).then_inc(loaded[s], 16)
                    if final:
                        sp.wait_ge(vec, V.at(i - 1, "out", s))
                        sp.dma_start(slot(x_in, s), part(k.XD, i, s)).then_inc(loaded[s], 16)

            def store(i):
                for s in range(2):
                    if edges:
                        sp.wait_ge(vec, V.at(i, SUMS[-1], s))
                        sp.dma_start(part(k.V5, i, s), slot(sums, s)).then_inc(stored[s], 16)
                    elif not final:
                        sp.wait_ge(act, A.at(i, "relu", s))
                        sp.dma_start(part(k.HD, i, s), slot(y, s)).then_inc(stored[s], 16)
            load(0)
            with sp.Fori(1, NI) as i:
                load(i)
                store(i - 1)
            store(NI - 1)
            if not final:
                for s in range(2):
                    sp.wait_ge(stored[s], NI * 16 + AHEAD)

        @block.vector
        def _(d):
            if edges:
                d.memset(tile(sums, 1, G - 1), 0.0).then_inc(cleared, 1)
                d.wait_ge(cleared, 1)
            d.sem_inc(vec, V.per)
            with d.Fori(0, NI) as i:
                for s in range(2):
                    if edges:
                        d.wait_ge(gathered[s], i * (16 * G) + (16 * G + gbase))
                    d.wait_ge(loaded[s], i * nload + nload)
                    d.wait_ge(pe, M.at(i - 1, "turned", s))
                    nc.vector.tensor_tensor(slot(z, s), slot(a_in, s), slot(h_in, s), ALU.add).then_inc(vec, 1)
                for s in range(2):
                    d.wait_ge(pe, M.at(i, "product", s))
                    if final:
                        d.wait_ge(scattered[s], i * (16 * G) + sbase)
                    elif edges:
                        d.wait_ge(vec, V.at(i - 1, SUMS[-1], s))
                    else:
                        d.wait_ge(stored[s], i * 16 + AHEAD)
                    nc.vector.tensor_tensor(by_tile(slot(y, s)), by_tile(pair(k, 2 * s)), every(b_out), ALU.add).then_inc(vec, 1)
                if final:
                    for s in range(2):
                        d.wait_ge(vec, V.at(i, "biased", s))
                        nc.vector.scalar_tensor_tensor(slot(y, s), slot(y, s), 0.0, slot(x_in, s), ALU.max, ALU.add).then_inc(vec, 1)
                if edges:
                    for s in range(2):
                        d.wait_ge(act, A.at(i, "relu", s))
                        d.wait_ge(stored[s], i * 16 + AHEAD)
                        running_sum(nc, k, d, vec, V, i, s, y, sums)
            if edges:
                d.wait_ge(vec, V.last())
                d.tensor_copy(k.tail[:, :], tile(sums, 1, G - 1))

        @block.scalar
        def _(a):
            a.sem_inc(act, A.per)
            with a.Fori(0, NI) as i:
                for s in range(2):
                    a.wait_ge(pe, M.at(i, "turned", s))
                    nc.scalar.activation(slot(zT, s), pair(k, 2 * s), ACT.Copy).then_inc(act, 1)
                for s in range(2):
                    a.wait_ge(pe, M.at(i, "inner", s))
                    nc.scalar.activation(slot(hidden, s), pair(k, 2 * s + 1), ACT.Relu, bias=b_in).then_inc(act, 1)
                if not final:
                    for s in range(2):
                        a.wait_ge(vec, V.at(i, "biased", s))
                        nc.scalar.activation(slot(y, s), slot(y, s), ACT.Relu).then_inc(act, 1)

        @block.tensor
        def _(t):
            t.sem_inc(pe, M.per)
            with t.Fori(0, NI) as i:
                for s in range(2):
                    t.wait_ge(vec, V.at(i, "z", s))
                    t.wait_ge(vec, V.at(i - 1, "biased", s))
                    transposed(nc, k, z, s, pair(k, 2 * s)).then_inc(pe, 1)
                for s in range(2):
                    t.wait_ge(act, A.at(i, "moved", s))
                    times_cols(nc, zT, s, w_in, pair(k, 2 * s + 1)).then_inc(pe, 1)
                for s in range(2):
                    t.wait_ge(act, A.at(i, "hidden", s))
                    times_rows(nc, hidden, s, w_out, pair(k, 2 * s)).then_inc(pe, 1)


def all_nodes(nc, k):
    ROWS = P * G
    V = Steps("u", "x3", "stats2", "stats3", "stats", "aggr2", "aggr3", "aggr", "rs2", "rs3", "rs", "nb2", "nb", "norm3",
              "out", "scaled",
              lag=dict(u=1, stats2=1, aggr2=1, rs2=1, nb2=1, scaled=1, x3=2, stats3=2, aggr3=2, rs3=2, norm3=2, out=3))
    A = Steps("hidden2", "hidden3", "sd2", "sd3", "sd", "norm2", "relu", "moved", "hidden1",
              lag=dict(sd2=1, norm2=1, sd3=2, moved=2, hidden1=2, hidden2=3, hidden3=3))
    M = Steps("inner2", "inner3", "product", "turned", "inner1", lag=dict(turned=2, inner1=2, inner2=3, inner3=3, product=3))
    X = Steps("xb", "x", "x3_kept", lag=dict(xb=1, x3_kept=2))
    N = -(-NODES // ROWS) // 2
    LAG = 3
    with Phase(nc, k, "all") as ph:
        vec, act, pe, pool, cleared = (ph.sem(n) for n in ("vector_steps", "scalar_steps", "tensor_steps", "gpsimd_steps", "cleared"))
        loaded, stored = ph.sem2("loaded"), ph.sem2("stored")
        x_in, x, xb, h, u, y, x3, x3k, h3, hT, aT, out = (
            ph.ring(n) for n in ("x_in", "x", "xb", "h", "u", "y", "x3", "x3k", "h3", "hT", "aT", "out"))
        st = [ph.sb(f"st{n}", [P, 2, G, 6]) for n in range(3)]
        mv = [ph.sb(f"mv{n}", [P, 2, G, 2]) for n in range(3)]
        sd, rs, nb = ([ph.sb(f"{w}{n}", [P, 2, G]) for n in range(3)] for w in ("sd", "rs", "nb"))
        block = ph.block()

        def rows(table, i, s):
            first = NODES - ROWS if (isinstance(i, int) and i == N - 1 and s == 1) else i * (2 * ROWS) + s * ROWS
            return table[bass.ds(first, ROWS), :].rearrange("(p k) f -> p (k f)", k=G)

        @block.sync
        def _(sp):
            def load(i, at):
                for s in range(2):
                    sp.wait_ge(pool, X.at(at - 1, "x", s))
                    sp.dma_start(slot(x_in, s), rows(k.x, i, s)).then_inc(loaded[s], 16)

            def store(i):
                for s in range(2):
                    sp.wait_ge(vec, V.at(i, "out", s))
                    if isinstance(i, int) and i == N - 1 and s == 1:
                        sp.wait_ge(stored[0], (LAG + N) * 16 + AHEAD)
                    sp.dma_start(rows(k.out, i, s), slot(out, s)).then_inc(stored[s], 16)
            for s in range(2):
                sp.sem_inc(stored[s], LAG * 16 + AHEAD)
            for i in range(LAG + 1):
                load(i, i)
            with sp.Fori(LAG + 1, N - 1) as i:
                load(i, i)
                store(i - (LAG + 1))
            load(N - 1, N - 1)
            store(N - 2 - LAG)
            for i in range(LAG):
                load(N - 1, N + i)
                store(N - 1 - LAG + i)
            store(N - 1)
            for s in range(2):
                sp.wait_ge(loaded[s], (N + LAG) * 16)
                sp.wait_ge(stored[s], (LAG + N) * 16 + AHEAD)

        @block.gpsimd
        def _(g):
            for b in (x, h, u, y, xb, x3, x3k, hT, aT):
                last = g.memset(b[:, :], 0.0)
            last.then_inc(cleared, 1)
            g.wait_ge(cleared, 1)
            g.sem_inc(pool, X.per)
            with g.Fori(0, N + LAG) as i:
                for s in range(2):
                    g.wait_ge(vec, V.at(i - 2, "x3", s))
                    g.wait_ge(pool, X.at(i - 1, "x", s))
                    nc.gpsimd.tensor_tensor(by_tile(slot(xb, s)), by_tile(slot(x, s)), every(k.ln_b[:, :]), ALU.add).then_inc(pool, 1)
                for s in range(2):
                    g.wait_ge(loaded[s], i * 16 + 16)
                    g.wait_ge(act, A.at(i - 1, "relu", s))
                    g.wait_ge(pool, X.at(i - 1, "xb", s))
                    nc.gpsimd.tensor_tensor(by_tile(slot(x, s)), by_tile(slot(x_in, s)), every(k.plain[:, :]), ALU.add).then_inc(pool, 1)
                for s in range(2):
                    wait_apart(g, k, vec, V.at(i - 3, "out", s))
                    nc.gpsimd.tensor_copy(slot(x3k, s), slot(x3, s)).then_inc(pool, 1)

        @block.vector
        def _(d):
            d.wait_ge(cleared, 1)
            d.sem_inc(vec, V.per)
            with d.Fori(0, N + LAG) as i:
                for s in range(2):
                    d.wait_ge(act, A.at(i - 1, "relu", s))
                    nc.vector.tensor_tensor(by_tile(slot(u, s)), by_tile(slot(h, s)), every(k.bias2[:, :]), ALU.add).then_inc(vec, 1)
                for s in range(2):
                    d.wait_ge(vec, V.at(i - 2, "scaled", s))
                    d.wait_ge(pool, X.at(i - 2, "xb", s))
                    d.wait_ge(pool, X.at(i - 3, "x3_kept", s))
                    nc.vector.tensor_tensor(slot(x3, s), slot(y, s), slot(xb, s), ALU.add).then_inc(vec, 1)
                for s in range(2):
                    d.wait_ge(vec, V.at(i - 1, "u", s))
                    stats(nc, u, s, st[1]).then_inc(vec, 1)
                for s in range(2):
                    d.wait_ge(vec, V.at(i - 2, "x3", s))
                    stats(nc, x3, s, st[2]).then_inc(vec, 1)
                for s in range(2):
                    d.wait_ge(pool, X.at(i, "x", s))
                    stats(nc, x, s, st[0]).then_inc(vec, 1)
                for n, lag in (("2", 1), ("3", 2), ("", 0)):
                    for s in range(2):
                        d.wait_ge(act, A.at(i - lag - 1, "sd" + n, s))
                        wait_apart(d, k, vec, V.at(i - lag, "stats" + n, s))
                        aggregate(nc, s, st[lag], mv[lag]).then_inc(vec, 1)
                for n, lag in (("2", 1), ("3", 2), ("", 0)):
                    for s in range(2):
                        d.wait_ge(act, A.at(i - lag, "sd" + n, s))
                        nc.vector.reciprocal(rs[lag][:, s, :], sd[lag][:, s, :]).then_inc(vec, 1)
                for n, lag in (("2", 1), ("", 0)):
                    for s in range(2):
                        d.wait_ge(vec, V.at(i - lag, "rs" + n, s))
                        nc.vector.scalar_tensor_tensor(nb[lag][:, s, :], mv[lag][:, s, :, 0], -1.0, rs[lag][:, s, :],
                                                       ALU.mult, ALU.mult).then_inc(vec, 1)
                for s in range(2):
                    d.wait_ge(vec, V.at(i - 2, "rs3", s))
                    d.wait_ge(pe, M.at(i - 3, "turned", s))
                    normalise(nc, x3, s, mv[2], rs[2], h3).then_inc(vec, 1)
                for s in range(2):
                    d.wait_ge(pe, M.at(i - 3, "product", s))
                    d.wait_ge(pool, X.at(i - 3, "x3_kept", s))
                    d.wait_ge(stored[s], i * 16 + AHEAD)
                    nc.vector.scalar_tensor_tensor(slot(out, s), pair(k, 2 * s), 0.0, slot(x3k, s), ALU.max, ALU.add).then_inc(vec, 1)
                for s in range(2):
                    d.wait_ge(act, A.at(i - 1, "norm2", s))
                    nc.vector.tensor_tensor(by_tile(slot(y, s)), by_tile(slot(y, s)), every(k.ln_g[:, :]), ALU.mult).then_inc(vec, 1)

        @block.scalar
        def _(a):
            a.wait_ge(cleared, 1)
            a.sem_inc(act, A.per)
            with a.Fori(0, N + LAG) as i:
                def norms(src, dst, n, lag, func):
                    for s in range(2):
                        a.wait_ge(vec, V.at(i - lag, "nb" + n, s))
                        for c in range(G):
                            last = nc.scalar.activation(tile(dst, s, c), tile(src, s, c), func,
                                                        scale=rs[lag][:, s, c:c + 1], bias=nb[lag][:, s, c:c + 1])
                        last.then_inc(act, 1)

                def hidden(n, lag, dst):
                    for s in range(2):
                        a.wait_ge(pe, M.at(i - lag, f"inner{n}", s))
                        if n == 1:
                            a.wait_ge(pe, M.at(i - 3, "product", s))
                        nc.scalar.activation(slot(dst, s), pair(k, 2 * s + 1), ACT.Relu, bias=k.b3[:, n - 1:n]).then_inc(act, 1)

                hidden(2, 3, hT)
                hidden(3, 3, aT)
                for n, lag in (("2", 1), ("3", 2), ("", 0)):
                    for s in range(2):
                        a.wait_ge(vec, V.at(i - lag, "aggr" + n, s))
                        deviation(nc, k, s, mv[lag], sd[lag]).then_inc(act, 1)
                norms(u, y, "2", 1, ACT.Identity)
                norms(x, h, "", 0, ACT.Relu)
                for s in range(2):
                    a.wait_ge(pe, M.at(i - 2, "turned", s))
                    nc.scalar.activation(slot(hT, s), pair(k, 2 * s + 1), ACT.Relu).then_inc(act, 1)
                hidden(1, 2, aT)

        @block.tensor
        def _(t):
            t.wait_ge(cleared, 1)
            t.sem_inc(pe, M.per)
            with t.Fori(0, N + LAG) as i:
                for s in range(2):
                    t.wait_ge(act, A.at(i - 3, "hidden1", s))
                    times_cols(nc, aT, s, k.w3[:, 1, :], pair(k, 2 * s + 1)).then_inc(pe, 1)
                for s in range(2):
                    t.wait_ge(act, A.at(i - 3, "hidden2", s))
                    times_cols(nc, hT, s, k.w3[:, 2, :], pair(k, 2 * s + 1)).then_inc(pe, 1)
                for s in range(2):
                    t.wait_ge(act, A.at(i - 3, "hidden3", s))
                    t.wait_ge(vec, V.at(i - 4, "out", s))
                    times_rows_plus(nc, k, aT, s, k.w3[:, 3, :], pair(k, 2 * s)).then_inc(pe, 1)
                for s in range(2):
                    t.wait_ge(vec, V.at(i - 2, "norm3", s))
                    transposed(nc, k, h3, s, pair(k, 2 * s + 1)).then_inc(pe, 1)
                for s in range(2):
                    t.wait_ge(act, A.at(i - 2, "moved", s))
                    times_cols(nc, hT, s, k.w3[:, 0, :], pair(k, 2 * s + 1)).then_inc(pe, 1)


def build(nc, x, src, dst, et4, et8, w, out, upto=99):
    with ExitStack() as ctx:
        k = Shared()
        k.x, k.src, k.dst, k.et4, k.et8, k.w, k.out = x, src, dst, et4, et8, w, out

        def dram(name, shape, dt=F32):
            return nc.dram_tensor(name, shape, dt, kind="Internal").ap()

        def sb(name, shape, dt=F32):
            return ctx.enter_context(nc.sbuf_tensor(name, shape, dt))

        k.slot_table, k.pair_table = dram("slot_table", (P * HI, 1), I32), dram("pair_table", (P * HI, 2))
        k.dst_rows, k.sorted_edges = dram("dst_rows", (P, T)), dram("sorted_edges", (EDGES, 4), I32)
        k.relT4, k.relT8 = dram("relT4", (T, P)), dram("relT8", (T, P))
        for_rows = (EPAD + P, D)
        k.T1, k.T2, k.V2, k.V3, k.V4 = (dram(n, for_rows) for n in ("T1", "T2", "V2", "V3", "V4"))
        k.V0, k.V1, k.V5, k.XS, k.XD, k.HS, k.HD, k.MSG = (
            dram(n, (EPAD, D)) for n in ("V0", "V1", "V5", "XS", "XD", "HS", "HD", "MSG"))

        k.dstf = sb("dstf", [P, T + 2])
        for_edges = [P, T]
        k.lo, k.hi, k.cont, k.end, k.real_end, k.more, k.fix, k.rel4, k.rel8, k.norm_out, k.norm_in = (
            sb(n, for_edges) for n in ("lo", "hi", "cont", "end", "real_end", "more", "fix", "rel4", "rel8", "norm_out", "norm_in"))
        k.src_i, k.dst_i, k.src_tab, k.slot_at, k.out_i, k.pos_i, k.slot_i = (
            sb(n, for_edges, I32) for n in ("src_i", "dst_i", "src_tab", "slot_at", "out_i", "pos_i", "slot_i"))
        k.fix_i = sb("fix_i", [P, 1], I32)
        k.dst_list, k.src_list, k.rel_list = sb("dst_list", [P, T + 2], I32), sb("src_list", [P, T], I32), sb("rel_list", [P, 2, T], I32)
        k.ident, k.into, k.intoT, k.back = (sb(n, [P, P]) for n in ("ident", "into", "intoT", "back"))
        k.tail, k.bn_a, k.bn_b, k.plain = (sb(n, [P, D]) for n in ("tail", "bn_a", "bn_b", "plain"))
        k.small = sb("small", [P, 36, T])
        k.sl, k.sr, k.es, k.ed = k.small[:, 0:8, :], k.small[:, 8:16, :], k.small[:, 16:20, :], k.small[:, 20:36, :]
        k.zeros, k.ones, k.eps, k.p_col = sb("zeros", [P, D]), sb("ones", [P, P]), sb("eps", [P, 1]), sb("p_col", [P, 1])
        k.hi_row = sb("hi_row", [P, HI], FP16)
        k.w0, k.w3 = sb("w0", [P, 2, D]), sb("w3", [P, 4, D])
        k.wf, k.w2 = sb("wf", [P, 4, D + H8]), sb("w2", [P, R4, D + H4])
        k.vdst, k.q2, k.rel_of = sb("vdst", [P, R4 * H4]), sb("q2", [P, P]), sb("rel_of", [P, 4])
        k.b3, k.gb, k.b3_row = sb("b3", [P, 3]), sb("gb", [P, 2]), sb("b3_row", [P, 2, D])
        k.b1_0, k.b2_0, k.attn_r, k.bias2, k.ln_g, k.ln_b = (sb(n, [P, D]) for n in ("b1_0", "b2_0", "attn_r", "bias2", "ln_g", "ln_b"))
        k.hm8, k.hm4, k.al, k.a4 = sb("hm8", [P, H8]), sb("hm4", [P, H4]), sb("al", [P, H8]), sb("a4", [P, 2, R4, H4])
        k.b2b = k.b3_row[:, 1, :]
        k.psum = ctx.enter_context(nc.psum_tensor("psum", [P, 4096], F32))
        k.setup_rows = SQUARES + 5
        k.gpsimd_sems = {n: [ctx.enter_context(nc.semaphore(f"{n}{s}")) for s in range(2)]
                         for n in ("gathered", "scattered", "fetched")}
        k.placed = ctx.enter_context(nc.semaphore("placed"))
        k.passed = ctx.enter_context(nc.semaphore("passed"))
        k.raised = dict.fromkeys(k.gpsimd_sems, 0)
        phases = [lambda nc, k: (order_edges(nc, k), setup(nc, k)), out_degrees, lookups,
                  conv1_edges, lambda nc, k: join_partitions(nc, k, k.V0, "j0"), conv1_nodes,
                  conv2_edges, lambda nc, k: join_partitions(nc, k, k.V1, "j1"), conv2_nodes,
                  lambda nc, k: relational_edges(nc, k, "r1", None, k.T2, None, True, 4, D + H8, k.wf, k.sl),
                  weigh_heads1,
                  lambda nc, k: weighted_edges(nc, k, "w1", H8, k.sl, k.V2),
                  lambda nc, k: join_partitions(nc, k, k.V2, "j2"),
                  batch_stats,
                  layer2_nodes,
                  lambda nc, k: relational_edges(nc, k, "r2", None, k.V2, None, False, 4, D + H4, k.w2, k.es),
                  weigh_edges2,
                  lambda nc, k: weighted_edges(nc, k, "w2", H4, k.es, k.V3),
                  lambda nc, k: join_partitions(nc, k, k.V3, "j3"),
                  lambda nc, k: layer3_inputs(nc, k, "n3", False),
                  lambda nc, k: layer3_inputs(nc, k, "e3", True),
                  lambda nc, k: join_partitions(nc, k, k.V4, "j4"),
                  lambda nc, k: graph_mlp(nc, k, "m1n", False, 0),
                  lambda nc, k: graph_mlp(nc, k, "m1e", True, 0),
                  lambda nc, k: join_partitions(nc, k, k.V5, "j5"),
                  all_nodes,
                  lambda nc, k: graph_mlp(nc, k, "m2n", False, 1)]
        for n, phase in enumerate(phases):
            if (n <= upto if isinstance(upto, int) else n in upto):
                phase(nc, k)


def kernel(**inputs):
    import numpy as np
    import concourse.bacc as bacc
    from concourse.bass_utils import run_bass_kernel_spmd

    nc = bacc.Bacc("TRN2", target_bir_lowering=False, num_devices=1)
    arrays = {name: np.ascontiguousarray(a) for name, a in inputs.items()}
    aps = {name: nc.dram_tensor(name, a.shape, mybir.dt.from_np(a.dtype), kind="ExternalInput").ap() for name, a in arrays.items()}
    out = nc.dram_tensor("out", (NODES, D), F32, kind="ExternalOutput").ap()
    build(nc, aps["x"], aps["src"], aps["dst"], aps["edge_type_4"], aps["edge_type_8"], aps, out)
    r = run_bass_kernel_spmd(nc, [arrays], core_ids=[0])
    return r.results[0]["out"]
```

```python
import concourse.bass as bass
from concourse import mybir
from contextlib import ExitStack

F32 = mybir.dt.float32
BF16 = mybir.dt.bfloat16
FP16 = mybir.dt.float16
I32 = mybir.dt.int32
ALU = mybir.AluOpType
ACT = mybir.ActivationFunctionType
AX = mybir.AxisListType

P = 128
D = 128
NODES = 100000
EDGES = 25000
T = 196
EPAD = P * T
REAL_LAST = EDGES - (P - 1) * T
G = 7
W = G * D
NI = T // (2 * G)
HI = 784
PAD_NODE = 2**24 - 1
SKIP = 1 << 20
NONE = EPAD
AHEAD = 1
EPS = 1e-5
R8, H8 = 8, 8
R4, H4 = 4, 4
SLOPE = 0.2


class Shared:
    pass


class Steps:

    def __init__(self, *names, lag=None):
        self.order, self.lag = [], lag or {}
        for n in names:
            self.order += [n] if isinstance(n, tuple) else [(n, 0), (n, 1)]
        self.per = len(self.order)

    def at(self, i, name, s=0):
        lag = self.lag.get((name, s), self.lag.get(name, 0))
        return (i + (1 + lag)) * self.per + (self.order.index((name, s)) + 1)

    def absent(self, eng, sem, i, name, count, s=0):
        eng.wait_ge(sem, (i + 1) * self.per + self.order.index((name, s)))
        eng.sem_inc(sem, count)

    def last(self, n=NI):
        return (n + 1) * self.per


def slotwise(*names):
    return [(n, s) for s in range(2) for n in names]


SUMS = tuple(f"sum{c}" for c in range(G))


def place(s, k=0):
    return s * W + k * D


def slot(buf, s):
    return buf[:, s * W:(s + 1) * W]


def tile(buf, s, k):
    return buf[:, s * W + k * D:s * W + (k + 1) * D]


def by_tile(ap):
    return ap.rearrange("p (k f) -> p k f", f=D)


def every(row, count=G):
    return row.unsqueeze(1).to_broadcast([P, count, D])


def cols(arr, i, s, k=0, n=1):
    return arr[:, bass.ds(i * (2 * G) + (s * G + k), n)]


def part(table, i, s):
    return table[0:EPAD, :].rearrange("(p t) f -> p (t f)", p=P)[:, bass.ds(i * (2 * W) + s * W, W)]



def stats(nc, x, s, st):
    for k in range(G):
        last = nc.vector.bn_stats(st[:, s, k, :], tile(x, s, k))
    return last


def aggregate(nc, s, st, mv):
    for c in range(G):
        last = nc.vector.bn_aggr(mv[:, s, c, :], st[:, s, c, :])
    return last


def deviation(nc, k, s, mv, sd):
    return nc.scalar.activation(sd[:, s, :], mv[:, s, :, 1], ACT.Sqrt, bias=k.eps[:, 0:1])


def normalise(nc, x, s, mv, rs, out):
    for k in range(G):
        last = nc.vector.tensor_scalar(tile(out, s, k), tile(x, s, k), mv[:, s, k, 0:1], rs[:, s, k:k + 1],
                                       ALU.subtract, ALU.mult)
    return last


def shift(nc, s, mv, rs, nb):
    return nc.vector.scalar_tensor_tensor(nb[:, s, :], mv[:, s, :, 0], -1.0, rs[:, s, :], ALU.mult, ALU.mult)


def scaled_rows(nc, x, s, rs, nb, out, func):
    for k in range(G):
        last = nc.scalar.activation(tile(out, s, k), tile(x, s, k), func, scale=rs[:, s, k:k + 1], bias=nb[:, s, k:k + 1])
    return last


def transposed(nc, k, x, s, psum):
    for c in range(G):
        last = nc.tensor.transpose(psum[:, c * D:(c + 1) * D], tile(x, s, c), k.ident[:, :])
    return last


def times_rows(nc, xT, s, w, psum):
    for c in range(G):
        last = nc.tensor.matmul(psum[:, c * D:(c + 1) * D], tile(xT, s, c), w, start=True, stop=True)
    return last


def times_rows_plus(nc, k, xT, s, w, psum):
    bias = k.b2b[0:1, :].unsqueeze(1)
    nc.tensor.matmul(psum[:, 0:512], k.ones[0:1, :], bias.to_broadcast([1, 4, D]), start=True, stop=False, skip_group_check=True)
    nc.tensor.matmul(psum[:, 512:W], k.ones[0:1, :], bias.to_broadcast([1, G - 4, D]), start=True, stop=False, skip_group_check=True)
    for c in range(G):
        last = nc.tensor.matmul(psum[:, c * D:(c + 1) * D], tile(xT, s, c), w, start=False, stop=True, skip_group_check=True)
    return last


def times_cols(nc, xT, s, w, psum):
    v = slot(xT, s)
    nc.tensor.matmul(psum[:, 0:512], w, v[:, 0:512], start=True, stop=True)
    return nc.tensor.matmul(psum[:, 512:W], w, v[:, 512:W], start=True, stop=True)


class Phase:

    def __init__(self, nc, k, name):
        self.nc, self.k, self.name = nc, k, name

    def __enter__(self):
        self.ctx = ExitStack()
        self.ctx.__enter__()
        self.sems = []
        return self

    def sb(self, name, shape, dt=F32):
        return self.ctx.enter_context(self.nc.sbuf_tensor(f"{self.name}_{name}", shape, dt))

    def ring(self, name):
        return self.sb(name, [P, 2 * W])

    def sem(self, name):
        s = self.ctx.enter_context(self.nc.semaphore(f"{self.name}_{name}"))
        self.sems.append(s)
        return s

    def sem2(self, name):
        return [self.sem(f"{name}{s}") for s in range(2)]

    def moves(self, name, raised):
        base = self.k.raised[name]
        self.k.raised[name] += raised
        return self.k.gpsimd_sems[name], base

    def block(self):
        self.open = self.nc.Block()
        return self.open.__enter__()

    def __exit__(self, *a):
        if a[0] is None:
            self.open.__exit__(None, None, None)
            for s in self.sems:
                self.nc.gpsimd.sem_clear(s)
            self.nc.all_engine_barrier()
        return self.ctx.__exit__(*a)


def order_edges(nc, k):
    BLOCK = T // 4
    with Phase(nc, k, "order") as ph:
        filled, loaded, edge_cols, v, pe, ranked = (
            ph.sem(n) for n in ("filled", "loaded", "edge_cols", "vector_done", "tensor_done", "ranked"))
        row_loaded, row_used, listed, iotas, staged, back = (
            ph.sem(n) for n in ("row_loaded", "row_used", "list_stored", "iotas", "staged", "sorted_back"))
        placed = k.placed
        dst_i, src_t, rel_i = k.dst_list, k.src_list, k.rel_list
        dstf = ph.sb("dstf", [P, T + 2])
        wrong, wrong_sum = ph.sb("wrong", [P, T]), ph.sb("wrong_sum", [P, 1])
        ones = ph.sb("ones", [P, 1])
        flag = ph.sb("flag", [1, 1], I32)
        cols_of, half = ph.sb("cols_of", [P, T]), ph.sb("half", [P, P])
        p_col = ph.sb("p_col", [P, 1])
        row, mine = ph.sb("row", [P, T]), ph.sb("mine", [P, T])
        smaller = ph.sb("smaller", [P, BLOCK, T])
        found = ph.sb("found", [P, BLOCK])
        rank, rank_i = ph.sb("rank", [P, T]), ph.sb("rank_i", [P, T], I32)
        record = ph.sb("record", [P, T, 4], I32)
        at, what = ph.sb("at", [P, 2 * G], I32), ph.sb("what", [P, 2 * G, 4], I32)
        head = (P - 1) * T
        block = ph.block()

        def edge_columns(sp, dst):
            with nc.allow_non_contiguous_dma(reason="two columns of the edge list"):
                sp.dma_start(dst_i[1:P, 0:1], dst[0:head].rearrange("(p t) -> p t", t=T)[:, T - 1:T]).then_inc(edge_cols, 16)
                sp.dma_start(dst_i[0:P - 2, T + 1:T + 2], dst[T:head].rearrange("(p t) -> p t", t=T)[:, 0:1]).then_inc(edge_cols, 16)
                sp.dma_start(dst_i[P - 2:P - 1, T + 1:T + 2], dst[head:head + 1].rearrange("(a t) -> a t", a=1)).then_inc(edge_cols, 16)

        def unsorted(eng):
            eng.wait_ge(v, FLAG)
            return eng.value_load(flag[0:1, 0:1], min_val=0, max_val=EPAD)

        @block.sync
        def _(sp):
            sp.wait_ge(filled, 1)
            for to, one in ((dst_i[:, 1:T + 1], k.dst), (src_t[:, :], k.src), (rel_i[:, 0, :], k.et4), (rel_i[:, 1, :], k.et8)):
                sp.dma_start(to[0:P - 1, :], one[0:head].rearrange("(p t) -> p t", t=T)).then_inc(loaded, 16)
                sp.dma_start(to[P - 1:P, 0:REAL_LAST], one[head:EDGES].rearrange("(a t) -> a t", a=1)).then_inc(loaded, 16)
            edge_columns(sp, k.dst)
            with sp.If(unsorted(sp) > 0):
                sp.dma_start(k.dst_rows, dstf[:, 1:T + 1]).then_inc(listed, 16)
                sp.wait_ge(listed, 16)
                sp.sem_inc(row_used, 1)
                with sp.Fori(0, P) as q:
                    sp.wait_ge(row_used, q + 1)
                    sp.dma_start(row[:, :], k.dst_rows[bass.ds(q, 1), :].to_broadcast([P, T])).then_inc(row_loaded, 16)
                sp.wait_ge(ranked, 2)
                places = k.sorted_edges.rearrange("n c -> (n c)")
                sp.dma_start(record[0:P - 1, :, :], places[0:head * 4].rearrange("(p t c) -> p t c", t=T, c=4)).then_inc(back, 16)
                sp.dma_start(record[P - 1:P, 0:REAL_LAST, :], places[head * 4:EDGES * 4].rearrange("(a t c) -> a t c", a=1, c=4)).then_inc(back, 16)
                edge_columns(sp, k.sorted_edges[:, 0:1].rearrange("n c -> (n c)"))
                sp.wait_ge(edge_cols, 96)

        @block.gpsimd
        def _(g):
            g.memset(dst_i[:, 0:1], -1)
            g.memset(dst_i[:, 1:T + 1], PAD_NODE)
            g.memset(dst_i[:, T + 1:T + 2], -1)
            g.memset(src_t[:, :], 0)
            g.memset(rel_i[:, :, :], 0).then_inc(filled, 1)
            g.iota(cols_of[:, :], pattern=[[1, T]], base=0, channel_multiplier=0, allow_small_or_imprecise_dtypes=True)
            g.iota(p_col[:, :], pattern=[[0, 1]], base=0, channel_multiplier=1, allow_small_or_imprecise_dtypes=True).then_inc(iotas, 1)
            with g.If(unsorted(g) > 0):
                g.wait_ge(ranked, 1)
                with g.Fori(0, NI) as i:
                    c = bass.ds(i * (2 * G), 2 * G)
                    g.tensor_copy(at[:, :], rank_i[:, c]).then_inc(staged, 1)
                    g.tensor_copy(what[:, :, :], record[:, c, :]).then_inc(staged, 1)
                    wait_apart(g, k, staged, i * 2 + 2)
                    for n in range(2 * G):
                        g.indirect_dma_start(k.sorted_edges, bass.IndirectOffsetOnAxis(ap=at[:, n:n + 1], axis=0),
                                             what[:, n, :], None, bounds_check=EDGES - 1, oob_is_err=False).then_inc(placed, 16)
                    wait_apart(g, k, placed, i * (2 * G * 16) + 2 * G * 16)
                g.sem_inc(ranked, 1)

        @block.vector
        def _(d):
            n = [0]

            def chain(ins):
                n[0] += 1
                ins.then_inc(v, 1)
                d.wait_ge(v, n[0])
            d.wait_ge(loaded, 16 * 8)
            d.wait_ge(edge_cols, 48)
            chain(d.memset(ones[:, :], 1.0))
            chain(d.tensor_copy(dstf[:, :], dst_i[:, :]))
            chain(d.tensor_tensor(wrong[:, :], dstf[:, 1:T + 1], dstf[:, 2:T + 2], ALU.is_gt))
            chain(d.tensor_scalar(mine[:, :], dstf[:, 1:T + 1], float(NODES), None, ALU.is_lt))
            chain(d.tensor_tensor(wrong[:, :], wrong[:, :], mine[:, :], ALU.mult))
            chain(d.tensor_reduce(wrong_sum[:, :], wrong[:, :], AX.X, ALU.add))
            assert n[0] == FLAG - 1
            d.wait_ge(pe, 1)
            chain(d.tensor_copy(flag[:, :], k.psum[0:1, 0:1]))
            with d.If(unsorted(d) > 0):
                d.wait_ge(iotas, 1)
                for c, one in enumerate((dst_i[:, 1:T + 1], src_t[:, :], rel_i[:, 0, :], rel_i[:, 1, :])):
                    chain(d.tensor_copy(record[:, :, c], one))
                chain(d.tensor_scalar(half[:, :], cols_of[:, 0:P], p_col[:, 0:1], 0.5, ALU.is_lt, ALU.mult))
                base = n[0]
                with d.Fori(0, T) as t:
                    d.tensor_scalar(mine[:, :], cols_of[:, :], cols_of[:, bass.ds(t, 1)], None, ALU.is_lt).then_inc(v, 1)
                    wait_apart(d, k, v, t * 3 + (base + 1))
                    d.scalar_tensor_tensor(wrong[:, :], dstf[:, 1:T + 1], dstf[:, bass.ds(t + 1, 1)], mine[:, :],
                                           ALU.is_equal, ALU.mult).then_inc(v, 1)
                    wait_apart(d, k, v, t * 3 + (base + 2))
                    d.tensor_reduce(rank[:, bass.ds(t, 1)], wrong[:, :], AX.X, ALU.add).then_inc(v, 1)
                    wait_apart(d, k, v, t * 3 + (base + 3))
                base += 3 * T
                steps = 1 + 3 * 4
                with d.Fori(0, P) as q:
                    done = [0]

                    def next_step(ins):
                        done[0] += 1
                        ins.then_inc(v, 1)
                        wait_apart(d, k, v, q * steps + (base + done[0]))
                    wait_apart(d, k, row_loaded, q * 16 + 16)
                    next_step(d.tensor_scalar(mine[:, :], row[:, :], half[:, bass.ds(q, 1)], None, ALU.subtract))
                    d.sem_inc(row_used, 1)
                    for b in range(4):
                        own = slice(b * BLOCK, (b + 1) * BLOCK)
                        next_step(d.tensor_tensor(smaller[:, :, :], mine[:, :].unsqueeze(1).to_broadcast([P, BLOCK, T]),
                                                  dstf[:, 1 + own.start:1 + own.stop].unsqueeze(2).to_broadcast([P, BLOCK, T]), ALU.is_lt))
                        next_step(d.tensor_reduce(found[:, :], smaller[:, :, :], AX.X, ALU.add))
                        next_step(d.tensor_tensor(rank[:, own], rank[:, own], found[:, :], ALU.add))
                n[0] = base + P * steps
                chain(d.tensor_scalar(mine[:, :], dstf[:, 1:T + 1], float(NODES), float(SKIP), ALU.is_ge, ALU.mult))
                chain(d.tensor_tensor(rank[:, :], rank[:, :], mine[:, :], ALU.add))
                chain(d.tensor_copy(rank_i[:, :], rank[:, :]))
                d.sem_inc(ranked, 1)
                d.wait_ge(back, 32)
                last = slice(0, REAL_LAST)
                for c, one in enumerate((dst_i[:, 1:T + 1], src_t[:, :], rel_i[:, 0, :], rel_i[:, 1, :])):
                    chain(d.tensor_copy(one, record[:, :, c]))

        @block.tensor
        def _(t):
            t.wait_ge(v, FLAG - 1)
            nc.tensor.matmul(k.psum[0:1, 0:1], wrong_sum[:, :], ones[:, :], start=True, stop=True).then_inc(pe, 1)


FLAG = 7


def setup(nc, k):
    with Phase(nc, k, "setup") as ph:
        consts, v, weights = (ph.sem(n) for n in ("consts", "vector_done", "weights_loaded"))
        pe_done, act_done, stored = ph.sem("tensor_done"), ph.sem("scalar_done"), ph.sem("stored")
        dst_i, src_t, rel_i = k.dst_list, k.src_list, k.rel_list
        tmp_i = ph.sb("tmp_i", [P, T], I32)
        tmp = ph.sb("tmp", [P, T])
        tmp2 = ph.sb("tmp2", [P, T])
        pos = ph.sb("pos", [P, T])
        sq = ph.sb("sq", [P, 4, P])
        hasfix = ph.sb("hasfix", [P, 2])
        upper = ph.sb("upper", [P, P])
        lower = ph.sb("lower", [P, P])
        relT = ph.sb("relT", [98, 4, P])
        row = ph.sb("row", [P, 8, D])
        none_rows = ph.sb("none_rows", [P, D])
        wv = ph.sb("wv", [P, 2, R4, D])
        wT = ph.sb("wT", [P, R4, D])
        att = ph.sb("att", [P, 2, R4, H4])
        wfT = ph.sb("wfT", [P, 4, D])
        attl = ph.sb("attl", [P, H8])
        compb = ph.sb("compb", [P, 32])
        jdx = ph.sb("jdx", [P, 2, 128])
        qm = ph.sb("qm", [P, 3, 64])
        big_none = ph.sb("big_none", [P, HI], I32)
        block = ph.block()
        PS = k.psum

        @block.sync
        def _(sp):
            sp.wait_ge(v, 5)
            sp.dma_start(k.slot_table.rearrange("(p j) a -> p (j a)", p=P), big_none[:, :]).then_inc(stored, 16)
            sp.wait_ge(act_done, 1)
            for h in range(2):
                sp.dma_start(k.relT8[98 * h:98 * h + 98, :], relT[:, h, :]).then_inc(stored, 16)
                sp.dma_start(k.relT4[98 * h:98 * h + 98, :], relT[:, 2 + h, :]).then_inc(stored, 16)
            sp.wait_ge(v, k.setup_rows)
            sp.dma_start(k.T1[EPAD:EPAD + P, :], none_rows[:, :]).then_inc(stored, 16)
            sp.dma_start(k.T2[EPAD:EPAD + P, :], k.b2_0[:, :]).then_inc(stored, 16)
            for t in (k.V2, k.V3, k.V4):
                sp.dma_start(t[EPAD:EPAD + P, :], k.zeros[:, 0:D]).then_inc(stored, 16)
            sp.wait_ge(stored, 16 * 10)

        @block.gpsimd
        def _(g):
            g.memset(k.ident[:, :], 0.0)
            g.memset(upper[:, :], 1.0)
            g.memset(lower[:, :], 1.0)
            g.memset(k.zeros[:, :], 0.0)
            g.memset(k.ones[:, :], 1.0)
            g.memset(k.eps[:, :], EPS)
            g.memset(qm[:, 0, :], 0.0)
            g.iota(tmp_i[:, :], pattern=[[1, T]], base=0, channel_multiplier=T)
            g.iota(k.hi_row[:, :], pattern=[[1, HI]], base=0, channel_multiplier=0, allow_small_or_imprecise_dtypes=True)
            g.iota(k.p_col[:, :], pattern=[[0, 1]], base=0, channel_multiplier=1, allow_small_or_imprecise_dtypes=True)\
                .then_inc(consts, 4)
            g.wait_ge(consts, 4)
            g.affine_select(out=k.ident[:, :], in_=k.ident[:, :], compare_op=ALU.not_equal, fill=1.0,
                            base=0, pattern=[[-1, P]], channel_multiplier=1)
            g.affine_select(out=upper[:, :], in_=upper[:, :], compare_op=ALU.is_gt, fill=0.0,
                            base=0, pattern=[[1, P]], channel_multiplier=-1)
            g.affine_select(out=lower[:, :], in_=lower[:, :], compare_op=ALU.is_gt, fill=0.0,
                            base=0, pattern=[[-1, P]], channel_multiplier=1)
            g.memset(qm[:, 1, :], 1.0).then_inc(consts, 1)
            g.wait_ge(consts, 5)
            q3 = qm[:, 1, :].rearrange("p (j b) -> p j b", b=4)
            g.affine_select(out=q3, in_=q3, compare_op=ALU.is_ge, fill=0.0,
                            base=0, pattern=[[-8, 16], [0, 4]], channel_multiplier=1).then_inc(consts, 1)
            g.wait_ge(consts, 6)
            g.affine_select(out=q3, in_=q3, compare_op=ALU.is_ge, fill=0.0,
                            base=7, pattern=[[8, 16], [0, 4]], channel_multiplier=-1).then_inc(consts, 1)

        @block.scalar
        def _(a):
            def rows(dst, src):
                a.dma_start(dst, src).then_inc(weights, 16)
            bc = lambda ap: ap.rearrange("(a n) -> a n", a=1).to_broadcast([P, D])
            rows(k.w0[:, 0, :], k.w['L0_gnn_W1'])
            rows(k.w0[:, 1, :], k.w['L0_gnn_W2'])
            rows(k.wf[:, :, 0:D], k.w['L1_gnn_weight'].rearrange("b i o -> (b i) o").rearrange("(c k) o -> k c o", k=P))
            rows(k.w2[:, :, 0:D], k.w['L2_gnn_W'].rearrange("r i o -> i r o"))
            for n, name in enumerate(('L3_gnn_W1a', 'L3_gnn_W1b', 'L3_gnn_W2a', 'L3_gnn_W2b')):
                rows(k.w3[:, n, :], k.w[name])
            with nc.allow_non_contiguous_dma(reason="bias columns and attention vectors"):
                for n, name in enumerate(('L3_gnn_b1a', 'L3_gnn_b1b', 'L3_gnn_b2a')):
                    rows(k.b3[:, n:n + 1], k.w[name].rearrange("(n a) -> n a", a=1))
                rows(k.gb[:, 0:1], k.w['L1_gnn_gamma'].rearrange("(n a) -> n a", a=1))
                rows(k.gb[:, 1:2], k.w['L1_gnn_beta'].rearrange("(n a) -> n a", a=1))
                rows(attl[:, 0:1], k.w['L1_gnn_attn_l'].rearrange("h (d a) -> (h d) a", a=1))
                for m, name in enumerate(('L2_gnn_attn_src', 'L2_gnn_attn_dst')):
                    rows(att[:, m, :, 0:1], k.w[name].rearrange("r h (d a) -> (h d) r a", a=1))
                for n in range(16):
                    rows(compb[8 * n:8 * n + 8, 0:4], k.w['L1_gnn_w_comp'])
            rows(k.b1_0[:, :], bc(k.w['L0_gnn_b1']))
            rows(k.b2_0[:, :], bc(k.w['L0_gnn_b2']))
            rows(k.attn_r[:, :], k.w['L1_gnn_attn_r'].rearrange("h d -> (h d)").rearrange("(a n) -> a n", a=1).to_broadcast([P, D]))
            rows(k.bias2[:, :], bc(k.w['L2_gnn_bias']))
            rows(k.ln_g[:, :], bc(k.w['L2_gnn_ln_gamma']))
            rows(k.ln_b[:, :], bc(k.w['L2_gnn_ln_beta']))
            rows(k.b3_row[:, 0, :], bc(k.w['L3_gnn_b1b']))
            rows(k.b3_row[:, 1, :], bc(k.w['L3_gnn_b2b']))
            a.wait_ge(pe_done, 2)
            a.activation(relT[:, :, :], PS[0:98, 0:4 * P], ACT.Copy).then_inc(act_done, 1)
            a.wait_ge(pe_done, 4)
            a.activation(wfT[:, :, :], PS[:, 2048:2560], ACT.Copy).then_inc(act_done, 1)
            a.activation(wT[:, :, :], PS[:, 2560:3072], ACT.Copy).then_inc(act_done, 1)
            a.wait_ge(pe_done, 6)
            a.activation(k.wf[:, :, D:D + H8], PS[:, 3072:3072 + 32].rearrange("p (c h) -> p c h", h=H8), ACT.Copy).then_inc(act_done, 1)
            pv = PS[:, 3584:3584 + 32].rearrange("p (m r h) -> p m r h", m=2, h=H4)
            a.activation(k.intoT[:, :], PS[:, 768:896], ACT.Copy)
            a.activation(k.w2[:, :, D:D + H4], pv[:, 0, :, :], ACT.Copy)
            a.activation(k.vdst[:, :].rearrange("p (r h) -> p r h", h=H4), pv[:, 1, :, :], ACT.Copy).then_inc(act_done, 1)

        @block.vector
        def _(d):
            n = [0]

            def chain(ins):
                n[0] += 1
                ins.then_inc(v, 1)
                d.wait_ge(v, n[0])

            chain(d.tensor_copy(k.dstf[:, :], dst_i[:, :]))
            chain(d.tensor_copy(k.src_i[:, :], src_t[:, :]))
            d.wait_ge(consts, 7)
            chain(d.tensor_copy(pos[:, :], tmp_i[:, :]))
            chain(d.memset(tmp[:, :], float(NONE)))
            chain(d.tensor_copy(big_none[:, :], tmp[:, 0:1].to_broadcast([P, HI])))
            chain(d.tensor_copy(k.rel4[:, :], rel_i[:, 0, :]))
            chain(d.tensor_copy(k.rel8[:, :], rel_i[:, 1, :]))
            chain(d.tensor_scalar(tmp_i[:, :], src_t[:, :], 127, None, ALU.bitwise_and))
            chain(d.tensor_copy(k.lo[:, :], tmp_i[:, :]))
            chain(d.tensor_scalar(tmp_i[:, :], src_t[:, :], 7, None, ALU.arith_shift_right))
            chain(d.tensor_copy(k.hi[:, :], tmp_i[:, :]))
            chain(d.scalar_tensor_tensor(tmp[:, :], k.lo[:, :], float(HI), k.hi[:, :], ALU.mult, ALU.add))
            chain(d.tensor_copy(k.src_tab[:, :], tmp[:, :]))
            chain(d.tensor_scalar(tmp2[:, :], pos[:, :], float(EDGES), 1.0, ALU.is_lt, ALU.mult))
            chain(d.scalar_tensor_tensor(k.lo[:, :], k.lo[:, :], 1.0, tmp2[:, :], ALU.add, ALU.mult))
            chain(d.tensor_scalar(k.lo[:, :], k.lo[:, :], 1.0, None, ALU.subtract))
            chain(d.tensor_tensor(k.cont[:, :], k.dstf[:, 1:T + 1], k.dstf[:, 0:T], ALU.is_equal))
            chain(d.memset(k.cont[:, 0:1], 0.0))
            chain(d.tensor_tensor(k.end[:, :], k.dstf[:, 1:T + 1], k.dstf[:, 2:T + 2], ALU.not_equal))
            chain(d.tensor_tensor(k.real_end[:, :], k.end[:, :], tmp2[:, :], ALU.mult))
            chain(d.tensor_scalar(k.more[:, :], k.end[:, :], -1.0, 1.0, ALU.mult, ALU.add))
            chain(d.tensor_scalar(k.fix[:, :], k.dstf[:, 1:T + 1], k.dstf[:, 1:2], None, ALU.is_equal))
            chain(d.tensor_tensor(k.fix[:, :], k.fix[:, :], k.end[:, :], ALU.mult))
            chain(d.tensor_reduce(hasfix[:, 0:1], k.fix[:, :], AX.X, ALU.add))
            chain(d.tensor_tensor(tmp[:, :], k.fix[:, :], pos[:, :], ALU.mult))
            chain(d.tensor_reduce(hasfix[:, 1:2], tmp[:, :], AX.X, ALU.add))
            chain(d.scalar_tensor_tensor(hasfix[:, 1:2], hasfix[:, 0:1], -float(SKIP), hasfix[:, 1:2], ALU.mult, ALU.add))
            chain(d.tensor_scalar(hasfix[:, 1:2], hasfix[:, 1:2], float(SKIP), None, ALU.add))
            chain(d.tensor_copy(k.fix_i[:, :], hasfix[:, 1:2]))
            chain(d.tensor_copy(tmp_i[:, :], k.dstf[:, 1:T + 1]))
            chain(d.tensor_scalar(tmp[:, :], k.dstf[:, 1:T + 1], -float(SKIP), None, ALU.add))
            chain(d.tensor_tensor(tmp[:, :], tmp[:, :], k.end[:, :], ALU.mult))
            chain(d.tensor_scalar(tmp[:, :], tmp[:, :], float(SKIP), None, ALU.add))
            chain(d.tensor_copy(k.out_i[:, :], tmp[:, :]))
            chain(d.tensor_scalar(rel_i[:, 0, :], tmp_i[:, :], 127, None, ALU.bitwise_and))
            chain(d.tensor_scalar(rel_i[:, 1, :], tmp_i[:, :], 7, None, ALU.arith_shift_right))
            chain(d.tensor_copy(tmp[:, :], rel_i[:, 0, :]))
            chain(d.tensor_copy(tmp2[:, :], rel_i[:, 1, :]))
            chain(d.scalar_tensor_tensor(tmp[:, :], tmp[:, :], float(HI), tmp2[:, :], ALU.mult, ALU.add))
            chain(d.tensor_scalar(tmp[:, :], tmp[:, :], -float(SKIP), None, ALU.add))
            chain(d.tensor_tensor(tmp[:, :], tmp[:, :], k.end[:, :], ALU.mult))
            chain(d.tensor_scalar(tmp[:, :], tmp[:, :], float(SKIP), None, ALU.add))
            chain(d.tensor_copy(k.slot_at[:, :], tmp[:, :]))
            chain(d.tensor_copy(k.pos_i[:, :], pos[:, :]))
            chain(d.tensor_scalar(tmp[:, :], k.dstf[:, 1:T + 1], float(NODES), None, ALU.is_lt))
            chain(d.tensor_tensor(tmp[:, :], tmp[:, :], k.dstf[:, 1:T + 1], ALU.mult))
            chain(d.tensor_copy(k.dst_i[:, :], tmp[:, :]))
            chain(d.tensor_copy(sq[:, 0, :], k.dstf[:, 1:2].to_broadcast([P, P])))
            chain(d.tensor_copy(sq[:, 1, :], k.dstf[:, T:T + 1].to_broadcast([P, P])))
            assert n[0] == SQUARES
            d.wait_ge(pe_done, 1)
            chain(d.tensor_scalar(sq[:, 2, :], PS[:, 512:640], k.dstf[:, T:T + 1], None, ALU.is_equal))
            chain(d.tensor_tensor(k.into[:, :], sq[:, 2, :], upper[:, :], ALU.mult))
            chain(d.tensor_scalar(sq[:, 3, :], PS[:, 640:768], k.dstf[:, 1:2], hasfix[:, 0:1], ALU.is_equal, ALU.mult))
            chain(d.tensor_tensor(k.back[:, :], sq[:, 3, :], lower[:, :], ALU.mult))
            d.wait_ge(weights, 16 * NWEIGHTS)
            chain(d.tensor_scalar(none_rows[:, :], k.b1_0[:, :], 0.0, None, ALU.max))
            assert n[0] == k.setup_rows
            q4 = k.q2[:, :].rearrange("p (c j b) -> p c j b", c=2, b=4)
            m3 = qm[:, 1, :].rearrange("p (j b) -> p j b", b=4)
            cb = compb[:, 0:4].unsqueeze(1).to_broadcast([P, 16, 4])
            chain(d.tensor_tensor(q4[:, 0, :, :], m3, cb, ALU.mult))
            chain(d.tensor_tensor(q4[:, 1, :, :], m3, cb, ALU.mult))
            for c in range(4):
                chain(d.memset(k.rel_of[0:64, c:c + 1], float(2 * c)))
                chain(d.memset(k.rel_of[64:P, c:c + 1], float(2 * c + 1)))
            hm8 = k.hm8[:, :]
            hm4 = k.hm4[:, :]
            chain(d.tensor_reduce(hm8, k.ident[:, :].rearrange("p (h e) -> p h e", h=H8), AX.X, ALU.add))
            chain(d.tensor_reduce(hm4, k.ident[:, :].rearrange("p (h e) -> p h e", h=H4), AX.X, ALU.add))
            chain(d.tensor_scalar(k.al[:, :], hm8, attl[:, 0:1], None, ALU.mult))
            for m in range(2):
                for r in range(R4):
                    chain(d.tensor_scalar(k.a4[:, m, r, :], hm4, att[:, m, r, 0:1], None, ALU.mult))
            assert n[0] == ATTENTION

        @block.tensor
        def _(t):
            t.wait_ge(v, SQUARES)
            nc.tensor.transpose(PS[:, 512:640], sq[:, 0, :], k.ident[:, :])
            nc.tensor.transpose(PS[:, 640:768], sq[:, 1, :], k.ident[:, :]).then_inc(pe_done, 1)
            for h in range(2):
                nc.tensor.transpose(PS[0:98, h * P:(h + 1) * P], k.rel8[:, 98 * h:98 * h + 98], k.ident[:, :])
                last = nc.tensor.transpose(PS[0:98, (h + 2) * P:(h + 3) * P], k.rel4[:, 98 * h:98 * h + 98], k.ident[:, :])
            last.then_inc(pe_done, 1)
            t.wait_ge(weights, 16 * NWEIGHTS)
            for c in range(4):
                last = nc.tensor.transpose(PS[:, 2048 + c * D:2048 + (c + 1) * D], k.wf[:, c, 0:D], k.ident[:, :])
            last.then_inc(pe_done, 1)
            for r in range(R4):
                last = nc.tensor.transpose(PS[:, 2560 + r * D:2560 + (r + 1) * D], k.w2[:, r, 0:D], k.ident[:, :])
            last.then_inc(pe_done, 1)
            t.wait_ge(act_done, 3)
            t.wait_ge(v, ATTENTION)
            for c in range(4):
                last = nc.tensor.matmul(PS[:, 3072 + c * H8:3072 + (c + 1) * H8], wfT[:, c, :], k.al[:, :], start=True, stop=True)
            last.then_inc(pe_done, 1)
            nc.tensor.transpose(PS[:, 768:896], k.into[:, :], k.ident[:, :])
            for m in range(2):
                for r in range(R4):
                    o = 3584 + (m * R4 + r) * H4
                    last = nc.tensor.matmul(PS[:, o:o + H4], wT[:, r, :], k.a4[:, m, r, :], start=True, stop=True)
            last.then_inc(pe_done, 1)


SQUARES = 49
ATTENTION = SQUARES + 5 + 2 + 8 + 3 + 8
NWEIGHTS = 4 + 4 + 3 + 2 + 1 + 2 + 16 + 8


def out_degrees(nc, k):
    S = Steps("hot")
    M = Steps("counted")
    with Phase(nc, k, "deg") as ph:
        vec, pe, staged, done, tab, act = (ph.sem(n) for n in ("vector_steps", "tensor_steps", "staged", "vector_done", "table_moved", "scalar_done"))
        scattered, sbase = ph.moves("scattered", NI * 16 * G)
        lo_hot = ph.sb("lo_hot", [P, 2, G, P], BF16)
        hi_hot = ph.sb("hi_hot", [P, 2, G, HI], BF16)
        at = ph.sb("at", [P, 2 * G], I32)
        what = ph.sb("what", [P, 2 * G], I32)
        deg = ph.sb("deg", [P, HI])
        slots = ph.sb("slots", [P, HI], I32)
        pair = ph.sb("pair", [P, HI, 2])
        zero = ph.sb("zero", [P, 512], BF16)
        block = ph.block()
        PS = k.psum

        @block.gpsimd
        def _(g):
            def scatter(i):
                for s in range(2):
                    if not isinstance(i, int):
                        wait_apart(g, k, scattered[s], i * (16 * G) + sbase)
                    g.tensor_copy(at[:, s * G:(s + 1) * G], cols(k.slot_at, i, s, 0, G)).then_inc(staged, 1)
                    g.tensor_copy(what[:, s * G:(s + 1) * G], cols(k.pos_i, i, s, 0, G)).then_inc(staged, 1)
                    wait_apart(g, k, staged, i * 4 + (2 * s + 2))
                    for c in range(s * G, (s + 1) * G):
                        g.indirect_dma_start(k.slot_table, bass.IndirectOffsetOnAxis(ap=at[:, c:c + 1], axis=0),
                                             what[:, c:c + 1], None, bounds_check=P * HI - 1,
                                             oob_is_err=False).then_inc(scattered[s], 16)
            scatter(0)
            with g.Fori(1, NI) as i:
                scatter(i)

        @block.vector
        def _(d):
            d.memset(zero[:, :], 0.0).then_inc(done, 1)
            d.sem_inc(vec, S.per)
            with d.Fori(0, NI) as i:
                for s in range(2):
                    d.wait_ge(pe, M.at(i - 1, "counted", s))
                    for c in range(G):
                        nc.vector.tensor_scalar(lo_hot[:, s, c, :], k.hi_row[:, 0:P], cols(k.lo, i, s, c), None, ALU.is_equal)
                        last = nc.vector.tensor_scalar(hi_hot[:, s, c, :], k.hi_row[:, :], cols(k.hi, i, s, c), None, ALU.is_equal)
                    last.then_inc(vec, 1)
            d.wait_ge(pe, M.last())
            d.tensor_scalar(deg[:, 0:HI // 2], PS[:, 0:HI // 2], 1.0, None, ALU.max)
            d.tensor_scalar(deg[:, HI // 2:HI], PS[:, 512:512 + HI // 2], 1.0, None, ALU.max).then_inc(done, 1)
            d.wait_ge(act, 1)
            d.reciprocal(pair[:, :, 1], deg[:, :]).then_inc(done, 1)
            d.wait_ge(tab, 16)
            d.tensor_copy(pair[:, :, 0], slots[:, :]).then_inc(done, 1)

        @block.scalar
        def _(a):
            a.wait_ge(done, 2)
            a.activation(deg[:, :], deg[:, :], ACT.Sqrt).then_inc(act, 1)

        @block.tensor
        def _(t):
            t.wait_ge(done, 1)
            nc.tensor.matmul(PS[:, 0:HI // 2], zero[:, 0:P], zero[:, 0:HI // 2], start=True, stop=False, skip_group_check=True)
            nc.tensor.matmul(PS[:, 512:512 + HI // 2], zero[:, 0:P], zero[:, 0:HI // 2], start=True, stop=False, skip_group_check=True)
            t.sem_inc(pe, M.per)
            with t.Fori(0, NI) as i:
                for s in range(2):
                    t.wait_ge(vec, S.at(i, "hot", s))
                    for c in range(G):
                        nc.tensor.matmul(PS[:, 0:HI // 2], lo_hot[:, s, c, :], hi_hot[:, s, c, 0:HI // 2],
                                         start=False, stop=False, skip_group_check=True)
                        last = nc.tensor.matmul(PS[:, 512:512 + HI // 2], lo_hot[:, s, c, :], hi_hot[:, s, c, HI // 2:HI],
                                                start=False, stop=False, skip_group_check=True)
                    last.then_inc(pe, 1)

        @block.sync
        def _(sp):
            for s in range(2):
                sp.wait_ge(scattered[s], NI * 16 * G + sbase)
            sp.dma_start(slots[:, :], k.slot_table.rearrange("(p j) a -> p (j a)", p=P)).then_inc(tab, 16)
            sp.wait_ge(done, 4)
            sp.dma_start(k.pair_table.rearrange("(p j) a -> p (j a)", p=P), pair[:, :, :].rearrange("p j a -> p (j a)")).then_inc(tab, 16)
            sp.wait_ge(tab, 32)


def iterations(eng, body):
    body(0, True, False, False)
    body(1, True, True, False)
    with eng.Fori(2, NI) as i:
        body(i, True, True, True)
    body(NI, False, True, True)
    body(NI + 1, False, False, True)


def start_ahead(eng, *sems):
    for pair_of_slots in sems:
        for sem in pair_of_slots:
            eng.sem_inc(sem, AHEAD)


def wait_apart(eng, k, sem, value):
    eng.wait_ge(sem, value)
    eng.sem_inc(k.passed, 1)


def gather_columns(nc, k, g, i, s, index, ring, staged, table, out, width, gathered):
    g.tensor_copy(ring[:, s * G:(s + 1) * G], cols(index, i, s, 0, G)).then_inc(staged, 1)
    wait_apart(g, k, staged, i * 2 + (s + 3))
    for c in range(G):
        o = (s * G + c) * width
        g.indirect_dma_start(out[:, o:o + width], None, table,
                             bass.IndirectOffsetOnAxis(ap=ring[:, s * G + c:s * G + c + 1], axis=0)).then_inc(gathered[s], 16)


def lookups(nc, k):
    S = Steps("kept")
    with Phase(nc, k, "look") as ph:
        vec, staged, v, pe, act = (ph.sem(n) for n in ("vector_steps", "staged", "vector_done", "tensor_done", "scalar_done"))
        gathered, gbase = ph.moves("gathered", NI * 16 * G)
        ring = ph.sb("ring", [P, 2 * G], I32)
        pairs = ph.sb("pairs", [P, 2 * G * 2])
        slotf = ph.sb("slotf", [P, T])
        none = ph.sb("none", [P, T])
        count = ph.sb("count", [P, T])
        carry = ph.sb("carry", [P, 1])
        block = ph.block()

        @block.gpsimd
        def _(g):
            g.sem_inc(staged, 2)
            with g.Fori(0, NI) as i:
                for s in range(2):
                    wait_apart(g, k, vec, S.at(i - 1, "kept", s))
                    gather_columns(nc, k, g, i, s, k.src_tab, ring, staged, k.pair_table, pairs, 2, gathered)

        @block.vector
        def _(d):
            d.sem_inc(vec, S.per)
            with d.Fori(0, NI) as i:
                for s in range(2):
                    d.wait_ge(gathered[s], i * (16 * G) + (16 * G + gbase))
                    got = pairs[:, s * 2 * G:(s + 1) * 2 * G].rearrange("p (c a) -> p c a", a=2)
                    nc.vector.tensor_copy(cols(slotf, i, s, 0, G), got[:, :, 0])
                    nc.vector.tensor_copy(cols(k.norm_out, i, s, 0, G), got[:, :, 1]).then_inc(vec, 1)
            n = [0]

            def chain(ins):
                n[0] += 1
                ins.then_inc(v, 1)
                d.wait_ge(v, n[0])
            d.wait_ge(vec, S.last())
            chain(d.tensor_scalar(none[:, :], slotf[:, :], float(NONE), k.p_col[:, 0:1], ALU.is_equal, ALU.mult))
            chain(d.tensor_tensor(slotf[:, :], slotf[:, :], none[:, :], ALU.add))
            chain(d.tensor_copy(k.slot_i[:, :], slotf[:, :]))
            chain(d.tensor_tensor_scan(count[:, :], k.cont[:, :], k.ones[:, 0:1].to_broadcast([P, T]), 0.0, ALU.mult, ALU.add))
            d.wait_ge(pe, 1)
            chain(d.tensor_copy(carry[:, :], k.psum[:, 0:1]))
            chain(d.scalar_tensor_tensor(count[:, :], k.fix[:, :], carry[:, 0:1], count[:, :], ALU.mult, ALU.add))
            d.wait_ge(act, 1)
            chain(d.reciprocal(k.norm_in[:, :], count[:, :]))

        @block.tensor
        def _(t):
            t.wait_ge(v, 4)
            nc.tensor.matmul(k.psum[:, 0:1], k.into[:, :], count[:, T - 1:T], start=True, stop=True).then_inc(pe, 1)

        @block.scalar
        def _(a):
            a.wait_ge(v, 6)
            a.activation(count[:, :], count[:, :], ACT.Sqrt).then_inc(act, 1)


def pair(k, j):
    return k.psum[:, j * 1024:j * 1024 + W]


def wide(k, j, c, n):
    o = j * 1024 + (c // 3) * 512 + (c % 3) * n
    return k.psum[:, o:o + n]


def running_sum(nc, k, d, vec, S, i, s, message, sums):
    for c in range(G):
        before = (tile(sums, s, c - 1), i, f"sum{c - 1}", s) if c else \
                 (tile(sums, 1 - s, G - 1), i if s else i - 1, SUMS[-1], 1 - s)
        d.wait_ge(vec, S.at(*before[1:]))
        nc.vector.scalar_tensor_tensor(tile(sums, s, c), before[0], cols(k.cont, i, s, c), tile(message, s, c),
                                       ALU.mult, ALU.add).then_inc(vec, 1)


def join_partitions(nc, k, V, name):
    with Phase(nc, k, name) as ph:
        pe, v, zeroed = (ph.sem(n) for n in ("tensor_done", "vector_done", "zeroed"))
        (fetched, _), fbase = ph.moves("fetched", 32)
        rows = ph.sb("rows", [P, D])
        block = ph.block()

        @block.tensor
        def _(t):
            nc.tensor.matmul(k.psum[:, 0:D], k.into[:, :], k.tail[:, :], start=True, stop=True).then_inc(pe, 1)

        @block.gpsimd
        def _(g):
            g.memset(rows[:, :], 0.0).then_inc(zeroed, 1)
            g.wait_ge(zeroed, 1)
            at = bass.IndirectOffsetOnAxis(ap=k.fix_i[:, 0:1], axis=0)
            g.indirect_dma_start(rows[:, :], None, V, at, bounds_check=EPAD - 1, oob_is_err=False).then_inc(fetched, 16)
            g.wait_ge(v, 1)
            g.indirect_dma_start(V, at, rows[:, :], None, bounds_check=EPAD - 1, oob_is_err=False).then_inc(fetched, 16)
            g.wait_ge(fetched, fbase + 32)

        @block.vector
        def _(d):
            d.wait_ge(fetched, fbase + 16)
            d.wait_ge(pe, 1)
            nc.vector.tensor_tensor(rows[:, :], rows[:, :], k.psum[:, 0:D], ALU.add).then_inc(v, 1)


def conv1_edges(nc, k):
    V = Steps(*slotwise("stats", "aggr", "rs", "rsn", "nb", *SUMS))
    A = Steps(*slotwise("sd", "relu"))
    with Phase(nc, k, "c1e") as ph:
        vec, act, staged, cleared = (ph.sem(n) for n in ("vector_steps", "scalar_steps", "staged", "cleared"))
        gathered, gbase = ph.moves("gathered", NI * 16 * G)
        kept, stored = ph.sem2("kept"), ph.sem2("stored")
        ring = ph.sb("ring", [P, 2 * G], I32)
        x, h, sums = ph.ring("x"), ph.ring("h"), ph.ring("sums")
        st, mv = ph.sb("st", [P, 2, G, 6]), ph.sb("mv", [P, 2, G, 2])
        sd, rs, nb = (ph.sb(n, [P, 2, G]) for n in ("sd", "rs", "nb"))
        block = ph.block()

        @block.gpsimd
        def _(g):
            g.sem_inc(staged, 2)
            with g.Fori(0, NI) as i:
                for s in range(2):
                    wait_apart(g, k, act, A.at(i - 1, "relu", s))
                    wait_apart(g, k, kept[s], i * 16 + AHEAD)
                    gather_columns(nc, k, g, i, s, k.src_i, ring, staged, k.x, x, D, gathered)

        @block.sync
        def _(sp):
            start_ahead(sp, kept, stored)
            with sp.Fori(0, NI) as i:
                for s in range(2):
                    sp.wait_ge(gathered[s], i * (16 * G) + (16 * G + gbase))
                    sp.dma_start(part(k.XS, i, s), slot(x, s)).then_inc(kept[s], 16)
                for s in range(2):
                    sp.wait_ge(vec, V.at(i, SUMS[-1], s))
                    sp.dma_start(part(k.V0, i, s), slot(sums, s)).then_inc(stored[s], 16)
            for s in range(2):
                sp.wait_ge(kept[s], NI * 16 + AHEAD)
                sp.wait_ge(stored[s], NI * 16 + AHEAD)

        @block.vector
        def _(d):
            d.memset(tile(sums, 1, G - 1), 0.0).then_inc(cleared, 1)
            d.wait_ge(cleared, 1)
            d.sem_inc(vec, V.per)
            with d.Fori(0, NI) as i:
                for s in range(2):
                    d.wait_ge(gathered[s], i * (16 * G) + (16 * G + gbase))
                    stats(nc, x, s, st).then_inc(vec, 1)
                    wait_apart(d, k, vec, V.at(i, "stats", s))
                    aggregate(nc, s, st, mv).then_inc(vec, 1)
                    d.wait_ge(act, A.at(i, "sd", s))
                    nc.vector.reciprocal(rs[:, s, :], sd[:, s, :]).then_inc(vec, 1)
                    d.wait_ge(vec, V.at(i, "rs", s))
                    nc.vector.tensor_tensor(rs[:, s, :], rs[:, s, :], cols(k.norm_out, i, s, 0, G), ALU.mult).then_inc(vec, 1)
                    d.wait_ge(vec, V.at(i, "rsn", s))
                    shift(nc, s, mv, rs, nb).then_inc(vec, 1)
                    d.wait_ge(act, A.at(i, "relu", s))
                    d.wait_ge(stored[s], i * 16 + AHEAD)
                    running_sum(nc, k, d, vec, V, i, s, h, sums)
            d.wait_ge(vec, V.last())
            d.tensor_copy(k.tail[:, :], tile(sums, 1, G - 1))

        @block.scalar
        def _(a):
            a.sem_inc(act, A.per)
            with a.Fori(0, NI) as i:
                for s in range(2):
                    a.wait_ge(vec, V.at(i, "aggr", s))
                    deviation(nc, k, s, mv, sd).then_inc(act, 1)
                    a.wait_ge(vec, V.at(i, "nb", s))
                    scaled_rows(nc, x, s, rs, nb, h, ACT.Relu).then_inc(act, 1)


def conv1_nodes(nc, k):
    V = Steps("scaled")
    A = Steps("moved", "relu")
    M = Steps("turned", "product")
    with Phase(nc, k, "c1n") as ph:
        vec, act, pe = (ph.sem(n) for n in ("vector_steps", "scalar_steps", "tensor_steps"))
        loaded, stored = ph.sem2("loaded"), ph.sem2("stored")
        va, vT, y = ph.ring("va"), ph.ring("vT"), ph.ring("y")
        block = ph.block()

        @block.sync
        def _(sp):
            start_ahead(sp, stored)
            def load(i):
                for s in range(2):
                    sp.wait_ge(pe, M.at(i - 1, "turned", s))
                    sp.dma_start(slot(va, s), part(k.V0, i, s)).then_inc(loaded[s], 16)

            def store(i):
                for s in range(2):
                    sp.wait_ge(act, A.at(i, "relu", s))
                    sp.dma_start(part(k.T1, i, s), slot(y, s)).then_inc(stored[s], 16)
            load(0)
            with sp.Fori(1, NI) as i:
                load(i)
                store(i - 1)
            store(NI - 1)
            for s in range(2):
                sp.wait_ge(stored[s], NI * 16 + AHEAD)

        @block.tensor
        def _(t):
            t.sem_inc(pe, M.per)
            with t.Fori(0, NI) as i:
                for s in range(2):
                    t.wait_ge(loaded[s], i * 16 + 16)
                    t.wait_ge(act, A.at(i - 1, "moved", s))
                    transposed(nc, k, va, s, pair(k, 2 * s)).then_inc(pe, 1)
                for s in range(2):
                    t.wait_ge(act, A.at(i, "moved", s))
                    t.wait_ge(vec, V.at(i - 1, "scaled", s))
                    times_rows(nc, vT, s, k.w0[:, 0, :], pair(k, 2 * s + 1)).then_inc(pe, 1)

        @block.scalar
        def _(a):
            a.sem_inc(act, A.per)
            with a.Fori(0, NI) as i:
                for s in range(2):
                    a.wait_ge(pe, M.at(i, "turned", s))
                    nc.scalar.activation(slot(vT, s), pair(k, 2 * s), ACT.Copy).then_inc(act, 1)
                for s in range(2):
                    a.wait_ge(vec, V.at(i, "scaled", s))
                    nc.scalar.activation(slot(y, s), slot(y, s), ACT.Relu).then_inc(act, 1)

        @block.vector
        def _(d):
            d.sem_inc(vec, V.per)
            with d.Fori(0, NI) as i:
                for s in range(2):
                    d.wait_ge(pe, M.at(i, "product", s))
                    d.wait_ge(stored[s], i * 16 + AHEAD)
                    for c in range(G):
                        o = pair(k, 2 * s + 1)[:, c * D:(c + 1) * D]
                        last = nc.vector.scalar_tensor_tensor(tile(y, s, c), o, cols(k.norm_in, i, s, c),
                                                              k.b1_0[:, :], ALU.mult, ALU.add)
                    last.then_inc(vec, 1)


def conv2_edges(nc, k):
    V = Steps(*slotwise(*SUMS))
    A = Steps("scaled")
    with Phase(nc, k, "c2e") as ph:
        vec, act, staged, cleared = (ph.sem(n) for n in ("vector_steps", "scalar_steps", "staged", "cleared"))
        gathered, gbase = ph.moves("gathered", NI * 16 * G)
        stored = ph.sem2("stored")
        ring = ph.sb("ring", [P, 2 * G], I32)
        y, m, sums = ph.ring("y"), ph.ring("m"), ph.ring("sums")
        block = ph.block()

        @block.gpsimd
        def _(g):
            g.sem_inc(staged, 2)
            with g.Fori(0, NI) as i:
                for s in range(2):
                    wait_apart(g, k, act, A.at(i - 1, "scaled", s))
                    gather_columns(nc, k, g, i, s, k.slot_i, ring, staged, k.T1, y, D, gathered)

        @block.scalar
        def _(a):
            a.sem_inc(act, A.per)
            with a.Fori(0, NI) as i:
                for s in range(2):
                    a.wait_ge(gathered[s], i * (16 * G) + (16 * G + gbase))
                    a.wait_ge(vec, V.at(i - 1, SUMS[-1], s))
                    for c in range(G):
                        last = nc.scalar.activation(tile(m, s, c), tile(y, s, c), ACT.Copy, scale=cols(k.norm_out, i, s, c))
                    last.then_inc(act, 1)

        @block.vector
        def _(d):
            d.memset(tile(sums, 1, G - 1), 0.0).then_inc(cleared, 1)
            d.wait_ge(cleared, 1)
            d.sem_inc(vec, V.per)
            with d.Fori(0, NI) as i:
                for s in range(2):
                    d.wait_ge(act, A.at(i, "scaled", s))
                    d.wait_ge(stored[s], i * 16 + AHEAD)
                    running_sum(nc, k, d, vec, V, i, s, m, sums)
            d.wait_ge(vec, V.last())
            d.tensor_copy(k.tail[:, :], tile(sums, 1, G - 1))

        @block.sync
        def _(sp):
            start_ahead(sp, stored)
            with sp.Fori(0, NI) as i:
                for s in range(2):
                    sp.wait_ge(vec, V.at(i, SUMS[-1], s))
                    sp.dma_start(part(k.V1, i, s), slot(sums, s)).then_inc(stored[s], 16)
            for s in range(2):
                sp.wait_ge(stored[s], NI * 16 + AHEAD)


def conv2_nodes(nc, k):
    V = Steps("out", "x1", "stats", "aggr", "rs", "norm", "weighted", "score")
    A = Steps("moved", "sd", "relu")
    M = Steps("turned", "product")
    with Phase(nc, k, "c2n") as ph:
        vec, act, pe, staged = (ph.sem(n) for n in ("vector_steps", "scalar_steps", "tensor_steps", "staged"))
        gathered, gbase = ph.moves("gathered", NI * 16 * G)
        loaded, stored = ph.sem2("loaded"), ph.sem2("stored")
        ring = ph.sb("ring", [P, 2 * G], I32)
        va, vT, y, x, x1, h, hw = (ph.ring(n) for n in ("va", "vT", "y", "x", "x1", "h", "hw"))
        st, mv = ph.sb("st", [P, 2, G, 6]), ph.sb("mv", [P, 2, G, 2])
        sd, rs = ph.sb("sd", [P, 2, G]), ph.sb("rs", [P, 2, G])
        block = ph.block()

        @block.gpsimd
        def _(g):
            g.sem_inc(staged, 2)
            with g.Fori(0, NI) as i:
                for s in range(2):
                    wait_apart(g, k, vec, V.at(i - 1, "x1", s))
                    gather_columns(nc, k, g, i, s, k.dst_i, ring, staged, k.x, x, D, gathered)

        @block.sync
        def _(sp):
            start_ahead(sp, stored)
            def load(i):
                for s in range(2):
                    sp.wait_ge(pe, M.at(i - 1, "turned", s))
                    sp.dma_start(slot(va, s), part(k.V1, i, s)).then_inc(loaded[s], 16)

            def store(i):
                for s in range(2):
                    sp.wait_ge(vec, V.at(i, "x1", s))
                    sp.dma_start(part(k.T2, i, s), slot(y, s)).then_inc(stored[s], 16)
                    sp.dma_start(part(k.XD, i, s), slot(x1, s)).then_inc(stored[s], 16)
            load(0)
            with sp.Fori(1, NI) as i:
                load(i)
                store(i - 1)
            store(NI - 1)
            for s in range(2):
                sp.wait_ge(stored[s], NI * 32 + AHEAD)

        @block.tensor
        def _(t):
            t.sem_inc(pe, M.per)
            with t.Fori(0, NI) as i:
                for s in range(2):
                    t.wait_ge(loaded[s], i * 16 + 16)
                    t.wait_ge(act, A.at(i - 1, "moved", s))
                    transposed(nc, k, va, s, pair(k, 2 * s)).then_inc(pe, 1)
                for s in range(2):
                    t.wait_ge(act, A.at(i, "moved", s))
                    t.wait_ge(vec, V.at(i - 1, "out", s))
                    times_rows(nc, vT, s, k.w0[:, 1, :], pair(k, 2 * s + 1)).then_inc(pe, 1)

        @block.scalar
        def _(a):
            a.sem_inc(act, A.per)
            with a.Fori(0, NI) as i:
                for s in range(2):
                    a.wait_ge(pe, M.at(i, "turned", s))
                    nc.scalar.activation(slot(vT, s), pair(k, 2 * s), ACT.Copy).then_inc(act, 1)
                for s in range(2):
                    a.wait_ge(vec, V.at(i, "aggr", s))
                    deviation(nc, k, s, mv, sd).then_inc(act, 1)
                for s in range(2):
                    a.wait_ge(vec, V.at(i, "norm", s))
                    nc.scalar.activation(slot(h, s), slot(h, s), ACT.Relu).then_inc(act, 1)

        @block.vector
        def _(d):
            d.sem_inc(vec, V.per)
            with d.Fori(0, NI) as i:
                for s in range(2):
                    d.wait_ge(pe, M.at(i, "product", s))
                    d.wait_ge(stored[s], i * 32 + AHEAD)
                    for c in range(G):
                        o = pair(k, 2 * s + 1)[:, c * D:(c + 1) * D]
                        last = nc.vector.scalar_tensor_tensor(tile(y, s, c), o, cols(k.norm_in, i, s, c),
                                                              k.b2_0[:, :], ALU.mult, ALU.add)
                    last.then_inc(vec, 1)
                for s in range(2):
                    d.wait_ge(gathered[s], i * (16 * G) + (16 * G + gbase))
                    d.wait_ge(vec, V.at(i, "out", s))
                    nc.vector.tensor_tensor(slot(x1, s), slot(x, s), slot(y, s), ALU.add).then_inc(vec, 1)
                for s in range(2):
                    d.wait_ge(vec, V.at(i, "x1", s))
                    stats(nc, x1, s, st).then_inc(vec, 1)
                for s in range(2):
                    wait_apart(d, k, vec, V.at(i, "stats", s))
                    aggregate(nc, s, st, mv).then_inc(vec, 1)
                for s in range(2):
                    d.wait_ge(act, A.at(i, "sd", s))
                    nc.vector.reciprocal(rs[:, s, :], sd[:, s, :]).then_inc(vec, 1)
                for s in range(2):
                    d.wait_ge(vec, V.at(i, "rs", s))
                    normalise(nc, x1, s, mv, rs, h).then_inc(vec, 1)
                for s in range(2):
                    d.wait_ge(act, A.at(i, "relu", s))
                    nc.vector.tensor_tensor(by_tile(slot(hw, s)), by_tile(slot(h, s)), every(k.attn_r[:, :]), ALU.mult).then_inc(vec, 1)
                for s in range(2):
                    d.wait_ge(vec, V.at(i, "weighted", s))
                    nc.vector.tensor_reduce(small(k.sr, i, s), slot(hw, s).rearrange("p (k h e) -> p k h e", h=H8, e=D // H8),
                                            AX.X, ALU.add).then_inc(vec, 1)


def small(arr, i, s):
    return arr[:, :, bass.ds(i * (2 * G) + s * G, G)].rearrange("p f c -> p c f")


def relational_edges(nc, k, name, table, first, width, weights, scores):
    second = not first
    adds = ("x",) if first else ("ax", "bx", "x")
    V = Steps(*adds, "stats", "aggr", "rs", "nb", "masked", *(("u",) if second else ()), lag=dict(masked=1))
    A = Steps("moved", "sd", ("message", 1), "relu", ("message", 0), lag={"moved": 1, ("message", 1): 2, ("message", 0): 1})
    M = Steps("turned", ("product", 1), *(("base",) if first else ()), ("product", 0),
              lag={"turned": 1, "base": 1, ("product", 1): 2, ("product", 0): 1})
    rel_rows = k.relT8 if first else k.relT4
    with Phase(nc, k, name) as ph:
        vec, act, pe, staged = (ph.sem(n) for n in ("vector_steps", "scalar_steps", "tensor_steps", "staged"))
        gathered, gbase = ph.moves("gathered", NI * 16 * G)
        loaded, stored, u_stored, told = (ph.sem2(n) for n in ("loaded", "stored", "u_stored", "message_stored"))
        rel_loaded = ph.sem2("rel_loaded")
        ring = ph.sb("ring", [P, 2 * G], I32)
        a_in, x_in, x1, h, rel, msg = (ph.ring(n) for n in ("a_in", "x_in", "x1", "h", "rel", "msg"))
        hT = ph.ring("hT")
        masked = ph.sb("masked", [P, 2, 4, W])
        ax, u = (ph.ring(n) if second else None for n in ("ax", "u"))
        st, mv = ph.sb("st", [P, 2, G, 6]), ph.sb("mv", [P, 2, G, 2])
        sd, rs, nb = (ph.sb(n, [P, 2, G]) for n in ("sd", "rs", "nb"))
        block = ph.block()

        @block.gpsimd
        def _(g):
            g.sem_inc(staged, 2)
            with g.Fori(0, NI) as i:
                for s in range(2):
                    wait_apart(g, k, vec, V.at(i - 1, adds[0], s))
                    gather_columns(nc, k, g, i, s, k.slot_i, ring, staged, table, a_in, D, gathered)

        @block.sync
        def _(sp):
            start_ahead(sp, stored, u_stored, told)

            def body(i, new, last, older):
                for s in range(2) if new else ():
                    if last:
                        sp.wait_ge(vec, V.at(i - 1, "x", s))
                    sp.dma_start(slot(x_in, s), part(k.XS, i, s)).then_inc(loaded[s], 16)
                for s in range(2) if last else ():
                    if older:
                        sp.wait_ge(vec, V.at(i - 2, "masked", s))
                    rows = rel_rows[bass.ds((i - 1) * (2 * G) + s * G, G), :].rearrange("(a t) p -> a (t p)", a=1).to_broadcast([P, W])
                    sp.dma_start(slot(rel, s), rows).then_inc(rel_loaded[s], 16)
                for s in range(2) if last else ():
                    sp.wait_ge(vec, V.at(i - 1, "x", s))
                    sp.dma_start(part(k.XS, i - 1, s), slot(x1, s)).then_inc(stored[s], 16)
                    if second:
                        sp.wait_ge(vec, V.at(i - 1, "u", s))
                        sp.dma_start(part(k.HS, i - 1, s), slot(u, s)).then_inc(u_stored[s], 16)
                for s in range(2) if older else ():
                    sp.wait_ge(act, A.at(i - 2, "message", s))
                    sp.dma_start(part(k.MSG, i - 2, s), slot(msg, s)).then_inc(told[s], 16)
            iterations(sp, body)
            for s in range(2):
                sp.wait_ge(stored[s], NI * 16 + AHEAD)
                sp.wait_ge(told[s], NI * 16 + AHEAD)
                if second:
                    sp.wait_ge(u_stored[s], NI * 16 + AHEAD)

        @block.vector
        def _(d):
            def body(i, new, last, older):
                if not new and last:
                    V.absent(d, vec, i, adds[0], 2 * (len(adds) + 4))
                for s in range(2) if new else ():
                    d.wait_ge(gathered[s], i * (16 * G) + (16 * G + gbase))
                    if first:
                        if last:
                            d.wait_ge(act, A.at(i - 1, "relu", s))
                        d.wait_ge(loaded[s], i * 16 + 16)
                        d.wait_ge(stored[s], i * 16 + AHEAD)
                        nc.vector.tensor_tensor(slot(x1, s), slot(a_in, s), slot(x_in, s), ALU.add).then_inc(vec, 1)
                    else:
                        nc.vector.tensor_tensor(by_tile(slot(ax, s)), by_tile(slot(a_in, s)), every(k.bn_a[:, :]), ALU.mult).then_inc(vec, 1)
                if second and new:
                    for s in range(2):
                        d.wait_ge(vec, V.at(i, "ax", s))
                        nc.vector.tensor_tensor(by_tile(slot(ax, s)), by_tile(slot(ax, s)), every(k.bn_b[:, :]), ALU.add).then_inc(vec, 1)
                    for s in range(2):
                        d.wait_ge(loaded[s], i * 16 + 16)
                        d.wait_ge(vec, V.at(i, "bx", s))
                        d.wait_ge(stored[s], i * 16 + AHEAD)
                        nc.vector.tensor_tensor(slot(x1, s), slot(ax, s), slot(x_in, s), ALU.add).then_inc(vec, 1)
                for s in range(2) if new else ():
                    d.wait_ge(vec, V.at(i, "x", s))
                    stats(nc, x1, s, st).then_inc(vec, 1)
                for s in range(2) if new else ():
                    wait_apart(d, k, vec, V.at(i, "stats", s))
                    aggregate(nc, s, st, mv).then_inc(vec, 1)
                for s in range(2) if new else ():
                    d.wait_ge(act, A.at(i, "sd", s))
                    nc.vector.reciprocal(rs[:, s, :], sd[:, s, :]).then_inc(vec, 1)
                for s in range(2) if new else ():
                    d.wait_ge(vec, V.at(i, "rs", s))
                    shift(nc, s, mv, rs, nb).then_inc(vec, 1)
                if new and not last:
                    V.absent(d, vec, i, "masked", 2)
                for s in range(2) if last else ():
                    if older:
                        d.wait_ge(pe, M.at(i - 2, "product", s))
                    d.wait_ge(rel_loaded[s], (i - 1) * 16 + 16)
                    if first:
                        d.wait_ge(pe, M.at(i - 1, "base", s))
                        right = pair(k, 1 - s)
                    else:
                        d.wait_ge(act, A.at(i - 1, "moved", s))
                        right = slot(hT, s)
                    for c in range(4):
                        which = k.rel_of[:, c:c + 1] if first else float(c)
                        step = nc.vector.scalar_tensor_tensor(masked[:, s, c, :], slot(rel, s), which, right, ALU.is_equal, ALU.mult)
                    step.then_inc(vec, 1)
                for s in range(2) if second and new else ():
                    d.wait_ge(act, A.at(i, "relu", s))
                    d.wait_ge(u_stored[s], i * 16 + AHEAD)
                    nc.vector.tensor_tensor(by_tile(slot(u, s)), by_tile(slot(h, s)), every(k.bias2[:, :]), ALU.add).then_inc(vec, 1)
            d.sem_inc(vec, V.per)
            iterations(d, body)

        @block.scalar
        def _(a):
            def body(i, new, last, older):
                def message(i, s):
                    a.wait_ge(pe, M.at(i, "product", s))
                    a.wait_ge(told[s], i * 16 + AHEAD)
                    for c, n in ((0, 3), (3, 3), (6, 1)):
                        got = k.psum[:, 2048 + c // 3 * 512:2048 + c // 3 * 512 + n * width].rearrange("p (c f) -> p c f", f=width)
                        nc.scalar.activation(by_tile(msg[:, place(s, c):place(s, c + n)]), got[:, :, 0:D], ACT.Copy)
                        step = nc.scalar.activation(scores[:, :, bass.ds(i * (2 * G) + (s * G + c), n)],
                                                    got[:, :, D:width].rearrange("p c f -> p f c"), ACT.Copy)
                    step.then_inc(act, 1)
                if not last and new:
                    A.absent(a, act, i, "moved", 2)
                for s in range(2) if last else ():
                    a.wait_ge(pe, M.at(i - 1, "turned", s))
                    if older:
                        a.wait_ge(*((pe, M.at(i - 2, "base", s)) if first else (vec, V.at(i - 2, "masked", s))))
                    nc.scalar.activation(slot(hT, s), pair(k, 0), ACT.Copy).then_inc(act, 1)
                if not new:
                    A.absent(a, act, i, "sd" if last else "moved", 2 if last else 4)
                for s in range(2) if new else ():
                    a.wait_ge(vec, V.at(i, "aggr", s))
                    deviation(nc, k, s, mv, sd).then_inc(act, 1)
                if older:
                    message(i - 2, 1)
                else:
                    A.absent(a, act, i, "message", 1, 1)
                if not new and last:
                    A.absent(a, act, i, "relu", 2)
                for s in range(2) if new else ():
                    a.wait_ge(vec, V.at(i, "nb", s))
                    if last:
                        a.wait_ge(pe, M.at(i - 1, "turned", s))
                    scaled_rows(nc, x1, s, rs, nb, h, ACT.Relu).then_inc(act, 1)
                if last:
                    message(i - 1, 0)
                elif new:
                    A.absent(a, act, i, "message", 1, 0)
            a.sem_inc(act, A.per)
            iterations(a, body)

        @block.tensor
        def _(t):
            def body(i, new, last, older):
                def product(i, s):
                    t.wait_ge(vec, V.at(i, "masked", s))
                    if s or not isinstance(i, int) or i:
                        t.wait_ge(act, A.at(i if s else i - 1, "message", 1 - s))
                    for c in range(G):
                        for r in range(4):
                            step = nc.tensor.matmul(wide(k, 2, c, width), masked[:, s, r, c * D:(c + 1) * D], weights[:, r, :],
                                                    start=(r == 0), stop=(r == 3))
                    step.then_inc(pe, 1)
                if not last and new:
                    return
                for s in range(2) if last else ():
                    t.wait_ge(act, A.at(i - 1, "relu", s))
                    if s:
                        t.wait_ge(act, A.at(i - 1, "moved", 0))
                    elif older:
                        t.wait_ge(*((vec, V.at(i - 2, "masked", 1)) if first else (act, A.at(i - 2, "moved", 1))))
                    transposed(nc, k, h, s, pair(k, 0)).then_inc(pe, 1)
                if not last:
                    M.absent(t, pe, i, "turned", 2)
                if older:
                    product(i - 2, 1)
                else:
                    M.absent(t, pe, i, "product", 1, 1)
                if first:
                    for s in range(2) if last else ():
                        t.wait_ge(act, A.at(i - 1, "moved", s))
                        if older and not s:
                            t.wait_ge(vec, V.at(i - 2, "masked", 0))
                        base = pair(k, 1 - s)
                        nc.tensor.matmul(base[:, 0:512], k.q2[:, :], slot(hT, s)[:, 0:512], start=True, stop=True)
                        nc.tensor.matmul(base[:, 512:W], k.q2[:, :], slot(hT, s)[:, 512:W], start=True, stop=True).then_inc(pe, 1)
                if last:
                    product(i - 1, 0)
            t.sem_inc(pe, 2 * M.per)
            iterations(t, body)


class Chain:

    def __init__(self, eng, sem):
        self.eng, self.sem, self.n = eng, sem, 0

    def __call__(self, ins):
        self.n += 1
        ins.then_inc(self.sem, 1)
        self.eng.wait_ge(self.sem, self.n)


def fetch_back(nc, k, d, chain, to_pe, from_pe, n, ends, work, firsts, rest, F):
    chain(nc.vector.tensor_tensor(work, ends, k.fix[:, :].unsqueeze(1).to_broadcast([P, F, T]), ALU.mult))
    chain(nc.vector.tensor_reduce(firsts, work, AX.X, ALU.add))
    d.sem_inc(to_pe, 1)
    d.wait_ge(from_pe, n)
    chain(nc.vector.tensor_copy(rest, k.psum[:, 0:F]))
    chain(nc.vector.tensor_tensor(work, ends, k.end[:, :].unsqueeze(1).to_broadcast([P, F, T]), ALU.mult))
    for f in range(F):
        last = nc.vector.tensor_tensor_scan(ends[:, f, ::-1], k.more[:, ::-1], work[:, f, ::-1], rest[:, f:f + 1], ALU.mult, ALU.add)
    chain(last)


def weigh_heads1(nc, k):
    with Phase(nc, k, "att1") as ph:
        v, to_pe, from_pe, act = (ph.sem(n) for n in ("vector_done", "firsts_ready", "rest_ready", "exp_done"))
        work = ph.sb("work", [P, H8, T])
        firsts, rest = ph.sb("firsts", [P, H8]), ph.sb("rest", [P, H8])
        top = ph.sb("top", [P, T])
        block = ph.block()

        @block.vector
        def _(d):
            chain = Chain(d, v)
            fetch_back(nc, k, d, chain, to_pe, from_pe, 1, k.sr, work[:, :, :], firsts[:, :], rest[:, :], H8)
            chain(d.tensor_tensor(work[:, :, :], k.sl, k.sr, ALU.add))
            chain(d.scalar_tensor_tensor(k.sl, work[:, :, :], SLOPE, work[:, :, :], ALU.mult, ALU.max))
            chain(d.tensor_reduce(top[:, :], k.sl.rearrange("p h t -> p t h"), AX.X, ALU.max))
            chain(d.tensor_tensor(k.sl, k.sl, top[:, :].unsqueeze(1).to_broadcast([P, H8, T]), ALU.subtract))
            assert chain.n == 9
            d.wait_ge(act, 1)
            chain(d.tensor_reduce(top[:, :], k.sl.rearrange("p h t -> p t h"), AX.X, ALU.add))
            chain(d.reciprocal(top[:, :], top[:, :]))
            d.tensor_tensor(k.sl, k.sl, top[:, :].unsqueeze(1).to_broadcast([P, H8, T]), ALU.mult)

        @block.tensor
        def _(t):
            t.wait_ge(to_pe, 1)
            t.wait_ge(v, 2)
            nc.tensor.matmul(k.psum[:, 0:H8], k.back[:, :], firsts[:, :], start=True, stop=True).then_inc(from_pe, 1)

        @block.scalar
        def _(a):
            a.wait_ge(v, 9)
            nc.scalar.activation(k.sl, k.sl, ACT.Exp).then_inc(act, 1)


def weigh_edges2(nc, k):
    with Phase(nc, k, "att2") as ph:
        v, to_pe, from_pe, act = (ph.sem(n) for n in ("vector_done", "asked", "answered", "exp_done"))
        F = R4 * H4
        full = [P, R4, H4, T]
        is_rel = ph.sb("is_rel", [P, R4, T])
        val, acc, work = ph.sb("val", full), ph.sb("acc", full), ph.sb("work", full)
        tails = ph.sb("tails", [P, 3, F])
        own = ph.sb("own", [P, H4, T])
        spread = ph.sb("spread", [P, F, P])
        block = ph.block()
        rel_b = is_rel[:, :, :].unsqueeze(2).to_broadcast(full)
        flat = lambda b: b[:, :, :, :].rearrange("p r h t -> p (r h) t")

        @block.vector
        def _(d):
            chain = Chain(d, v)

            def own_of(arr4):
                chain(d.tensor_tensor(work[:, :, :, :], arr4, rel_b, ALU.mult))
                chain(d.tensor_reduce(own[:, :, :], work[:, :, :, :].rearrange("p r h t -> p h t r"), AX.X, ALU.add))

            def scan(op):
                for f in range(F):
                    last = d.tensor_tensor_scan(flat(acc)[:, f, :], k.cont[:, :], flat(val)[:, f, :], 0.0, ALU.mult, op)
                chain(last)
                chain(d.tensor_copy(tails[:, 0, :], flat(acc)[:, :, T - 1]))

            for r in range(R4):
                chain(d.tensor_scalar(is_rel[:, r, :], k.rel4[:, :], float(r), None, ALU.is_equal))
            fetch_back(nc, k, d, chain, to_pe, from_pe, 1, k.ed, flat(work), tails[:, 0, :], tails[:, 1, :], F)
            assert chain.n == 9
            own_of(k.ed.rearrange("p (r h) t -> p r h t", h=H4))
            chain(d.tensor_tensor(own[:, :, :], own[:, :, :], k.es, ALU.add))
            chain(d.scalar_tensor_tensor(k.es, own[:, :, :], SLOPE, own[:, :, :], ALU.mult, ALU.max))
            chain(d.tensor_tensor(val[:, :, :, :], k.es.unsqueeze(1).to_broadcast(full), rel_b, ALU.mult))
            scan(ALU.max)
            chain(d.tensor_tensor(spread[:, :, :], tails[:, 0, :].unsqueeze(2).to_broadcast([P, F, P]),
                                  k.ident[:, :].unsqueeze(1).to_broadcast([P, F, P]), ALU.mult))
            assert chain.n == 17
            d.sem_inc(to_pe, 1)
            d.wait_ge(from_pe, 2)
            chain(d.tensor_tensor(spread[:, :, :], k.psum[:, 0:F * P].rearrange("p (f q) -> p f q", q=P),
                                  k.intoT[:, :].unsqueeze(1).to_broadcast([P, F, P]), ALU.mult))
            chain(d.tensor_reduce(tails[:, 2, :], spread[:, :, :], AX.X, ALU.max))
            for f in range(F):
                last = d.scalar_tensor_tensor(flat(acc)[:, f, :], k.fix[:, :], tails[:, 2, f:f + 1], flat(acc)[:, f, :], ALU.mult, ALU.max)
            chain(last)
            fetch_back(nc, k, d, chain, to_pe, from_pe, 3, flat(acc), flat(work), tails[:, 0, :], tails[:, 1, :], F)
            assert chain.n == 25
            own_of(acc[:, :, :, :])
            chain(d.tensor_tensor(k.es, k.es, own[:, :, :], ALU.subtract))
            assert chain.n == 28
            d.wait_ge(act, 1)
            chain(d.tensor_tensor(val[:, :, :, :], k.es.unsqueeze(1).to_broadcast(full), rel_b, ALU.mult))
            scan(ALU.add)
            assert chain.n == 31
            d.sem_inc(to_pe, 1)
            d.wait_ge(from_pe, 4)
            chain(d.tensor_copy(tails[:, 2, :], k.psum[:, 0:F]))
            for f in range(F):
                last = d.scalar_tensor_tensor(flat(acc)[:, f, :], k.fix[:, :], tails[:, 2, f:f + 1], flat(acc)[:, f, :], ALU.mult, ALU.add)
            chain(last)
            fetch_back(nc, k, d, chain, to_pe, from_pe, 5, flat(acc), flat(work), tails[:, 0, :], tails[:, 1, :], F)
            assert chain.n == 38
            own_of(acc[:, :, :, :])
            chain(d.tensor_scalar(own[:, :, :], own[:, :, :], 1e-8, None, ALU.add))
            chain(d.reciprocal(own[:, :, :], own[:, :, :]))
            chain(d.tensor_tensor(k.es, k.es, own[:, :, :], ALU.mult))

        @block.scalar
        def _(a):
            a.wait_ge(v, 28)
            nc.scalar.activation(k.es, k.es, ACT.Exp).then_inc(act, 1)

        @block.tensor
        def _(t):
            def product(n, steps, weights, m):
                t.wait_ge(to_pe, n)
                t.wait_ge(v, steps)
                nc.tensor.matmul(k.psum[:, 0:F], weights[:, :], tails[:, m, :], start=True, stop=True).then_inc(from_pe, 1)
            product(1, 6, k.back, 0)
            t.wait_ge(to_pe, 2)
            t.wait_ge(v, 17)
            for c in range(4):
                last = nc.tensor.matmul(k.psum[:, c * 512:(c + 1) * 512], k.ones[:, :],
                                        spread[:, 4 * c:4 * c + 4, :].rearrange("p f q -> p (f q)"), start=True, stop=True)
            last.then_inc(from_pe, 1)
            product(3, 22, k.back, 0)
            product(4, 31, k.into, 0)
            product(5, 35, k.back, 0)


def weighted_edges(nc, k, name, heads, att, V_table):
    V = Steps("weighted", *slotwise(*SUMS))
    with Phase(nc, k, name) as ph:
        vec, cleared = ph.sem("vector_steps"), ph.sem("cleared")
        loaded, stored = ph.sem2("loaded"), ph.sem2("stored")
        m, w, sums = ph.ring("m"), ph.ring("w"), ph.ring("sums")
        block = ph.block()

        @block.sync
        def _(sp):
            start_ahead(sp, stored)
            def load(i):
                for s in range(2):
                    sp.wait_ge(vec, V.at(i - 1, "weighted", s))
                    sp.dma_start(slot(m, s), part(k.MSG, i, s)).then_inc(loaded[s], 16)

            def store(i):
                for s in range(2):
                    sp.wait_ge(vec, V.at(i, SUMS[-1], s))
                    sp.dma_start(part(V_table, i, s), slot(sums, s)).then_inc(stored[s], 16)
            load(0)
            with sp.Fori(1, NI) as i:
                load(i)
                store(i - 1)
            store(NI - 1)
            for s in range(2):
                sp.wait_ge(stored[s], NI * 16 + AHEAD)

        @block.vector
        def _(d):
            d.memset(tile(sums, 1, G - 1), 0.0).then_inc(cleared, 1)
            d.wait_ge(cleared, 1)
            d.sem_inc(vec, V.per)
            with d.Fori(0, NI) as i:
                for s in range(2):
                    d.wait_ge(loaded[s], i * 16 + 16)
                    d.wait_ge(vec, V.at(i - 1, SUMS[-1], s))
                    e = D // heads
                    view = lambda b: slot(b, s).rearrange("p (k h e) -> p k h e", h=heads, e=e)
                    for c in range(G):
                        wt = att[:, :, bass.ds(i * (2 * G) + (s * G + c), 1)].to_broadcast([P, heads, e])
                        last = nc.vector.tensor_tensor(view(w)[:, c, :, :], view(m)[:, c, :, :], wt, ALU.mult)
                    last.then_inc(vec, 1)
                for s in range(2):
                    d.wait_ge(vec, V.at(i, "weighted", s))
                    d.wait_ge(stored[s], i * 16 + AHEAD)
                    running_sum(nc, k, d, vec, V, i, s, w, sums)
            d.wait_ge(vec, V.last())
            d.tensor_copy(k.tail[:, :], tile(sums, 1, G - 1))


def batch_stats(nc, k):
    A = Steps("squared")
    M = Steps("summed")
    with Phase(nc, k, "bn") as ph:
        act, pe, v, tdone, ready = (ph.sem(n) for n in ("scalar_steps", "tensor_steps", "vector_done", "tensor_done", "sqrt_done"))
        loaded = ph.sem2("loaded")
        va, sq = ph.ring("va"), ph.ring("sq")
        c = ph.sb("c", [P, 6])
        dg = ph.sb("dg", [P, 2, P])
        block = ph.block()

        @block.sync
        def _(sp):
            with sp.Fori(0, NI) as i:
                for s in range(2):
                    sp.wait_ge(pe, M.at(i - 1, "summed", s))
                    sp.dma_start(slot(va, s), part(k.V2, i, s)).then_inc(loaded[s], 16)

        @block.scalar
        def _(a):
            a.sem_inc(act, A.per)
            with a.Fori(0, NI) as i:
                for s in range(2):
                    a.wait_ge(loaded[s], i * 16 + 16)
                    a.wait_ge(pe, M.at(i - 1, "summed", s))
                    nc.scalar.activation(slot(sq, s), slot(va, s), ACT.Square).then_inc(act, 1)
            a.wait_ge(v, 4)
            nc.scalar.activation(c[:, 3:4], c[:, 2:3], ACT.Sqrt, bias=k.eps[:, 0:1]).then_inc(ready, 1)

        @block.tensor
        def _(t):
            S, Q = k.psum[:, 0:1], k.psum[:, 512:513]
            nc.tensor.matmul(S, k.zeros[:, :], k.ones[:, 0:1], start=True, stop=False, skip_group_check=True)
            nc.tensor.matmul(Q, k.zeros[:, :], k.ones[:, 0:1], start=True, stop=False, skip_group_check=True)
            t.sem_inc(pe, M.per)
            with t.Fori(0, NI) as i:
                for s in range(2):
                    t.wait_ge(loaded[s], i * 16 + 16)
                    t.wait_ge(act, A.at(i, "squared", s))
                    for j in range(G):
                        nc.tensor.matmul(S, tile(va, s, j), cols(k.real_end, i, s, j), start=False, stop=False, skip_group_check=True)
                        last = nc.tensor.matmul(Q, tile(sq, s, j), cols(k.real_end, i, s, j), start=False, stop=False, skip_group_check=True)
                    last.then_inc(pe, 1)
            t.wait_ge(v, 10)
            nc.tensor.matmul(k.psum[:, 1024:1024 + 2 * P], k.ones[:, :], dg[:, :, :].rearrange("p a q -> p (a q)"),
                             start=True, stop=True).then_inc(tdone, 1)

        @block.vector
        def _(d):
            chain = Chain(d, v)
            d.wait_ge(pe, M.last())
            chain(d.tensor_scalar(c[:, 0:1], k.psum[:, 0:1], 1.0 / NODES, None, ALU.mult))
            chain(d.tensor_scalar(c[:, 1:2], k.psum[:, 512:513], 1.0 / NODES, None, ALU.mult))
            chain(d.tensor_tensor(c[:, 2:3], c[:, 0:1], c[:, 0:1], ALU.mult))
            chain(d.tensor_tensor(c[:, 2:3], c[:, 1:2], c[:, 2:3], ALU.subtract))
            d.wait_ge(ready, 1)
            chain(d.reciprocal(c[:, 3:4], c[:, 3:4]))
            chain(d.tensor_tensor(c[:, 3:4], c[:, 3:4], k.gb[:, 0:1], ALU.mult))
            chain(d.tensor_tensor(c[:, 4:5], c[:, 0:1], c[:, 3:4], ALU.mult))
            chain(d.tensor_tensor(c[:, 4:5], k.gb[:, 1:2], c[:, 4:5], ALU.subtract))
            chain(d.tensor_scalar(dg[:, 0, :], k.ident[:, :], c[:, 3:4], None, ALU.mult))
            chain(d.tensor_scalar(dg[:, 1, :], k.ident[:, :], c[:, 4:5], None, ALU.mult))
            d.wait_ge(tdone, 1)
            chain(d.tensor_copy(k.bn_a[:, :], k.psum[:, 1024:1024 + P]))
            chain(d.tensor_copy(k.bn_b[:, :], k.psum[:, 1024 + P:1024 + 2 * P]))
            chain(d.tensor_tensor(k.plain[:, :], k.bn_b[:, :], k.b2_0[:, :], ALU.add))


def layer2_nodes(nc, k):
    V = Steps("ax", "bx", "x", "u", "scores", "stats", "aggr", "rs", "nb", lag=dict(u=1, scores=1))
    A = Steps("moved", "sd", "relu", lag=dict(moved=1))
    M = Steps("turned", "product")
    F = R4 * H4
    with Phase(nc, k, "n2") as ph:
        vec, act, pe = (ph.sem(n) for n in ("vector_steps", "scalar_steps", "tensor_steps"))
        loaded, stored, u_stored = ph.sem2("loaded"), ph.sem2("stored"), ph.sem2("u_stored")
        a_in, x_in, ax, x1, h, u, hT = (ph.ring(n) for n in ("a_in", "x_in", "ax", "x1", "h", "u", "hT"))
        st, mv = ph.sb("st", [P, 2, G, 6]), ph.sb("mv", [P, 2, G, 2])
        sd, rs, nb = (ph.sb(n, [P, 2, G]) for n in ("sd", "rs", "nb"))
        block = ph.block()

        @block.sync
        def _(sp):
            start_ahead(sp, stored, u_stored)

            def body(i, new, last, older):
                for s in range(2) if new else ():
                    if last:
                        sp.wait_ge(vec, V.at(i - 1, "x", s))
                    sp.dma_start(slot(a_in, s), part(k.V2, i, s)).then_inc(loaded[s], 16)
                    sp.dma_start(slot(x_in, s), part(k.XD, i, s)).then_inc(loaded[s], 16)
                for s in range(2) if last else ():
                    sp.wait_ge(vec, V.at(i - 1, "x", s))
                    sp.dma_start(part(k.XD, i - 1, s), slot(x1, s)).then_inc(stored[s], 16)
                for s in range(2) if older else ():
                    sp.wait_ge(vec, V.at(i - 2, "u", s))
                    sp.dma_start(part(k.HD, i - 2, s), slot(u, s)).then_inc(u_stored[s], 16)
            iterations(sp, body)
            for s in range(2):
                sp.wait_ge(stored[s], NI * 16 + AHEAD)
                sp.wait_ge(u_stored[s], NI * 16 + AHEAD)

        @block.vector
        def _(d):
            def body(i, new, last, older):
                if last and not new:
                    V.absent(d, vec, i, "ax", 6)
                for s in range(2) if new else ():
                    d.wait_ge(loaded[s], i * 32 + 32)
                    nc.vector.tensor_tensor(by_tile(slot(ax, s)), by_tile(slot(a_in, s)), every(k.bn_a[:, :]), ALU.mult).then_inc(vec, 1)
                for s in range(2) if new else ():
                    d.wait_ge(vec, V.at(i, "ax", s))
                    nc.vector.tensor_tensor(by_tile(slot(ax, s)), by_tile(slot(ax, s)), every(k.bn_b[:, :]), ALU.add).then_inc(vec, 1)
                for s in range(2) if new else ():
                    d.wait_ge(vec, V.at(i, "bx", s))
                    if last:
                        d.wait_ge(act, A.at(i - 1, "relu", s))
                    d.wait_ge(stored[s], i * 16 + AHEAD)
                    nc.vector.tensor_tensor(slot(x1, s), slot(ax, s), slot(x_in, s), ALU.add).then_inc(vec, 1)
                if new and not last:
                    V.absent(d, vec, i, "u", 4)
                for s in range(2) if last else ():
                    d.wait_ge(act, A.at(i - 1, "relu", s))
                    d.wait_ge(u_stored[s], (i - 1) * 16 + AHEAD)
                    nc.vector.tensor_tensor(by_tile(slot(u, s)), by_tile(slot(h, s)), every(k.bias2[:, :]), ALU.add).then_inc(vec, 1)
                for s in range(2) if last else ():
                    d.wait_ge(pe, M.at(i - 1, "product", s))
                    got = pair(k, 2 * s + 1)[:, 0:G * F].rearrange("p (c f) -> p c f", f=F)
                    nc.vector.tensor_copy(small(k.ed, i - 1, s), got).then_inc(vec, 1)
                for s in range(2) if new else ():
                    d.wait_ge(vec, V.at(i, "x", s))
                    stats(nc, x1, s, st).then_inc(vec, 1)
                for s in range(2) if new else ():
                    wait_apart(d, k, vec, V.at(i, "stats", s))
                    aggregate(nc, s, st, mv).then_inc(vec, 1)
                for s in range(2) if new else ():
                    d.wait_ge(act, A.at(i, "sd", s))
                    nc.vector.reciprocal(rs[:, s, :], sd[:, s, :]).then_inc(vec, 1)
                for s in range(2) if new else ():
                    d.wait_ge(vec, V.at(i, "rs", s))
                    shift(nc, s, mv, rs, nb).then_inc(vec, 1)
            d.sem_inc(vec, V.per)
            iterations(d, body)

        @block.scalar
        def _(a):
            def body(i, new, last, older):
                if new and not last:
                    A.absent(a, act, i, "moved", 2)
                for s in range(2) if last else ():
                    a.wait_ge(pe, M.at(i - 1, "turned", s))
                    if older:
                        a.wait_ge(pe, M.at(i - 2, "product", s))
                    nc.scalar.activation(slot(hT, s), pair(k, 2 * s), ACT.Copy).then_inc(act, 1)
                for s in range(2) if new else ():
                    a.wait_ge(vec, V.at(i, "aggr", s))
                    deviation(nc, k, s, mv, sd).then_inc(act, 1)
                for s in range(2) if new else ():
                    a.wait_ge(vec, V.at(i, "nb", s))
                    if last:
                        a.wait_ge(pe, M.at(i - 1, "turned", s))
                    scaled_rows(nc, x1, s, rs, nb, h, ACT.Relu).then_inc(act, 1)
            a.sem_inc(act, A.per)
            iterations(a, body)

        @block.tensor
        def _(t):
            t.sem_inc(pe, M.per)
            with t.Fori(0, NI) as i:
                for s in range(2):
                    t.wait_ge(act, A.at(i, "relu", s))
                    t.wait_ge(act, A.at(i - 1, "moved", s))
                    transposed(nc, k, h, s, pair(k, 2 * s)).then_inc(pe, 1)
                for s in range(2):
                    t.wait_ge(act, A.at(i, "moved", s))
                    t.wait_ge(vec, V.at(i - 1, "scores", s))
                    for c in range(G):
                        last = nc.tensor.matmul(pair(k, 2 * s + 1)[:, c * F:(c + 1) * F], tile(hT, s, c), k.vdst[:, :], start=True, stop=True)
                    last.then_inc(pe, 1)


def layer3_inputs(nc, k, name, edges):
    late = ("scaled", "shifted", "x", "stats2", "aggr2", "rs2", "nb2") + SUMS
    V = Steps("scaled", "shifted", "x", "stats2", "aggr2", "o", "rs2", "nb2", "stats", "aggr", "rs", "nb",
              *(slotwise(*SUMS) if edges else ()), lag=dict.fromkeys(late, 1))
    A = Steps("sd2", "relu", "sd", "norm", lag=dict(sd2=1, relu=1))
    x_table, u_table = (k.XS, k.HS) if edges else (k.XD, k.HD)
    with Phase(nc, k, name) as ph:
        vec, act, staged, cleared = (ph.sem(n) for n in ("vector_steps", "scalar_steps", "staged", "cleared"))
        gathered, gbase = ph.moves("gathered", NI * 16 * G if edges else 0)
        loaded, x_loaded, stored = ph.sem2("loaded"), ph.sem2("x_loaded"), ph.sem2("stored")
        summed = ph.sem2("sums_stored")
        ring = ph.sb("ring", [P, 2 * G], I32)
        a_in, u_in, x_in, o, y, x3, h = (ph.ring(n) for n in ("a_in", "u_in", "x_in", "o", "y", "x3", "h"))
        sums = ph.ring("sums") if edges else None
        st, st2 = (ph.sb(n, [P, 2, G, 6]) for n in ("st", "st2"))
        mv, mv2 = (ph.sb(n, [P, 2, G, 2]) for n in ("mv", "mv2"))
        sd, rs, nb, sd2, rs2, nb2 = (ph.sb(n, [P, 2, G]) for n in ("sd", "rs", "nb", "sd2", "rs2", "nb2"))
        block = ph.block()
        nload = 16 if edges else 32
        nstore = 16 if edges else 32

        if edges:
            @block.gpsimd
            def _(g):
                g.sem_inc(staged, 2)
                with g.Fori(0, NI) as i:
                    for s in range(2):
                        wait_apart(g, k, vec, V.at(i - 1, "o", s))
                        gather_columns(nc, k, g, i, s, k.slot_i, ring, staged, k.V3, a_in, D, gathered)

        @block.sync
        def _(sp):
            start_ahead(sp, stored, summed)

            def body(i, new, last, older):
                for s in range(2) if last else ():
                    if older:
                        sp.wait_ge(vec, V.at(i - 2, "x", s))
                    sp.dma_start(slot(x_in, s), part(x_table, i - 1, s)).then_inc(x_loaded[s], 16)
                for s in range(2) if older and not edges else ():
                    sp.wait_ge(vec, V.at(i - 2, "x", s))
                    sp.dma_start(part(k.XD, i - 2, s), slot(x3, s)).then_inc(stored[s], 16)
                for s in range(2) if new else ():
                    if last:
                        sp.wait_ge(vec, V.at(i - 1, "o", s))
                    if not edges:
                        sp.dma_start(slot(a_in, s), part(k.V3, i, s)).then_inc(loaded[s], 16)
                    sp.dma_start(slot(u_in, s), part(u_table, i, s)).then_inc(loaded[s], 16)
                for s in range(2) if older else ():
                    sp.wait_ge(act, A.at(i - 2, "relu", s))
                    sp.dma_start(part(u_table, i - 2, s), slot(h, s)).then_inc(stored[s], 16)
                for s in range(2) if older and edges else ():
                    sp.wait_ge(vec, V.at(i - 2, SUMS[-1], s))
                    sp.dma_start(part(k.V4, i - 2, s), slot(sums, s)).then_inc(summed[s], 16)
            iterations(sp, body)
            for s in range(2):
                sp.wait_ge(stored[s], NI * nstore + AHEAD)
                if edges:
                    sp.wait_ge(summed[s], NI * 16 + AHEAD)

        @block.vector
        def _(d):
            def body(i, new, last, older):
                if new and not last:
                    V.absent(d, vec, i, "scaled", 10)
                for s in range(2) if last else ():
                    d.wait_ge(act, A.at(i - 1, "norm", s))
                    nc.vector.tensor_tensor(by_tile(slot(y, s)), by_tile(slot(y, s)), every(k.ln_g[:, :]), ALU.mult).then_inc(vec, 1)
                for s in range(2) if last else ():
                    d.wait_ge(vec, V.at(i - 1, "scaled", s))
                    nc.vector.tensor_tensor(by_tile(slot(y, s)), by_tile(slot(y, s)), every(k.ln_b[:, :]), ALU.add).then_inc(vec, 1)
                for s in range(2) if last else ():
                    d.wait_ge(vec, V.at(i - 1, "shifted", s))
                    d.wait_ge(x_loaded[s], (i - 1) * 16 + 16)
                    if older:
                        d.wait_ge(act, A.at(i - 2, "relu", s))
                    d.wait_ge(stored[s], (i - 1) * nstore + AHEAD)
                    nc.vector.tensor_tensor(slot(x3, s), slot(y, s), slot(x_in, s), ALU.add).then_inc(vec, 1)
                for s in range(2) if last else ():
                    d.wait_ge(vec, V.at(i - 1, "x", s))
                    stats(nc, x3, s, st2).then_inc(vec, 1)
                for s in range(2) if last else ():
                    wait_apart(d, k, vec, V.at(i - 1, "stats2", s))
                    aggregate(nc, s, st2, mv2).then_inc(vec, 1)
                for s in range(2) if new else ():
                    if edges:
                        d.wait_ge(gathered[s], i * (16 * G) + (16 * G + gbase))
                    d.wait_ge(loaded[s], i * nload + nload)
                    nc.vector.tensor_tensor(slot(o, s), slot(a_in, s), slot(u_in, s), ALU.add).then_inc(vec, 1)
                if last and not new:
                    V.absent(d, vec, i, "o", 2)
                if new and not last:
                    V.absent(d, vec, i, "rs2", 4)
                for s in range(2) if last else ():
                    d.wait_ge(act, A.at(i - 1, "sd2", s))
                    nc.vector.reciprocal(rs2[:, s, :], sd2[:, s, :]).then_inc(vec, 1)
                for s in range(2) if last else ():
                    d.wait_ge(vec, V.at(i - 1, "rs2", s))
                    shift(nc, s, mv2, rs2, nb2).then_inc(vec, 1)
                for s in range(2) if new else ():
                    d.wait_ge(vec, V.at(i, "o", s))
                    stats(nc, o, s, st).then_inc(vec, 1)
                for s in range(2) if new else ():
                    wait_apart(d, k, vec, V.at(i, "stats", s))
                    aggregate(nc, s, st, mv).then_inc(vec, 1)
                for s in range(2) if new else ():
                    d.wait_ge(act, A.at(i, "sd", s))
                    nc.vector.reciprocal(rs[:, s, :], sd[:, s, :]).then_inc(vec, 1)
                for s in range(2) if new else ():
                    d.wait_ge(vec, V.at(i, "rs", s))
                    shift(nc, s, mv, rs, nb).then_inc(vec, 1)
                if edges:
                    if last and not new:
                        V.absent(d, vec, i, "stats", 8)
                    if new and not last:
                        V.absent(d, vec, i, "sum0", 2 * G)
                    for s in range(2) if last else ():
                        d.wait_ge(act, A.at(i - 1, "relu", s))
                        d.wait_ge(summed[s], (i - 1) * 16 + AHEAD)
                        running_sum(nc, k, d, vec, V, i - 1, s, h, sums)
            if edges:
                d.memset(tile(sums, 1, G - 1), 0.0).then_inc(cleared, 1)
                d.wait_ge(cleared, 1)
            d.sem_inc(vec, V.per)
            iterations(d, body)
            if edges:
                d.wait_ge(vec, V.at(NI - 1, SUMS[-1], 1))
                d.tensor_copy(k.tail[:, :], tile(sums, 1, G - 1))

        @block.scalar
        def _(a):
            def body(i, new, last, older):
                if new and not last:
                    A.absent(a, act, i, "sd2", 4)
                for s in range(2) if last else ():
                    a.wait_ge(vec, V.at(i - 1, "aggr2", s))
                    deviation(nc, k, s, mv2, sd2).then_inc(act, 1)
                for s in range(2) if last else ():
                    a.wait_ge(vec, V.at(i - 1, "nb2", s))
                    scaled_rows(nc, x3, s, rs2, nb2, h, ACT.Relu).then_inc(act, 1)
                for s in range(2) if new else ():
                    a.wait_ge(vec, V.at(i, "aggr", s))
                    deviation(nc, k, s, mv, sd).then_inc(act, 1)
                for s in range(2) if new else ():
                    a.wait_ge(vec, V.at(i, "nb", s))
                    scaled_rows(nc, o, s, rs, nb, y, ACT.Identity).then_inc(act, 1)
            a.sem_inc(act, A.per)
            iterations(a, body)


def graph_mlp(nc, k, name, edges, layer):
    final = layer == 1
    V = Steps("z", "biased", *(("out",) if final else ()), *(slotwise(*SUMS) if edges else ()),
              lag=dict.fromkeys(("biased", "out") + SUMS, 1))
    A = Steps("moved", *(() if final else ("relu",)), "hidden", lag=dict(relu=1))
    M = Steps("turned", "inner", "product")
    sum_table = k.V5 if final else k.V4
    with Phase(nc, k, name) as ph:
        vec, act, pe, staged, cleared = (ph.sem(n) for n in ("vector_steps", "scalar_steps", "tensor_steps", "staged", "cleared"))
        gathered, gbase = ph.moves("gathered", NI * 16 * G if edges else 0)
        scattered, sbase = ph.moves("scattered", NI * 16 * G if final else 0)
        loaded, x_loaded, stored = ph.sem2("loaded"), ph.sem2("x_loaded"), ph.sem2("stored")
        ring = ph.sb("ring", [P, 2 * G], I32)
        a_in, h_in, z, zT, hidden, y = (ph.ring(n) for n in ("a_in", "h_in", "z", "zT", "hidden", "y"))
        x_in = ph.ring("x_in") if final else None
        sums = ph.ring("sums") if edges else None
        block = ph.block()
        nload = 16 + 16 * (not edges)
        w_in, w_out = k.w3[:, 2 * layer, :], k.w3[:, 2 * layer + 1, :]
        b_in, b_out = k.b3[:, 2 * layer:2 * layer + 1], k.b3_row[:, layer, :]

        @block.gpsimd
        def _(g):
            if edges or final:
                g.sem_inc(staged, 2)
                with g.Fori(0, NI) as i:
                    for s in range(2):
                        if edges:
                            wait_apart(g, k, vec, V.at(i - 1, "z", s))
                            gather_columns(nc, k, g, i, s, k.slot_i, ring, staged, k.V4, a_in, D, gathered)
                        else:
                            wait_apart(g, k, scattered[s], i * (16 * G) + sbase)
                            g.tensor_copy(ring[:, s * G:(s + 1) * G], cols(k.out_i, i, s, 0, G)).then_inc(staged, 1)
                            wait_apart(g, k, staged, i * 2 + (s + 3))
                            wait_apart(g, k, vec, V.at(i, "out", s))
                            for c in range(G):
                                at = bass.IndirectOffsetOnAxis(ap=ring[:, s * G + c:s * G + c + 1], axis=0)
                                g.indirect_dma_start(k.out, at, tile(y, s, c), None, bounds_check=NODES - 1,
                                                     oob_is_err=False).then_inc(scattered[s], 16)
                if final:
                    for s in range(2):
                        g.wait_ge(scattered[s], NI * 16 * G + sbase)

        @block.sync
        def _(sp):
            start_ahead(sp, stored)
            def body(i, new, last, older):
                for s in range(2) if final and last else ():
                    if older:
                        sp.wait_ge(vec, V.at(i - 2, "out", s))
                    sp.dma_start(slot(x_in, s), part(k.XD, i - 1, s)).then_inc(x_loaded[s], 16)
                for s in range(2) if new else ():
                    if last:
                        sp.wait_ge(vec, V.at(i - 1, "z", s))
                    if not edges:
                        sp.dma_start(slot(a_in, s), part(sum_table, i, s)).then_inc(loaded[s], 16)
                    sp.dma_start(slot(h_in, s), part(k.HS if edges else k.HD, i, s)).then_inc(loaded[s], 16)
                for s in range(2) if older else ():
                    if edges:
                        sp.wait_ge(vec, V.at(i - 2, SUMS[-1], s))
                        sp.dma_start(part(k.V5, i - 2, s), slot(sums, s)).then_inc(stored[s], 16)
                    elif not final:
                        sp.wait_ge(act, A.at(i - 2, "relu", s))
                        sp.dma_start(part(k.HD, i - 2, s), slot(y, s)).then_inc(stored[s], 16)
            iterations(sp, body)
            if not final:
                for s in range(2):
                    sp.wait_ge(stored[s], NI * 16 + AHEAD)

        @block.vector
        def _(d):
            def body(i, new, last, older):
                for s in range(2) if new else ():
                    if edges:
                        d.wait_ge(gathered[s], i * (16 * G) + (16 * G + gbase))
                    d.wait_ge(loaded[s], i * nload + nload)
                    if last:
                        d.wait_ge(pe, M.at(i - 1, "turned", s))
                    nc.vector.tensor_tensor(slot(z, s), slot(a_in, s), slot(h_in, s), ALU.add).then_inc(vec, 1)
                if last and not new:
                    V.absent(d, vec, i, "z", 2)
                if new and not last:
                    V.absent(d, vec, i, "biased", V.per - 2)
                for s in range(2) if last else ():
                    d.wait_ge(pe, M.at(i - 1, "product", s))
                    if final:
                        if older:
                            d.wait_ge(scattered[s], (i - 1) * (16 * G) + sbase)
                    elif edges:
                        d.wait_ge(vec, V.at(i - 2, SUMS[-1], s))
                    else:
                        d.wait_ge(stored[s], (i - 1) * 16 + AHEAD)
                    nc.vector.tensor_tensor(by_tile(slot(y, s)), by_tile(pair(k, 2 * s)), every(b_out), ALU.add).then_inc(vec, 1)
                if final:
                    for s in range(2) if last else ():
                        d.wait_ge(vec, V.at(i - 1, "biased", s))
                        d.wait_ge(x_loaded[s], (i - 1) * 16 + 16)
                        nc.vector.scalar_tensor_tensor(slot(y, s), slot(y, s), 0.0, slot(x_in, s), ALU.max, ALU.add).then_inc(vec, 1)
                if edges:
                    for s in range(2) if last else ():
                        d.wait_ge(act, A.at(i - 1, "relu", s))
                        d.wait_ge(stored[s], (i - 1) * 16 + AHEAD)
                        running_sum(nc, k, d, vec, V, i - 1, s, y, sums)
            if edges:
                d.memset(tile(sums, 1, G - 1), 0.0).then_inc(cleared, 1)
                d.wait_ge(cleared, 1)
            d.sem_inc(vec, V.per)
            iterations(d, body)
            if edges:
                d.wait_ge(vec, V.at(NI - 1, SUMS[-1], 1))
                d.tensor_copy(k.tail[:, :], tile(sums, 1, G - 1))

        @block.scalar
        def _(a):
            def body(i, new, last, older):
                for s in range(2) if new else ():
                    a.wait_ge(pe, M.at(i, "turned", s))
                    nc.scalar.activation(slot(zT, s), pair(k, 2 * s), ACT.Copy).then_inc(act, 1)
                if not final:
                    if last and not new:
                        A.absent(a, act, i, "moved", 2)
                    if new and not last:
                        A.absent(a, act, i, "relu", 2)
                    for s in range(2) if last else ():
                        a.wait_ge(vec, V.at(i - 1, "biased", s))
                        nc.scalar.activation(slot(y, s), slot(y, s), ACT.Relu).then_inc(act, 1)
                for s in range(2) if new else ():
                    a.wait_ge(pe, M.at(i, "inner", s))
                    nc.scalar.activation(slot(hidden, s), pair(k, 2 * s + 1), ACT.Relu, bias=b_in).then_inc(act, 1)
            a.sem_inc(act, A.per)
            iterations(a, body)

        @block.tensor
        def _(t):
            t.sem_inc(pe, M.per)
            with t.Fori(0, NI) as i:
                for s in range(2):
                    t.wait_ge(vec, V.at(i, "z", s))
                    t.wait_ge(vec, V.at(i - 1, "biased", s))
                    transposed(nc, k, z, s, pair(k, 2 * s)).then_inc(pe, 1)
                for s in range(2):
                    t.wait_ge(act, A.at(i, "moved", s))
                    times_cols(nc, zT, s, w_in, pair(k, 2 * s + 1)).then_inc(pe, 1)
                for s in range(2):
                    t.wait_ge(act, A.at(i, "hidden", s))
                    times_rows(nc, hidden, s, w_out, pair(k, 2 * s)).then_inc(pe, 1)


def all_nodes(nc, k):
    ROWS = P * G
    V = Steps("u", "x3", "stats2", "stats3", "stats", "aggr2", "aggr3", "aggr", "rs2", "rs3", "rs", "nb2", "nb", "norm3",
              "out", "scaled",
              lag=dict(u=1, stats2=1, aggr2=1, rs2=1, nb2=1, scaled=1, x3=2, stats3=2, aggr3=2, rs3=2, norm3=2, out=3))
    A = Steps("hidden2", "hidden3", "sd2", "sd3", "sd", "norm2", "relu", "moved", "hidden1",
              lag=dict(sd2=1, norm2=1, sd3=2, moved=2, hidden1=2, hidden2=3, hidden3=3))
    M = Steps("inner2", "inner3", "product", "turned", "inner1", lag=dict(turned=2, inner1=2, inner2=3, inner3=3, product=3))
    X = Steps("xb", "x", "x3_kept", lag=dict(xb=1, x3_kept=2))
    N = -(-NODES // ROWS) // 2
    LAG = 3
    with Phase(nc, k, "all") as ph:
        vec, act, pe, pool, cleared = (ph.sem(n) for n in ("vector_steps", "scalar_steps", "tensor_steps", "gpsimd_steps", "cleared"))
        loaded, stored = ph.sem2("loaded"), ph.sem2("stored")
        x_in, x, xb, h, u, y, x3, x3k, h3, hT, aT, out = (
            ph.ring(n) for n in ("x_in", "x", "xb", "h", "u", "y", "x3", "x3k", "h3", "hT", "aT", "out"))
        st = [ph.sb(f"st{n}", [P, 2, G, 6]) for n in range(3)]
        mv = [ph.sb(f"mv{n}", [P, 2, G, 2]) for n in range(3)]
        sd, rs, nb = ([ph.sb(f"{w}{n}", [P, 2, G]) for n in range(3)] for w in ("sd", "rs", "nb"))
        block = ph.block()

        def rows(table, i, s):
            first = NODES - ROWS if (isinstance(i, int) and i == N - 1 and s == 1) else i * (2 * ROWS) + s * ROWS
            return table[bass.ds(first, ROWS), :].rearrange("(p k) f -> p (k f)", k=G)

        @block.sync
        def _(sp):
            def load(i, at):
                for s in range(2):
                    sp.wait_ge(pool, X.at(at - 1, "x", s))
                    sp.dma_start(slot(x_in, s), rows(k.x, i, s)).then_inc(loaded[s], 16)

            def store(i):
                for s in range(2):
                    sp.wait_ge(vec, V.at(i, "out", s))
                    if isinstance(i, int) and i == N - 1 and s == 1:
                        sp.wait_ge(stored[0], (LAG + N) * 16 + AHEAD)
                    sp.dma_start(rows(k.out, i, s), slot(out, s)).then_inc(stored[s], 16)
            for s in range(2):
                sp.sem_inc(stored[s], LAG * 16 + AHEAD)
            for i in range(LAG + 1):
                load(i, i)
            with sp.Fori(LAG + 1, N - 1) as i:
                load(i, i)
                store(i - (LAG + 1))
            load(N - 1, N - 1)
            store(N - 2 - LAG)
            for i in range(LAG):
                load(N - 1, N + i)
                store(N - 1 - LAG + i)
            store(N - 1)
            for s in range(2):
                sp.wait_ge(loaded[s], (N + LAG) * 16)
                sp.wait_ge(stored[s], (LAG + N) * 16 + AHEAD)

        @block.gpsimd
        def _(g):
            for b in (x, h, u, y, xb, x3, x3k, hT, aT):
                last = g.memset(b[:, :], 0.0)
            last.then_inc(cleared, 1)
            g.wait_ge(cleared, 1)
            g.sem_inc(pool, X.per)
            with g.Fori(0, N + LAG) as i:
                for s in range(2):
                    g.wait_ge(vec, V.at(i - 2, "x3", s))
                    g.wait_ge(pool, X.at(i - 1, "x", s))
                    nc.gpsimd.tensor_tensor(by_tile(slot(xb, s)), by_tile(slot(x, s)), every(k.ln_b[:, :]), ALU.add).then_inc(pool, 1)
                for s in range(2):
                    g.wait_ge(loaded[s], i * 16 + 16)
                    g.wait_ge(act, A.at(i - 1, "relu", s))
                    g.wait_ge(pool, X.at(i - 1, "xb", s))
                    nc.gpsimd.tensor_tensor(by_tile(slot(x, s)), by_tile(slot(x_in, s)), every(k.plain[:, :]), ALU.add).then_inc(pool, 1)
                for s in range(2):
                    wait_apart(g, k, vec, V.at(i - 3, "out", s))
                    nc.gpsimd.tensor_copy(slot(x3k, s), slot(x3, s)).then_inc(pool, 1)

        @block.vector
        def _(d):
            d.wait_ge(cleared, 1)
            d.sem_inc(vec, V.per)
            with d.Fori(0, N + LAG) as i:
                for s in range(2):
                    d.wait_ge(act, A.at(i - 1, "relu", s))
                    nc.vector.tensor_tensor(by_tile(slot(u, s)), by_tile(slot(h, s)), every(k.bias2[:, :]), ALU.add).then_inc(vec, 1)
                for s in range(2):
                    d.wait_ge(vec, V.at(i - 2, "scaled", s))
                    d.wait_ge(pool, X.at(i - 2, "xb", s))
                    d.wait_ge(pool, X.at(i - 3, "x3_kept", s))
                    nc.vector.tensor_tensor(slot(x3, s), slot(y, s), slot(xb, s), ALU.add).then_inc(vec, 1)
                for s in range(2):
                    d.wait_ge(vec, V.at(i - 1, "u", s))
                    stats(nc, u, s, st[1]).then_inc(vec, 1)
                for s in range(2):
                    d.wait_ge(vec, V.at(i - 2, "x3", s))
                    stats(nc, x3, s, st[2]).then_inc(vec, 1)
                for s in range(2):
                    d.wait_ge(pool, X.at(i, "x", s))
                    stats(nc, x, s, st[0]).then_inc(vec, 1)
                for n, lag in (("2", 1), ("3", 2), ("", 0)):
                    for s in range(2):
                        d.wait_ge(act, A.at(i - lag - 1, "sd" + n, s))
                        wait_apart(d, k, vec, V.at(i - lag, "stats" + n, s))
                        aggregate(nc, s, st[lag], mv[lag]).then_inc(vec, 1)
                for n, lag in (("2", 1), ("3", 2), ("", 0)):
                    for s in range(2):
                        d.wait_ge(act, A.at(i - lag, "sd" + n, s))
                        nc.vector.reciprocal(rs[lag][:, s, :], sd[lag][:, s, :]).then_inc(vec, 1)
                for n, lag in (("2", 1), ("", 0)):
                    for s in range(2):
                        d.wait_ge(vec, V.at(i - lag, "rs" + n, s))
                        nc.vector.scalar_tensor_tensor(nb[lag][:, s, :], mv[lag][:, s, :, 0], -1.0, rs[lag][:, s, :],
                                                       ALU.mult, ALU.mult).then_inc(vec, 1)
                for s in range(2):
                    d.wait_ge(vec, V.at(i - 2, "rs3", s))
                    d.wait_ge(pe, M.at(i - 3, "turned", s))
                    normalise(nc, x3, s, mv[2], rs[2], h3).then_inc(vec, 1)
                for s in range(2):
                    d.wait_ge(pe, M.at(i - 3, "product", s))
                    d.wait_ge(pool, X.at(i - 3, "x3_kept", s))
                    d.wait_ge(stored[s], i * 16 + AHEAD)
                    nc.vector.scalar_tensor_tensor(slot(out, s), pair(k, 2 * s), 0.0, slot(x3k, s), ALU.max, ALU.add).then_inc(vec, 1)
                for s in range(2):
                    d.wait_ge(act, A.at(i - 1, "norm2", s))
                    nc.vector.tensor_tensor(by_tile(slot(y, s)), by_tile(slot(y, s)), every(k.ln_g[:, :]), ALU.mult).then_inc(vec, 1)

        @block.scalar
        def _(a):
            a.wait_ge(cleared, 1)
            a.sem_inc(act, A.per)
            with a.Fori(0, N + LAG) as i:
                def norms(src, dst, n, lag, func):
                    for s in range(2):
                        a.wait_ge(vec, V.at(i - lag, "nb" + n, s))
                        for c in range(G):
                            last = nc.scalar.activation(tile(dst, s, c), tile(src, s, c), func,
                                                        scale=rs[lag][:, s, c:c + 1], bias=nb[lag][:, s, c:c + 1])
                        last.then_inc(act, 1)

                def hidden(n, lag, dst):
                    for s in range(2):
                        a.wait_ge(pe, M.at(i - lag, f"inner{n}", s))
                        if n == 1:
                            a.wait_ge(pe, M.at(i - 3, "product", s))
                        nc.scalar.activation(slot(dst, s), pair(k, 2 * s + 1), ACT.Relu, bias=k.b3[:, n - 1:n]).then_inc(act, 1)

                hidden(2, 3, hT)
                hidden(3, 3, aT)
                for n, lag in (("2", 1), ("3", 2), ("", 0)):
                    for s in range(2):
                        a.wait_ge(vec, V.at(i - lag, "aggr" + n, s))
                        deviation(nc, k, s, mv[lag], sd[lag]).then_inc(act, 1)
                norms(u, y, "2", 1, ACT.Identity)
                norms(x, h, "", 0, ACT.Relu)
                for s in range(2):
                    a.wait_ge(pe, M.at(i - 2, "turned", s))
                    nc.scalar.activation(slot(hT, s), pair(k, 2 * s + 1), ACT.Relu).then_inc(act, 1)
                hidden(1, 2, aT)

        @block.tensor
        def _(t):
            t.wait_ge(cleared, 1)
            t.sem_inc(pe, M.per)
            with t.Fori(0, N + LAG) as i:
                for s in range(2):
                    t.wait_ge(act, A.at(i - 3, "hidden1", s))
                    times_cols(nc, aT, s, k.w3[:, 1, :], pair(k, 2 * s + 1)).then_inc(pe, 1)
                for s in range(2):
                    t.wait_ge(act, A.at(i - 3, "hidden2", s))
                    times_cols(nc, hT, s, k.w3[:, 2, :], pair(k, 2 * s + 1)).then_inc(pe, 1)
                for s in range(2):
                    t.wait_ge(act, A.at(i - 3, "hidden3", s))
                    t.wait_ge(vec, V.at(i - 4, "out", s))
                    times_rows_plus(nc, k, aT, s, k.w3[:, 3, :], pair(k, 2 * s)).then_inc(pe, 1)
                for s in range(2):
                    t.wait_ge(vec, V.at(i - 2, "norm3", s))
                    transposed(nc, k, h3, s, pair(k, 2 * s + 1)).then_inc(pe, 1)
                for s in range(2):
                    t.wait_ge(act, A.at(i - 2, "moved", s))
                    times_cols(nc, hT, s, k.w3[:, 0, :], pair(k, 2 * s + 1)).then_inc(pe, 1)


def build(nc, x, src, dst, et4, et8, w, out):
    with ExitStack() as ctx:
        k = Shared()
        k.x, k.src, k.dst, k.et4, k.et8, k.w, k.out = x, src, dst, et4, et8, w, out

        def dram(name, shape, dt=F32):
            return nc.dram_tensor(name, shape, dt, kind="Internal").ap()

        def sb(name, shape, dt=F32):
            return ctx.enter_context(nc.sbuf_tensor(name, shape, dt))

        k.slot_table, k.pair_table = dram("slot_table", (P * HI, 1), I32), dram("pair_table", (P * HI, 2))
        k.dst_rows, k.sorted_edges = dram("dst_rows", (P, T)), dram("sorted_edges", (EDGES, 4), I32)
        k.relT4, k.relT8 = dram("relT4", (T, P)), dram("relT8", (T, P))
        for_rows = (EPAD + P, D)
        k.T1, k.T2, k.V2, k.V3, k.V4 = (dram(n, for_rows) for n in ("T1", "T2", "V2", "V3", "V4"))
        k.V0, k.V1, k.V5, k.XS, k.XD, k.HS, k.HD, k.MSG = (
            dram(n, (EPAD, D)) for n in ("V0", "V1", "V5", "XS", "XD", "HS", "HD", "MSG"))

        k.dstf = sb("dstf", [P, T + 2])
        for_edges = [P, T]
        k.lo, k.hi, k.cont, k.end, k.real_end, k.more, k.fix, k.rel4, k.rel8, k.norm_out, k.norm_in = (
            sb(n, for_edges) for n in ("lo", "hi", "cont", "end", "real_end", "more", "fix", "rel4", "rel8", "norm_out", "norm_in"))
        k.src_i, k.dst_i, k.src_tab, k.slot_at, k.out_i, k.pos_i, k.slot_i = (
            sb(n, for_edges, I32) for n in ("src_i", "dst_i", "src_tab", "slot_at", "out_i", "pos_i", "slot_i"))
        k.fix_i = sb("fix_i", [P, 1], I32)
        k.dst_list, k.src_list, k.rel_list = sb("dst_list", [P, T + 2], I32), sb("src_list", [P, T], I32), sb("rel_list", [P, 2, T], I32)
        k.ident, k.into, k.intoT, k.back = (sb(n, [P, P]) for n in ("ident", "into", "intoT", "back"))
        k.tail, k.bn_a, k.bn_b, k.plain = (sb(n, [P, D]) for n in ("tail", "bn_a", "bn_b", "plain"))
        k.small = sb("small", [P, 36, T])
        k.sl, k.sr, k.es, k.ed = k.small[:, 0:8, :], k.small[:, 8:16, :], k.small[:, 16:20, :], k.small[:, 20:36, :]
        k.zeros, k.ones, k.eps, k.p_col = sb("zeros", [P, D]), sb("ones", [P, P]), sb("eps", [P, 1]), sb("p_col", [P, 1])
        k.hi_row = sb("hi_row", [P, HI], FP16)
        k.w0, k.w3 = sb("w0", [P, 2, D]), sb("w3", [P, 4, D])
        k.wf, k.w2 = sb("wf", [P, 4, D + H8]), sb("w2", [P, R4, D + H4])
        k.vdst, k.q2, k.rel_of = sb("vdst", [P, R4 * H4]), sb("q2", [P, P]), sb("rel_of", [P, 4])
        k.b3, k.gb, k.b3_row = sb("b3", [P, 3]), sb("gb", [P, 2]), sb("b3_row", [P, 2, D])
        k.b1_0, k.b2_0, k.attn_r, k.bias2, k.ln_g, k.ln_b = (sb(n, [P, D]) for n in ("b1_0", "b2_0", "attn_r", "bias2", "ln_g", "ln_b"))
        k.hm8, k.hm4, k.al, k.a4 = sb("hm8", [P, H8]), sb("hm4", [P, H4]), sb("al", [P, H8]), sb("a4", [P, 2, R4, H4])
        k.b2b = k.b3_row[:, 1, :]
        k.psum = ctx.enter_context(nc.psum_tensor("psum", [P, 4096], F32))
        k.setup_rows = SQUARES + 5
        k.gpsimd_sems = {n: [ctx.enter_context(nc.semaphore(f"{n}{s}")) for s in range(2)]
                         for n in ("gathered", "scattered", "fetched")}
        k.placed = ctx.enter_context(nc.semaphore("placed"))
        k.passed = ctx.enter_context(nc.semaphore("passed"))
        k.raised = dict.fromkeys(k.gpsimd_sems, 0)
        phases = [order_edges, setup, out_degrees, lookups,
                  conv1_edges, lambda nc, k: join_partitions(nc, k, k.V0, "j0"), conv1_nodes,
                  conv2_edges, lambda nc, k: join_partitions(nc, k, k.V1, "j1"), conv2_nodes,
                  lambda nc, k: relational_edges(nc, k, "r1", k.T2, True, D + H8, k.wf, k.sl),
                  weigh_heads1,
                  lambda nc, k: weighted_edges(nc, k, "w1", H8, k.sl, k.V2),
                  lambda nc, k: join_partitions(nc, k, k.V2, "j2"),
                  batch_stats,
                  layer2_nodes,
                  lambda nc, k: relational_edges(nc, k, "r2", k.V2, False, D + H4, k.w2, k.es),
                  weigh_edges2,
                  lambda nc, k: weighted_edges(nc, k, "w2", H4, k.es, k.V3),
                  lambda nc, k: join_partitions(nc, k, k.V3, "j3"),
                  lambda nc, k: layer3_inputs(nc, k, "n3", False),
                  lambda nc, k: layer3_inputs(nc, k, "e3", True),
                  lambda nc, k: join_partitions(nc, k, k.V4, "j4"),
                  lambda nc, k: graph_mlp(nc, k, "m1n", False, 0),
                  lambda nc, k: graph_mlp(nc, k, "m1e", True, 0),
                  lambda nc, k: join_partitions(nc, k, k.V5, "j5"),
                  all_nodes,
                  lambda nc, k: graph_mlp(nc, k, "m2n", False, 1)]
        for phase in phases:
            phase(nc, k)


def kernel(**inputs):
    import numpy as np
    import concourse.bacc as bacc
    from concourse.bass_utils import run_bass_kernel_spmd

    nc = bacc.Bacc("TRN2", target_bir_lowering=False, num_devices=1)
    arrays = {name: np.ascontiguousarray(a) for name, a in inputs.items()}
    aps = {name: nc.dram_tensor(name, a.shape, mybir.dt.from_np(a.dtype), kind="ExternalInput").ap() for name, a in arrays.items()}
    out = nc.dram_tensor("out", (NODES, D), F32, kind="ExternalOutput").ap()
    build(nc, aps["x"], aps["src"], aps["dst"], aps["edge_type_4"], aps["edge_type_8"], aps, out)
    r = run_bass_kernel_spmd(nc, [arrays], core_ids=[0])
    return r.results[0]["out"]
```
